# Optimizing a Trainium2 kernel written in Bass

```python
import numpy as np
import jax
import jax.numpy as jnp

def _softmax(x, axis=-1):
    return jax.nn.softmax(x, axis=axis)

def _gelu(x):
    return jax.nn.gelu(x, approximate=True)

def _silu(x):
    return jax.nn.silu(x)

def _sigmoid(x):
    return jax.nn.sigmoid(x)

def _layernorm(x, axis=-1, eps=1e-05):
    m = jnp.mean(x, axis=axis, keepdims=True)
    v = jnp.var(x, axis=axis, keepdims=True)
    return (x - m) / jnp.sqrt(v + eps)

def _scatter_add(tgt, idx, src, axis=0):
    return tgt.at[idx].add(src)

def _segment_sum(src, seg, n):
    return jax.ops.segment_sum(src, seg, n)
kernel_name = 'mk_xattn_seq_d4_seqx_r8_2e4dce'

def setup_inputs(seed: int=0):
    np.random.seed(seed)
    _w = jnp.asarray

    def _rec_inputs():
        import jax
        import jax.numpy as jnp
        _rk = jax.random.key(seed)
        x = -0.0002928 + 1 * jax.random.normal(jax.random.fold_in(_rk, 1), (4, 256, 256), jnp.float32)
        _lenS = 256 - jax.random.randint(jax.random.fold_in(_rk, 7), (4,), 0, max(1, 256 // 4) + 1, jnp.int32)
        _lenS2 = 256 - jax.random.randint(jax.random.fold_in(_rk, 8), (4,), 0, max(1, 256 // 4) + 1, jnp.int32)
        _ctx_2048P = jax.random.normal(jax.random.fold_in(_rk, 11), (4, 16, 256), jnp.float32)
        _ctx_2048c = jax.random.dirichlet(jax.random.fold_in(_rk, 511), 0.3 * jnp.ones((16,), jnp.float32), (4, 256))
        _ctx_2048t = jnp.einsum('bsk,bkd->bsd', _ctx_2048c, _ctx_2048P)
        _ctx_2048t = _ctx_2048t * jax.lax.rsqrt(jnp.mean(jnp.square(_ctx_2048t)) + 1e-12) * 0.953939
        ctx_2048 = 0.000189249 + 0.0999589 * (_ctx_2048t + 0.3 * jax.random.normal(jax.random.fold_in(_rk, 611), (4, 256, 256), jnp.float32))
        _validS = jnp.arange(256)[None, :] < _lenS[:, None]
        _validS2 = jnp.arange(256)[None, :] < _lenS2[:, None]
        _causal = jnp.tril(jnp.ones((256, 256), dtype=bool))
        mask_BxS2_bf1 = jnp.ones((4, 256), dtype=bool)
        return (x, ctx_2048, mask_BxS2_bf1)
    x, ctx_2048, mask_BxS2_bf1 = _rec_inputs()

    def _L0_xattn_setup():
        import jax, jax.numpy as jnp
        import numpy as np
        B, L, E, H = (4, 64, 256, 32)
        S = E // H
        EXTRA_MAA, EXTRA_DECAY = (32, 64)
        EPS = 1e-05

        def _ln(x, w, b):
            m = jnp.mean(x, axis=-1, keepdims=True)
            v = jnp.mean((x - m) ** 2, axis=-1, keepdims=True)
            return (x - m) * jax.lax.rsqrt(v + EPS) * w + b

        def _token_shift(xn, prev_row):
            first = (prev_row - xn[:, 0])[:, None]
            rest = xn[:, :-1] - xn[:, 1:]
            return jnp.concatenate([first, rest], axis=1)
        key = jax.random.key(seed)
        ks = jax.random.split(key, 24)
        rn = lambda k, shp, s=1.0: jax.random.normal(k, shp, dtype=jnp.float32) * s
        return dict(x=rn(ks[0], (B, L, E)), state=rn(ks[1], (B, 2 + S, E), 0.1), ln1_w=jnp.ones((E,), jnp.float32), ln1_b=jnp.zeros((E,), jnp.float32), ln2_w=jnp.ones((E,), jnp.float32), ln2_b=jnp.zeros((E,), jnp.float32), maa_x=rn(ks[2], (E,), 0.02), maa_w1=rn(ks[3], (E, 5 * EXTRA_MAA), 0.02), maa_w2=rn(ks[4], (5, EXTRA_MAA, E), 0.02), maa_stack=rn(ks[5], (5, E), 0.02), time_decay=rn(ks[6], (E,), 0.5), decay_w1=rn(ks[7], (E, EXTRA_DECAY), 0.02), decay_w2=rn(ks[8], (EXTRA_DECAY, E), 0.02), faaaa=rn(ks[9], (H, S), 0.1), Wr=rn(ks[10], (E, E), 0.02), Wk=rn(ks[11], (E, E), 0.02), Wv=rn(ks[12], (E, E), 0.02), Wg=rn(ks[13], (E, E), 0.02), Wo=rn(ks[14], (E, E), 0.02), gn_w=jnp.ones((E,), jnp.float32), gn_b=jnp.zeros((E,), jnp.float32), ffn_maa_k=rn(ks[15], (E,), 0.02), ffn_maa_r=rn(ks[16], (E,), 0.02), ffn_Wk=rn(ks[17], (E, E), 0.02), ffn_Wr=rn(ks[18], (E, E), 0.02), ffn_Wv=rn(ks[19], (E, E), 0.02), i=0)
    _L0_xattn_all = _L0_xattn_setup()
    _L0_xattn_in = {k: v for k, v in _L0_xattn_all.items() if k in ('ln1_w', 'ln1_b', 'ln2_w', 'ln2_b', 'maa_x', 'maa_w1', 'maa_w2', 'maa_stack', 'time_decay', 'decay_w1', 'decay_w2', 'faaaa', 'Wr', 'Wk', 'Wv', 'Wg', 'Wo', 'gn_w', 'gn_b', 'ffn_maa_k', 'ffn_maa_r', 'ffn_Wk', 'ffn_Wr', 'ffn_Wv')}
    del _L0_xattn_all

    def _L1_xattn_setup():
        import jax, jax.numpy as jnp
        import numpy as np
        HIDDEN = 256
        HEADS = 16
        HEAD_DIM = HIDDEN // HEADS
        LN_EPS = 1e-05
        GATE_INIT = 0.5

        def _layer_norm(x, gamma, beta):
            mu = jnp.mean(x, axis=-1, keepdims=True)
            var = jnp.mean(jnp.square(x - mu), axis=-1, keepdims=True)
            return (x - mu) * jax.lax.rsqrt(var + LN_EPS) * gamma + beta
        key = jax.random.key(seed)
        ks = jax.random.split(key, 8)
        B, T_TEXT, T_AUDIO = (4, 256, 1500)
        s = 0.02
        return {'hidden_states': jax.random.normal(ks[0], (B, T_TEXT, HIDDEN), jnp.float32), 'audio_kv': jax.random.normal(ks[1], (B, T_AUDIO, HIDDEN), jnp.float32), 'audio_attention_mask': jnp.ones((B, T_AUDIO), dtype=bool), 'Wq': jax.random.normal(ks[2], (HIDDEN, HIDDEN), jnp.float32) * s, 'Wk': jax.random.normal(ks[3], (HIDDEN, HIDDEN), jnp.float32) * s, 'Wv': jax.random.normal(ks[4], (HIDDEN, HIDDEN), jnp.float32) * s, 'Wo': jax.random.normal(ks[5], (HIDDEN, HIDDEN), jnp.float32) * s, 'ln_gamma': jnp.ones((HIDDEN,), jnp.float32), 'ln_beta': jnp.zeros((HIDDEN,), jnp.float32), 'gate': jnp.array([GATE_INIT], jnp.float32)}
    _L1_xattn_all = _L1_xattn_setup()
    _L1_xattn_in = {k: v for k, v in _L1_xattn_all.items() if k in ('Wq', 'Wk', 'Wv', 'Wo', 'ln_gamma', 'ln_beta', 'gate')}
    del _L1_xattn_all

    def _L2_xattn_setup():
        import jax, jax.numpy as jnp
        import numpy as np
        B, L, E, H = (4, 64, 256, 32)
        S = E // H
        EXTRA_MAA, EXTRA_DECAY = (32, 64)
        EPS = 1e-05

        def _ln(x, w, b):
            m = jnp.mean(x, axis=-1, keepdims=True)
            v = jnp.mean((x - m) ** 2, axis=-1, keepdims=True)
            return (x - m) * jax.lax.rsqrt(v + EPS) * w + b

        def _token_shift(xn, prev_row):
            first = (prev_row - xn[:, 0])[:, None]
            rest = xn[:, :-1] - xn[:, 1:]
            return jnp.concatenate([first, rest], axis=1)
        key = jax.random.key(seed)
        ks = jax.random.split(key, 24)
        rn = lambda k, shp, s=1.0: jax.random.normal(k, shp, dtype=jnp.float32) * s
        return dict(x=rn(ks[0], (B, L, E)), state=rn(ks[1], (B, 2 + S, E), 0.1), ln1_w=jnp.ones((E,), jnp.float32), ln1_b=jnp.zeros((E,), jnp.float32), ln2_w=jnp.ones((E,), jnp.float32), ln2_b=jnp.zeros((E,), jnp.float32), maa_x=rn(ks[2], (E,), 0.02), maa_w1=rn(ks[3], (E, 5 * EXTRA_MAA), 0.02), maa_w2=rn(ks[4], (5, EXTRA_MAA, E), 0.02), maa_stack=rn(ks[5], (5, E), 0.02), time_decay=rn(ks[6], (E,), 0.5), decay_w1=rn(ks[7], (E, EXTRA_DECAY), 0.02), decay_w2=rn(ks[8], (EXTRA_DECAY, E), 0.02), faaaa=rn(ks[9], (H, S), 0.1), Wr=rn(ks[10], (E, E), 0.02), Wk=rn(ks[11], (E, E), 0.02), Wv=rn(ks[12], (E, E), 0.02), Wg=rn(ks[13], (E, E), 0.02), Wo=rn(ks[14], (E, E), 0.02), gn_w=jnp.ones((E,), jnp.float32), gn_b=jnp.zeros((E,), jnp.float32), ffn_maa_k=rn(ks[15], (E,), 0.02), ffn_maa_r=rn(ks[16], (E,), 0.02), ffn_Wk=rn(ks[17], (E, E), 0.02), ffn_Wr=rn(ks[18], (E, E), 0.02), ffn_Wv=rn(ks[19], (E, E), 0.02), i=0)
    _L2_xattn_all = _L2_xattn_setup()
    _L2_xattn_in = {k: v for k, v in _L2_xattn_all.items() if k in ('ln1_w', 'ln1_b', 'ln2_w', 'ln2_b', 'maa_x', 'maa_w1', 'maa_w2', 'maa_stack', 'time_decay', 'decay_w1', 'decay_w2', 'faaaa', 'Wr', 'Wk', 'Wv', 'Wg', 'Wo', 'gn_w', 'gn_b', 'ffn_maa_k', 'ffn_maa_r', 'ffn_Wk', 'ffn_Wr', 'ffn_Wv')}
    del _L2_xattn_all

    def _L3_xattn_setup():
        import jax, jax.numpy as jnp
        import numpy as np
        B, Q, S1, S2 = (4, 32, 256, 256)
        D, H, K, F = (256, 16, 128, 1024)
        LN_EPS = 1e-05

        def _layer_norm(x, scale, offset):
            mu = jnp.mean(x, axis=-1, keepdims=True)
            var = jnp.var(x, axis=-1, keepdims=True)
            return (x - mu) * jax.lax.rsqrt(var + LN_EPS) * scale + offset

        def _cross_attention(q_in, kv_in, wq, bq, wk, bk, wv, bv, wo, bo, bias_k, bias_v):
            b, q_len, _ = q_in.shape
            t = kv_in.shape[1]
            qh = (q_in @ wq + bq).reshape(b, q_len, H, K)
            kh = (kv_in @ wk + bk).reshape(b, t, H, K)
            vh = (kv_in @ wv + bv).reshape(b, t, H, K)
            kh = jnp.concatenate([kh, jnp.broadcast_to(bias_k, (b, 1, H, K))], axis=1)
            vh = jnp.concatenate([vh, jnp.broadcast_to(bias_v, (b, 1, H, K))], axis=1)
            scale = jnp.sqrt(jnp.asarray(K, q_in.dtype))
            logits = jnp.einsum('bqhk,bthk->bhqt', qh, kh) / scale
            weights = jax.nn.softmax(logits, axis=-1)
            ctx = jnp.einsum('bhqt,bthk->bqhk', weights, vh).reshape(b, q_len, H * K)
            return ctx @ wo + bo

        def _forward(x, xf_1, xf_2, ln1_scale, ln1_offset, wq1, bq1, wk1, bk1, wv1, bv1, wo1, bo1, bias_k1, bias_v1, ln2_scale, ln2_offset, wq2, bq2, wk2, bk2, wv2, bv2, wo2, bo2, bias_k2, bias_v2, ln_mlp_scale, ln_mlp_offset, w_fc1, b_fc1, w_fc2, b_fc2):
            res = x
            h = _layer_norm(x, ln1_scale, ln1_offset)
            x = res + _cross_attention(h, xf_1, wq1, bq1, wk1, bk1, wv1, bv1, wo1, bo1, bias_k1, bias_v1)
            res = x
            h = _layer_norm(x, ln2_scale, ln2_offset)
            x = res + _cross_attention(h, xf_2, wq2, bq2, wk2, bk2, wv2, bv2, wo2, bo2, bias_k2, bias_v2)
            h = _layer_norm(x, ln_mlp_scale, ln_mlp_offset)
            h = jax.nn.gelu(h @ w_fc1 + b_fc1, approximate=False) @ w_fc2 + b_fc2
            return x + h
        key = jax.random.key(seed)
        ks = iter(jax.random.split(key, 64))

        def rn(shape, s=0.02):
            return jax.random.normal(next(ks), shape, jnp.float32) * s
        inp = {'x': rn((B, Q, D), 1.0), 'xf_1': rn((B, S1, D), 1.0), 'xf_2': rn((B, S2, D), 1.0)}
        for i in (1, 2):
            inp[f'ln{i}_scale'] = jnp.ones((D,), jnp.float32)
            inp[f'ln{i}_offset'] = jnp.zeros((D,), jnp.float32)
            inp[f'wq{i}'] = rn((D, H * K))
            inp[f'bq{i}'] = jnp.zeros((H * K,), jnp.float32)
            inp[f'wk{i}'] = rn((D, H * K))
            inp[f'bk{i}'] = jnp.zeros((H * K,), jnp.float32)
            inp[f'wv{i}'] = rn((D, H * K))
            inp[f'bv{i}'] = jnp.zeros((H * K,), jnp.float32)
            inp[f'wo{i}'] = rn((H * K, D))
            inp[f'bo{i}'] = jnp.zeros((D,), jnp.float32)
            inp[f'bias_k{i}'] = rn((1, 1, H, K))
            inp[f'bias_v{i}'] = rn((1, 1, H, K))
        inp['ln_mlp_scale'] = jnp.ones((D,), jnp.float32)
        inp['ln_mlp_offset'] = jnp.zeros((D,), jnp.float32)
        inp['w_fc1'] = rn((D, F))
        inp['b_fc1'] = jnp.zeros((F,), jnp.float32)
        inp['w_fc2'] = rn((F, D))
        inp['b_fc2'] = jnp.zeros((D,), jnp.float32)
        return inp
    _L3_xattn_all = _L3_xattn_setup()
    _L3_xattn_in = {k: v for k, v in _L3_xattn_all.items() if k in ('ln1_scale', 'ln1_offset', 'wq1', 'bq1', 'wk1', 'bk1', 'wv1', 'bv1', 'wo1', 'bo1', 'bias_k1', 'bias_v1', 'ln2_scale', 'ln2_offset', 'wq2', 'bq2', 'wk2', 'bk2', 'wv2', 'bv2', 'wo2', 'bo2', 'bias_k2', 'bias_v2', 'ln_mlp_scale', 'ln_mlp_offset', 'w_fc1', 'b_fc1', 'w_fc2', 'b_fc2')}
    del _L3_xattn_all
    return {'x': x, 'ctx_2048': ctx_2048, 'mask_BxS2_bf1': mask_BxS2_bf1, 'L0_xattn_ln1_w': _L0_xattn_in['ln1_w'], 'L0_xattn_ln1_b': _L0_xattn_in['ln1_b'], 'L0_xattn_ln2_w': _L0_xattn_in['ln2_w'], 'L0_xattn_ln2_b': _L0_xattn_in['ln2_b'], 'L0_xattn_maa_x': _L0_xattn_in['maa_x'], 'L0_xattn_maa_w1': _L0_xattn_in['maa_w1'], 'L0_xattn_maa_w2': _L0_xattn_in['maa_w2'], 'L0_xattn_maa_stack': _L0_xattn_in['maa_stack'], 'L0_xattn_time_decay': _L0_xattn_in['time_decay'], 'L0_xattn_decay_w1': _L0_xattn_in['decay_w1'], 'L0_xattn_decay_w2': _L0_xattn_in['decay_w2'], 'L0_xattn_faaaa': _L0_xattn_in['faaaa'], 'L0_xattn_Wr': _L0_xattn_in['Wr'], 'L0_xattn_Wk': _L0_xattn_in['Wk'], 'L0_xattn_Wv': _L0_xattn_in['Wv'], 'L0_xattn_Wg': _L0_xattn_in['Wg'], 'L0_xattn_Wo': _L0_xattn_in['Wo'], 'L0_xattn_gn_w': _L0_xattn_in['gn_w'], 'L0_xattn_gn_b': _L0_xattn_in['gn_b'], 'L0_xattn_ffn_maa_k': _L0_xattn_in['ffn_maa_k'], 'L0_xattn_ffn_maa_r': _L0_xattn_in['ffn_maa_r'], 'L0_xattn_ffn_Wk': _L0_xattn_in['ffn_Wk'], 'L0_xattn_ffn_Wr': _L0_xattn_in['ffn_Wr'], 'L0_xattn_ffn_Wv': _L0_xattn_in['ffn_Wv'], 'L1_xattn_Wq': _L1_xattn_in['Wq'], 'L1_xattn_Wk': _L1_xattn_in['Wk'], 'L1_xattn_Wv': _L1_xattn_in['Wv'], 'L1_xattn_Wo': _L1_xattn_in['Wo'], 'L1_xattn_ln_gamma': _L1_xattn_in['ln_gamma'], 'L1_xattn_ln_beta': _L1_xattn_in['ln_beta'], 'L1_xattn_gate': _L1_xattn_in['gate'], 'L2_xattn_ln1_w': _L2_xattn_in['ln1_w'], 'L2_xattn_ln1_b': _L2_xattn_in['ln1_b'], 'L2_xattn_ln2_w': _L2_xattn_in['ln2_w'], 'L2_xattn_ln2_b': _L2_xattn_in['ln2_b'], 'L2_xattn_maa_x': _L2_xattn_in['maa_x'], 'L2_xattn_maa_w1': _L2_xattn_in['maa_w1'], 'L2_xattn_maa_w2': _L2_xattn_in['maa_w2'], 'L2_xattn_maa_stack': _L2_xattn_in['maa_stack'], 'L2_xattn_time_decay': _L2_xattn_in['time_decay'], 'L2_xattn_decay_w1': _L2_xattn_in['decay_w1'], 'L2_xattn_decay_w2': _L2_xattn_in['decay_w2'], 'L2_xattn_faaaa': _L2_xattn_in['faaaa'], 'L2_xattn_Wr': _L2_xattn_in['Wr'], 'L2_xattn_Wk': _L2_xattn_in['Wk'], 'L2_xattn_Wv': _L2_xattn_in['Wv'], 'L2_xattn_Wg': _L2_xattn_in['Wg'], 'L2_xattn_Wo': _L2_xattn_in['Wo'], 'L2_xattn_gn_w': _L2_xattn_in['gn_w'], 'L2_xattn_gn_b': _L2_xattn_in['gn_b'], 'L2_xattn_ffn_maa_k': _L2_xattn_in['ffn_maa_k'], 'L2_xattn_ffn_maa_r': _L2_xattn_in['ffn_maa_r'], 'L2_xattn_ffn_Wk': _L2_xattn_in['ffn_Wk'], 'L2_xattn_ffn_Wr': _L2_xattn_in['ffn_Wr'], 'L2_xattn_ffn_Wv': _L2_xattn_in['ffn_Wv'], 'L3_xattn_ln1_scale': _L3_xattn_in['ln1_scale'], 'L3_xattn_ln1_offset': _L3_xattn_in['ln1_offset'], 'L3_xattn_wq1': _L3_xattn_in['wq1'], 'L3_xattn_bq1': _L3_xattn_in['bq1'], 'L3_xattn_wk1': _L3_xattn_in['wk1'], 'L3_xattn_bk1': _L3_xattn_in['bk1'], 'L3_xattn_wv1': _L3_xattn_in['wv1'], 'L3_xattn_bv1': _L3_xattn_in['bv1'], 'L3_xattn_wo1': _L3_xattn_in['wo1'], 'L3_xattn_bo1': _L3_xattn_in['bo1'], 'L3_xattn_bias_k1': _L3_xattn_in['bias_k1'], 'L3_xattn_bias_v1': _L3_xattn_in['bias_v1'], 'L3_xattn_ln2_scale': _L3_xattn_in['ln2_scale'], 'L3_xattn_ln2_offset': _L3_xattn_in['ln2_offset'], 'L3_xattn_wq2': _L3_xattn_in['wq2'], 'L3_xattn_bq2': _L3_xattn_in['bq2'], 'L3_xattn_wk2': _L3_xattn_in['wk2'], 'L3_xattn_bk2': _L3_xattn_in['bk2'], 'L3_xattn_wv2': _L3_xattn_in['wv2'], 'L3_xattn_bv2': _L3_xattn_in['bv2'], 'L3_xattn_wo2': _L3_xattn_in['wo2'], 'L3_xattn_bo2': _L3_xattn_in['bo2'], 'L3_xattn_bias_k2': _L3_xattn_in['bias_k2'], 'L3_xattn_bias_v2': _L3_xattn_in['bias_v2'], 'L3_xattn_ln_mlp_scale': _L3_xattn_in['ln_mlp_scale'], 'L3_xattn_ln_mlp_offset': _L3_xattn_in['ln_mlp_offset'], 'L3_xattn_w_fc1': _L3_xattn_in['w_fc1'], 'L3_xattn_b_fc1': _L3_xattn_in['b_fc1'], 'L3_xattn_w_fc2': _L3_xattn_in['w_fc2'], 'L3_xattn_b_fc2': _L3_xattn_in['b_fc2']}

def reference(x, ctx_2048, mask_BxS2_bf1, L0_xattn_ln1_w, L0_xattn_ln1_b, L0_xattn_ln2_w, L0_xattn_ln2_b, L0_xattn_maa_x, L0_xattn_maa_w1, L0_xattn_maa_w2, L0_xattn_maa_stack, L0_xattn_time_decay, L0_xattn_decay_w1, L0_xattn_decay_w2, L0_xattn_faaaa, L0_xattn_Wr, L0_xattn_Wk, L0_xattn_Wv, L0_xattn_Wg, L0_xattn_Wo, L0_xattn_gn_w, L0_xattn_gn_b, L0_xattn_ffn_maa_k, L0_xattn_ffn_maa_r, L0_xattn_ffn_Wk, L0_xattn_ffn_Wr, L0_xattn_ffn_Wv, L1_xattn_Wq, L1_xattn_Wk, L1_xattn_Wv, L1_xattn_Wo, L1_xattn_ln_gamma, L1_xattn_ln_beta, L1_xattn_gate, L2_xattn_ln1_w, L2_xattn_ln1_b, L2_xattn_ln2_w, L2_xattn_ln2_b, L2_xattn_maa_x, L2_xattn_maa_w1, L2_xattn_maa_w2, L2_xattn_maa_stack, L2_xattn_time_decay, L2_xattn_decay_w1, L2_xattn_decay_w2, L2_xattn_faaaa, L2_xattn_Wr, L2_xattn_Wk, L2_xattn_Wv, L2_xattn_Wg, L2_xattn_Wo, L2_xattn_gn_w, L2_xattn_gn_b, L2_xattn_ffn_maa_k, L2_xattn_ffn_maa_r, L2_xattn_ffn_Wk, L2_xattn_ffn_Wr, L2_xattn_ffn_Wv, L3_xattn_ln1_scale, L3_xattn_ln1_offset, L3_xattn_wq1, L3_xattn_bq1, L3_xattn_wk1, L3_xattn_bk1, L3_xattn_wv1, L3_xattn_bv1, L3_xattn_wo1, L3_xattn_bo1, L3_xattn_bias_k1, L3_xattn_bias_v1, L3_xattn_ln2_scale, L3_xattn_ln2_offset, L3_xattn_wq2, L3_xattn_bq2, L3_xattn_wk2, L3_xattn_bk2, L3_xattn_wv2, L3_xattn_bv2, L3_xattn_wo2, L3_xattn_bo2, L3_xattn_bias_k2, L3_xattn_bias_v2, L3_xattn_ln_mlp_scale, L3_xattn_ln_mlp_offset, L3_xattn_w_fc1, L3_xattn_b_fc1, L3_xattn_w_fc2, L3_xattn_b_fc2):
    import jax
    import jax.numpy as jnp

    def _L0_xattn_ref(x, state, ln1_w, ln1_b, ln2_w, ln2_b, maa_x, maa_w1, maa_w2, maa_stack, time_decay, decay_w1, decay_w2, faaaa, Wr, Wk, Wv, Wg, Wo, gn_w, gn_b, ffn_maa_k, ffn_maa_r, ffn_Wk, ffn_Wr, ffn_Wv, i):
        import jax, jax.numpy as jnp
        import numpy as np
        B, L, E, H = (4, 64, 256, 32)
        S = E // H
        EXTRA_MAA, EXTRA_DECAY = (32, 64)
        EPS = 1e-05

        def _ln(x, w, b):
            m = jnp.mean(x, axis=-1, keepdims=True)
            v = jnp.mean((x - m) ** 2, axis=-1, keepdims=True)
            return (x - m) * jax.lax.rsqrt(v + EPS) * w + b

        def _token_shift(xn, prev_row):
            first = (prev_row - xn[:, 0])[:, None]
            rest = xn[:, :-1] - xn[:, 1:]
            return jnp.concatenate([first, rest], axis=1)
        b, l = (x.shape[0], x.shape[1])
        i0 = (2 + S) * i + 0
        i1 = (2 + S) * i + 1
        xn = _ln(x, ln1_w, ln1_b)
        sx = _token_shift(xn, state[:, i1])
        xxx = jnp.tanh((xn + sx * maa_x) @ maa_w1).reshape(b, l, 5, 1, EXTRA_MAA)
        xxx = jnp.matmul(xxx, maa_w2).reshape(b, l, 5, E)
        x5 = xn[:, :, None] + sx[:, :, None] * (maa_stack + xxx)
        w = jnp.exp(-jnp.exp(time_decay + jnp.tanh(x5[:, :, 1] @ decay_w1) @ decay_w2))
        w = w.reshape(b, l, H, S)
        r = (x5[:, :, 3] @ Wr.T).reshape(b, l, H, S)
        k = (x5[:, :, 0] @ Wk.T).reshape(b, l, H, S)
        v = (x5[:, :, 2] @ Wv.T).reshape(b, l, H, S)
        g = jax.nn.silu(x5[:, :, 4] @ Wg.T)
        s0 = state[:, (2 + S) * i + 2:(2 + S) * (i + 1)].reshape(b, H, S, S)
        u = faaaa[None, :, :, None]

        def step(s, rkvw):
            r_t, k_t, v_t, w_t = rkvw
            a = k_t[:, :, :, None] * v_t[:, :, None, :]
            out = jnp.einsum('bhk,bhkd->bhd', r_t, u * a + s)
            return (a + w_t[:, :, :, None] * s, out)
        xs = tuple((jnp.moveaxis(t, 1, 0) for t in (r, k, v, w)))
        _, outs = jax.lax.scan(step, s0, xs)
        att = jnp.moveaxis(outs, 0, 1).reshape(b, l, E)
        a4 = att.reshape(b, l, H, S)
        m = jnp.mean(a4, axis=-1, keepdims=True)
        var = jnp.mean((a4 - m) ** 2, axis=-1, keepdims=True)
        att = ((a4 - m) * jax.lax.rsqrt(var + EPS)).reshape(b, l, E) * gn_w + gn_b
        x = x + att * g @ Wo.T
        xn2 = _ln(x, ln2_w, ln2_b)
        sx2 = _token_shift(xn2, state[:, i0])
        xk = xn2 + sx2 * ffn_maa_k
        xr = xn2 + sx2 * ffn_maa_r
        rr = jax.nn.sigmoid(xr @ ffn_Wr.T)
        kk = jnp.square(jax.nn.relu(xk @ ffn_Wk.T))
        x = x + rr * (kk @ ffn_Wv.T)
        return x

    def _L1_xattn_ref(hidden_states, audio_kv, audio_attention_mask, Wq, Wk, Wv, Wo, ln_gamma, ln_beta, gate):
        import jax, jax.numpy as jnp
        import numpy as np
        HIDDEN = 256
        HEADS = 16
        HEAD_DIM = HIDDEN // HEADS
        LN_EPS = 1e-05
        GATE_INIT = 0.5

        def _layer_norm(x, gamma, beta):
            mu = jnp.mean(x, axis=-1, keepdims=True)
            var = jnp.mean(jnp.square(x - mu), axis=-1, keepdims=True)
            return (x - mu) * jax.lax.rsqrt(var + LN_EPS) * gamma + beta
        B, Tt, D = hidden_states.shape
        Ta = audio_kv.shape[1]
        scale = HEAD_DIM ** (-0.5)
        a = _layer_norm(audio_kv, ln_gamma, ln_beta)
        Q = (hidden_states @ Wq.T).reshape(B, Tt, HEADS, HEAD_DIM).transpose(0, 2, 1, 3)
        K = (a @ Wk.T).reshape(B, Ta, HEADS, HEAD_DIM).transpose(0, 2, 1, 3)
        V = (a @ Wv.T).reshape(B, Ta, HEADS, HEAD_DIM).transpose(0, 2, 1, 3)
        scores = jnp.einsum('bhtd,bhsd->bhts', Q, K) * scale
        mask = audio_attention_mask[:, None, None, :]
        scores = jnp.where(mask, scores, jnp.float32(-jnp.inf))
        attn = jax.nn.softmax(scores, axis=-1)
        out = jnp.einsum('bhts,bhsd->bhtd', attn, V)
        out = out.transpose(0, 2, 1, 3).reshape(B, Tt, D)
        out = out @ Wo.T
        return hidden_states + jnp.tanh(gate) * out

    def _L2_xattn_ref(x, state, ln1_w, ln1_b, ln2_w, ln2_b, maa_x, maa_w1, maa_w2, maa_stack, time_decay, decay_w1, decay_w2, faaaa, Wr, Wk, Wv, Wg, Wo, gn_w, gn_b, ffn_maa_k, ffn_maa_r, ffn_Wk, ffn_Wr, ffn_Wv, i):
        import jax, jax.numpy as jnp
        import numpy as np
        B, L, E, H = (4, 64, 256, 32)
        S = E // H
        EXTRA_MAA, EXTRA_DECAY = (32, 64)
        EPS = 1e-05

        def _ln(x, w, b):
            m = jnp.mean(x, axis=-1, keepdims=True)
            v = jnp.mean((x - m) ** 2, axis=-1, keepdims=True)
            return (x - m) * jax.lax.rsqrt(v + EPS) * w + b

        def _token_shift(xn, prev_row):
            first = (prev_row - xn[:, 0])[:, None]
            rest = xn[:, :-1] - xn[:, 1:]
            return jnp.concatenate([first, rest], axis=1)
        b, l = (x.shape[0], x.shape[1])
        i0 = (2 + S) * i + 0
        i1 = (2 + S) * i + 1
        xn = _ln(x, ln1_w, ln1_b)
        sx = _token_shift(xn, state[:, i1])
        xxx = jnp.tanh((xn + sx * maa_x) @ maa_w1).reshape(b, l, 5, 1, EXTRA_MAA)
        xxx = jnp.matmul(xxx, maa_w2).reshape(b, l, 5, E)
        x5 = xn[:, :, None] + sx[:, :, None] * (maa_stack + xxx)
        w = jnp.exp(-jnp.exp(time_decay + jnp.tanh(x5[:, :, 1] @ decay_w1) @ decay_w2))
        w = w.reshape(b, l, H, S)
        r = (x5[:, :, 3] @ Wr.T).reshape(b, l, H, S)
        k = (x5[:, :, 0] @ Wk.T).reshape(b, l, H, S)
        v = (x5[:, :, 2] @ Wv.T).reshape(b, l, H, S)
        g = jax.nn.silu(x5[:, :, 4] @ Wg.T)
        s0 = state[:, (2 + S) * i + 2:(2 + S) * (i + 1)].reshape(b, H, S, S)
        u = faaaa[None, :, :, None]

        def step(s, rkvw):
            r_t, k_t, v_t, w_t = rkvw
            a = k_t[:, :, :, None] * v_t[:, :, None, :]
            out = jnp.einsum('bhk,bhkd->bhd', r_t, u * a + s)
            return (a + w_t[:, :, :, None] * s, out)
        xs = tuple((jnp.moveaxis(t, 1, 0) for t in (r, k, v, w)))
        _, outs = jax.lax.scan(step, s0, xs)
        att = jnp.moveaxis(outs, 0, 1).reshape(b, l, E)
        a4 = att.reshape(b, l, H, S)
        m = jnp.mean(a4, axis=-1, keepdims=True)
        var = jnp.mean((a4 - m) ** 2, axis=-1, keepdims=True)
        att = ((a4 - m) * jax.lax.rsqrt(var + EPS)).reshape(b, l, E) * gn_w + gn_b
        x = x + att * g @ Wo.T
        xn2 = _ln(x, ln2_w, ln2_b)
        sx2 = _token_shift(xn2, state[:, i0])
        xk = xn2 + sx2 * ffn_maa_k
        xr = xn2 + sx2 * ffn_maa_r
        rr = jax.nn.sigmoid(xr @ ffn_Wr.T)
        kk = jnp.square(jax.nn.relu(xk @ ffn_Wk.T))
        x = x + rr * (kk @ ffn_Wv.T)
        return x

    def _L3_xattn_ref(x, xf_1, xf_2, ln1_scale, ln1_offset, wq1, bq1, wk1, bk1, wv1, bv1, wo1, bo1, bias_k1, bias_v1, ln2_scale, ln2_offset, wq2, bq2, wk2, bk2, wv2, bv2, wo2, bo2, bias_k2, bias_v2, ln_mlp_scale, ln_mlp_offset, w_fc1, b_fc1, w_fc2, b_fc2):
        import jax, jax.numpy as jnp
        import numpy as np
        B, Q, S1, S2 = (4, 32, 256, 256)
        D, H, K, F = (256, 16, 128, 1024)
        LN_EPS = 1e-05

        def _layer_norm(x, scale, offset):
            mu = jnp.mean(x, axis=-1, keepdims=True)
            var = jnp.var(x, axis=-1, keepdims=True)
            return (x - mu) * jax.lax.rsqrt(var + LN_EPS) * scale + offset

        def _cross_attention(q_in, kv_in, wq, bq, wk, bk, wv, bv, wo, bo, bias_k, bias_v):
            b, q_len, _ = q_in.shape
            t = kv_in.shape[1]
            qh = (q_in @ wq + bq).reshape(b, q_len, H, K)
            kh = (kv_in @ wk + bk).reshape(b, t, H, K)
            vh = (kv_in @ wv + bv).reshape(b, t, H, K)
            kh = jnp.concatenate([kh, jnp.broadcast_to(bias_k, (b, 1, H, K))], axis=1)
            vh = jnp.concatenate([vh, jnp.broadcast_to(bias_v, (b, 1, H, K))], axis=1)
            scale = jnp.sqrt(jnp.asarray(K, q_in.dtype))
            logits = jnp.einsum('bqhk,bthk->bhqt', qh, kh) / scale
            weights = jax.nn.softmax(logits, axis=-1)
            ctx = jnp.einsum('bhqt,bthk->bqhk', weights, vh).reshape(b, q_len, H * K)
            return ctx @ wo + bo

        def _forward(x, xf_1, xf_2, ln1_scale, ln1_offset, wq1, bq1, wk1, bk1, wv1, bv1, wo1, bo1, bias_k1, bias_v1, ln2_scale, ln2_offset, wq2, bq2, wk2, bk2, wv2, bv2, wo2, bo2, bias_k2, bias_v2, ln_mlp_scale, ln_mlp_offset, w_fc1, b_fc1, w_fc2, b_fc2):
            res = x
            h = _layer_norm(x, ln1_scale, ln1_offset)
            x = res + _cross_attention(h, xf_1, wq1, bq1, wk1, bk1, wv1, bv1, wo1, bo1, bias_k1, bias_v1)
            res = x
            h = _layer_norm(x, ln2_scale, ln2_offset)
            x = res + _cross_attention(h, xf_2, wq2, bq2, wk2, bk2, wv2, bv2, wo2, bo2, bias_k2, bias_v2)
            h = _layer_norm(x, ln_mlp_scale, ln_mlp_offset)
            h = jax.nn.gelu(h @ w_fc1 + b_fc1, approximate=False) @ w_fc2 + b_fc2
            return x + h
        return _forward(x, xf_1, xf_2, ln1_scale, ln1_offset, wq1, bq1, wk1, bk1, wv1, bv1, wo1, bo1, bias_k1, bias_v1, ln2_scale, ln2_offset, wq2, bq2, wk2, bk2, wv2, bv2, wo2, bo2, bias_k2, bias_v2, ln_mlp_scale, ln_mlp_offset, w_fc1, b_fc1, w_fc2, b_fc2)
    x = _L0_xattn_ref(x, ctx_2048, L0_xattn_ln1_w, L0_xattn_ln1_b, L0_xattn_ln2_w, L0_xattn_ln2_b, L0_xattn_maa_x, L0_xattn_maa_w1, L0_xattn_maa_w2, L0_xattn_maa_stack, L0_xattn_time_decay, L0_xattn_decay_w1, L0_xattn_decay_w2, L0_xattn_faaaa, L0_xattn_Wr, L0_xattn_Wk, L0_xattn_Wv, L0_xattn_Wg, L0_xattn_Wo, L0_xattn_gn_w, L0_xattn_gn_b, L0_xattn_ffn_maa_k, L0_xattn_ffn_maa_r, L0_xattn_ffn_Wk, L0_xattn_ffn_Wr, L0_xattn_ffn_Wv, 0)
    x = _L1_xattn_ref(x, ctx_2048, mask_BxS2_bf1, L1_xattn_Wq, L1_xattn_Wk, L1_xattn_Wv, L1_xattn_Wo, L1_xattn_ln_gamma, L1_xattn_ln_beta, L1_xattn_gate)
    x = _L2_xattn_ref(x, ctx_2048, L2_xattn_ln1_w, L2_xattn_ln1_b, L2_xattn_ln2_w, L2_xattn_ln2_b, L2_xattn_maa_x, L2_xattn_maa_w1, L2_xattn_maa_w2, L2_xattn_maa_stack, L2_xattn_time_decay, L2_xattn_decay_w1, L2_xattn_decay_w2, L2_xattn_faaaa, L2_xattn_Wr, L2_xattn_Wk, L2_xattn_Wv, L2_xattn_Wg, L2_xattn_Wo, L2_xattn_gn_w, L2_xattn_gn_b, L2_xattn_ffn_maa_k, L2_xattn_ffn_maa_r, L2_xattn_ffn_Wk, L2_xattn_ffn_Wr, L2_xattn_ffn_Wv, 0)
    x = _L3_xattn_ref(x, ctx_2048, ctx_2048, L3_xattn_ln1_scale, L3_xattn_ln1_offset, L3_xattn_wq1, L3_xattn_bq1, L3_xattn_wk1, L3_xattn_bk1, L3_xattn_wv1, L3_xattn_bv1, L3_xattn_wo1, L3_xattn_bo1, L3_xattn_bias_k1, L3_xattn_bias_v1, L3_xattn_ln2_scale, L3_xattn_ln2_offset, L3_xattn_wq2, L3_xattn_bq2, L3_xattn_wk2, L3_xattn_bk2, L3_xattn_wv2, L3_xattn_bv2, L3_xattn_wo2, L3_xattn_bo2, L3_xattn_bias_k2, L3_xattn_bias_v2, L3_xattn_ln_mlp_scale, L3_xattn_ln_mlp_offset, L3_xattn_w_fc1, L3_xattn_b_fc1, L3_xattn_w_fc2, L3_xattn_b_fc2)
    return x

_drawn_inputs = setup_inputs


def setup_inputs(seed=0):
    import zlib

    import numpy as np

    out = dict(_drawn_inputs(seed))
    spreads = {'L0_xattn_ln1_w': (1.0, 0.564),
     'L0_xattn_ln1_b': (0.0, 0.572),
     'L0_xattn_ln2_w': (1.0, 0.6),
     'L0_xattn_ln2_b': (0.0, 0.8),
     'L0_xattn_gn_w': (1.0, 0.6),
     'L0_xattn_gn_b': (0.0, 0.8),
     'L1_xattn_ln_gamma': (1.0, 0.6),
     'L1_xattn_ln_beta': (0.0, 2.0),
     'L2_xattn_ln1_w': (1.0, 0.551),
     'L2_xattn_ln1_b': (0.0, 0.595),
     'L2_xattn_ln2_w': (1.0, 0.6),
     'L2_xattn_ln2_b': (0.0, 0.8),
     'L2_xattn_gn_w': (1.0, 0.6),
     'L2_xattn_gn_b': (0.0, 0.8),
     'L3_xattn_ln1_scale': (1.0, 0.6),
     'L3_xattn_ln1_offset': (0.0, 2.0),
     'L3_xattn_bq1': (0.0, 2.0),
     'L3_xattn_bk1': (0.0, 2.0),
     'L3_xattn_bv1': (0.0, 0.1),
     'L3_xattn_bo1': (0.0, 0.1),
     'L3_xattn_ln2_scale': (1.0, 0.6),
     'L3_xattn_ln2_offset': (0.0, 2.0),
     'L3_xattn_bq2': (0.0, 2.0),
     'L3_xattn_bk2': (0.0, 2.0),
     'L3_xattn_bv2': (0.0, 0.1),
     'L3_xattn_bo2': (0.0, 0.1),
     'L3_xattn_ln_mlp_scale': (1.0, 0.6),
     'L3_xattn_ln_mlp_offset': (0.0, 0.774),
     'L3_xattn_b_fc1': (0.0, 0.609),
     'L3_xattn_b_fc2': (0.0, 0.1)}
    factors = {'L0_xattn_maa_x': 8.0,
     'L0_xattn_maa_w1': 6.944,
     'L0_xattn_maa_w2': 6.96,
     'L0_xattn_maa_stack': 8.0,
     'L0_xattn_time_decay': 2.778,
     'L0_xattn_decay_w1': 8.0,
     'L0_xattn_decay_w2': 8.0,
     'L0_xattn_faaaa': 5.559,
     'L0_xattn_ffn_maa_k': 8.0,
     'L0_xattn_ffn_maa_r': 8.0,
     'L0_xattn_ffn_Wk': 3.08,
     'L0_xattn_ffn_Wr': 8.0,
     'L0_xattn_ffn_Wv': 2.845,
     'L1_xattn_Wq': 8.0,
     'L1_xattn_Wk': 8.0,
     'L2_xattn_maa_x': 8.0,
     'L2_xattn_maa_w1': 7.292,
     'L2_xattn_maa_w2': 7.296,
     'L2_xattn_maa_stack': 8.0,
     'L2_xattn_time_decay': 2.804,
     'L2_xattn_decay_w1': 8.0,
     'L2_xattn_decay_w2': 8.0,
     'L2_xattn_faaaa': 5.626,
     'L2_xattn_ffn_maa_k': 8.0,
     'L2_xattn_ffn_maa_r': 8.0,
     'L2_xattn_ffn_Wk': 3.042,
     'L2_xattn_ffn_Wr': 8.0,
     'L2_xattn_ffn_Wv': 2.829,
     'L3_xattn_wq1': 33.569,
     'L3_xattn_wk1': 44.286,
     'L3_xattn_wv1': 4.117,
     'L3_xattn_bias_k1': 64.0,
     'L3_xattn_bias_v1': 64.0,
     'L3_xattn_wq2': 33.662,
     'L3_xattn_wk2': 46.975,
     'L3_xattn_wv2': 4.053,
     'L3_xattn_bias_k2': 64.0,
     'L3_xattn_bias_v2': 59.341}
    for name, (base, spread) in spreads.items():
        noise = np.random.default_rng([zlib.crc32(name.encode()), seed]).standard_normal(out[name].shape)
        drawn = base * np.exp(spread * noise) if base else spread * noise
        out[name] = jnp.asarray(drawn.astype(out[name].dtype))
    for name, factor in factors.items():
        out[name] = (out[name] * factor).astype(out[name].dtype)
    return out
```

```python
from contextlib import ExitStack

import concourse.bass as bass
from concourse import mybir

F32 = mybir.dt.float32
F32R = mybir.dt.float32r
U8 = mybir.dt.uint8
ALU = mybir.AluOpType
ACT = mybir.ActivationFunctionType
AX_X = mybir.AxisListType.X

P = 128
B, T, E = 4, 256, 256
NTOK = B * T
C = E // P
TILES = NTOK // P
HALF = 512
S = 8
EPS = 1e-5
H1, D1 = 16, 16
HPC = P // D1
H3, D3 = 16, 128
KEYS = T + 2
F3 = 1024
FT = F3 // P

W1, W2, DW1, DW2 = 0, 2 * 256, 2 * 256 + 5 * 256, 2 * 256 + 5 * 256 + 2 * 128
WK, WV, WR, WG, WO, FK, FR, FV = (DW2 + 256 + 512 * i for i in range(8))
NW = FV + 512
LN1W, LN1B, LN2W, LN2B, MAAX, STACK, TD, GNW, GNB, FMK, FMR = 0, 2, 4, 6, 8, 10, 20, 22, 24, 26, 28
UCOL = 30
NV = UCOL + S
G1, B1, GATE, LN3, BFC1 = 0, 2, 4, 5, 17
BQ, BK, BIASK = (BFC1 + FT + 32 * i for i in range(3))
HMASK = BIASK + 32
NVA = HMASK + HPC
MOST_NEGATIVE = -3.0e38
MIX = [1, 0, 2, 3, 4]
POOL_K = 3


def build_program(nc, x_in, ctx_in, mask_in, prev_in, s0_in, const_in, wrk_in, vec_in, veca_in,
                  w1l_in, w3_in, rows_in, bv_in, biasv_in, fc1_in, fc2_in, out):
    with ExitStack() as stack:
        def sem(name):
            return stack.enter_context(nc.semaphore(name))

        def sb(name, shape, dt=F32, where=stack):
            return where.enter_context(nc.sbuf_tensor(name, shape, dt))

        X = sb("X", [P, TILES, E])
        XNT = sb("XNT", [P, TILES, E])
        STAT = sb("STAT", [P, TILES, 6])
        MV = sb("MV", [P, TILES, 2])
        VE = sb("VE", [P, 3, TILES])
        CONST = sb("CONST", [P, 3, P])
        IDENT, CENTER, MEAN8 = CONST[:, 0, :], CONST[:, 1, :], CONST[:, 2, :]
        EPSC = sb("EPSC", [P, 1])
        VEC = sb("VEC", [P, 2, NV])
        VECA = sb("VECA", [P, NVA])
        PREV = sb("PREV", [P, 2, TILES])
        S0 = sb("S0", [P, S * S])
        CTh = sb("CTh", [P, C, NTOK], F32R)
        CTl = sb("CTl", [P, C, NTOK], F32R)
        KV1 = sb("KV1", [P, 2, 2048])
        K1 = KV1[:, 0, :].rearrange("p (c t) -> p c t", c=C)
        V1 = KV1[:, 1, :].rearrange("p (m d) -> p m d", m=TILES)
        W1L = sb("W1L", [P, 4, C, E])
        BFC2 = sb("BFC2", [P, E])
        CF = sb("CF", [P, T])

        with ExitStack() as scope:
            AR = sb("AR", [P, 14 * 2048 + 2056], F32, scope)
            WRK = sb("WRK", [P, NW], F32, scope)
        with ExitStack() as scope:
            Q1h = sb("Q1h", [P, C, NTOK], F32R, scope)
            Q1l = sb("Q1l", [P, C, NTOK], F32R, scope)
            KMh = sb("KMh", [P, 2, NTOK], F32R, scope)
            KMl = sb("KMl", [P, 2, NTOK], F32R, scope)
            XT1 = sb("XT1", [P, C, NTOK], F32, scope)
            MU8 = sb("MU8", [P, B * T], U8, scope)
            MASKB = sb("MASKB", [P, B * T], F32, scope)
            SM = sb("SM", [P, 2, 2, T], F32, scope)
            P1 = sb("P1", [P, 2, 2, T], F32, scope)
            PT1 = sb("PT1", [P, 2, 2, T], F32, scope)
            NM1 = sb("NM1", [P, 2, 2], F32, scope)
            NS1 = sb("NS1", [P, 2, 2], F32, scope)
            RS1 = sb("RS1", [P, 2, TILES], F32, scope)
            RI1 = sb("RI1", [P, 2, TILES], F32, scope)
            AO = sb("AO", [P, TILES, E], F32, scope)
            AOT = sb("AOT", [P, C, NTOK], F32, scope)
            GT = sb("GT", [P, 1], F32, scope)
            CARRY = sb("CARRY", [P, 1], F32, scope)
        with ExitStack() as scope:
            HF = sb("HF", [P, C, NTOK], F32, scope)
            Hh = sb("Hh", [P, C, NTOK], F32R, scope)
            Hl = sb("Hl", [P, C, NTOK], F32R, scope)
            W3 = sb("W3", [P, 2, 4, E], F32, scope)
            W3h = sb("W3h", [P, 2, 4, E], F32R, scope)
            W3l = sb("W3l", [P, 2, 4, E], F32R, scope)
            Q3h = sb("Q3h", [P, 2, NTOK], F32R, scope)
            Q3l = sb("Q3l", [P, 2, NTOK], F32R, scope)
            K3h = sb("K3h", [P, 2, B, KEYS], F32R, scope)
            K3l = sb("K3l", [P, 2, B, KEYS], F32R, scope)
            V3 = sb("V3", [P, TILES, D3], F32, scope)
            V3h = sb("V3h", [P, 2, TILES, D3], F32R, scope)
            V3l = sb("V3l", [P, 2, TILES, D3], F32R, scope)
            HB = sb("HB", [P, 2, 3], F32, scope)
            BV = sb("BV", [P, 2, D3], F32, scope)
            P3 = sb("P3", [P, 2, 2, KEYS], F32, scope)
            PT3h = sb("PT3h", [P, 2, 2, T], F32R, scope)
            PT3l = sb("PT3l", [P, 2, 2, T], F32R, scope)
            C3h = sb("C3h", [P, 2, NTOK], F32R, scope)
            C3l = sb("C3l", [P, 2, NTOK], F32R, scope)
            NM3 = sb("NM3", [P, 2, 2], F32, scope)
            NS3 = sb("NS3", [P, 2, 2], F32, scope)
            RS3 = sb("RS3", [P, 2, 2], F32, scope)
            RI3 = sb("RI3", [P, 2, 2], F32, scope)
            PB = sb("PB", [P, TILES, 32], F32, scope)
            PBT = sb("PBT", [32, NTOK], F32, scope)
            BVD = sb("BVD", [P, H3, 32], F32, scope)
            WAUX = sb("WAUX", [32, E], F32, scope)
        WOALL = KV1[:, :, :].rearrange("p k (h e) -> p (k h) e", e=E)
        with ExitStack() as scope:
            HM3 = sb("HM3", [P, C, NTOK], F32, scope)
            G3 = sb("G3", [P, FT, NTOK], F32, scope)
        FC1 = W1L[:, :, :, :].rearrange("p w c e -> p (w c e)").rearrange("p (c f) -> p c f", c=C)
        FC2 = KV1[:, 0, :].rearrange("p (f e) -> p f e", f=FT)

        def slot(i, n=1):
            return AR[:, i * 2048:(i + n) * 2048]

        def fm(i):
            return slot(i).rearrange("p (a t) -> p a t", a=8)

        XN = AR[:, 14 * 2048:14 * 2048 + 2056].rearrange("p (a t) -> p a t", a=8)
        SX = fm(1)
        X5 = [fm(2), fm(3), fm(4)]
        KT, VT, RT, WT = (fm(i) for i in (5, 6, 7, 8))
        KS, VS, RS, WS = (fm(i) for i in (9, 10, 11, 12))
        M1 = slot(11).rearrange("p (m t) -> p m t", m=2)
        DT = slot(13)[:, 0:NTOK]
        TH = fm(0)
        G2 = fm(13)
        RK, T1 = fm(4), fm(1)
        AK = [fm(2), fm(3)]
        MK = [fm(8), fm(0)]
        SS = [AR[:, 5 * 2048 + 2056 * i:5 * 2048 + 2056 * (i + 1)].rearrange("p (d t) -> p d t", d=S)
              for i in (0, 1)]
        AS, ATT, SQ, SD, YT = (fm(i) for i in (4, 9, 10, 11, 12))
        XK, XR, KK, KK2, RR, FT1 = (fm(i) for i in (2, 3, 4, 5, 6, 7))
        CRAW = slot(9).rearrange("p (m d) -> p m d", m=TILES)
        AT = fm(12)

        banks = [stack.enter_context(nc.psum_tensor(f"bank{i}", [P, 512], F32)) for i in range(8)]

        ld_x, ld_c, ld_small, ld_wrk, ld_w1l, ld_mask = (sem(n) for n in (
            "ld_x", "ld_c", "ld_small", "ld_wrk", "ld_w1l", "ld_mask"))
        eps_set, gate_done = sem("eps_set"), sem("gate_done")
        ln_stats, ln_mv, ln_var, ln_root, ln_inv, ln_rows = (sem(n) for n in (
            "ln_stats", "ln_mv", "ln_var", "ln_root", "ln_inv", "ln_rows"))
        turned = sem("turned")
        x_sum = sem("x_sum")
        ct_hi, ct_lo, at_ready, k1_proj, k1_hi, k1_lo, v1_proj, v1_ready, mask_f, mask_r, mask_b = (
            sem(n) for n in ("ct_hi", "ct_lo", "at_ready", "k1_proj", "k1_hi", "k1_lo", "v1_proj",
                             "v1_ready", "mask_f", "mask_r", "mask_b"))
        xn_ready, sx_ready, xmix_ready, m1_ready, m1_tanh, mix_ready, mix_scaled, x5_ready = (
            sem(n) for n in ("xn_ready", "sx_ready", "xmix_ready", "m1_ready", "m1_tanh", "mix_ready",
                             "mix_scaled", "x5_ready"))
        proj_ready, proj_out, decay_e, gate_th, g_ready = (
            sem(n) for n in ("proj_ready", "proj_out", "decay_e", "gate_th", "g_ready"))
        moved = {n: sem(f"moved_{n}") for n in "wkvra"}
        coef_rk, coef_ready, bonus_ready, state0, outer_dve, outer_pool, scanned, read_out, summed = (
            sem(n) for n in ("coef_rk", "coef_ready", "bonus_ready", "state0", "outer_dve", "outer_pool",
                             "scanned", "read_out", "summed"))
        att_out, centered, squared, gvar, groot, ginv, gnorm, gaff, y_ready, wo_ready = (
            sem(n) for n in ("att_out", "centered", "squared", "gvar", "groot", "ginv", "gnorm", "gaff",
                             "y_ready", "wo_ready"))
        xkr_ready, fk_ready, fk_pos, fk_sq, fr_ready, fr_th, fv_ready, fv_mul = (
            sem(n) for n in ("xkr_ready", "fk_ready", "fk_pos", "fk_sq", "fr_ready", "fr_th", "fv_ready",
                             "fv_mul"))
        xt_ready, q1_proj, q1_hi, q1_lo, km_hi, km_lo = (
            sem(n) for n in ("xt_ready", "q1_proj", "q1_hi", "q1_lo", "km_hi", "km_lo"))
        sc_ready, sc_masked, sc_max, p1_ready, p1_turned, pt_dve, pt_act, pv_done, o_inv, o_out = (
            sem(n) for n in ("sc_ready", "sc_masked", "sc_max", "p1_ready", "p1_turned", "pt_dve", "pt_act",
                             "pv_done", "o_inv", "o_out"))
        ao_turned, out1_ready = sem("ao_turned"), sem("out1_ready")
        ld_w3, ld_bv = ([sem(f"{n}{par}") for par in range(2)] for n in ("ld_w3_", "ld_bv_"))
        ld_wo, ld_aux, ld_bo, ld_fc1, ld_fc2, ld_bfc2 = (
            sem(n) for n in ("ld_wo", "ld_aux", "ld_bo", "ld_fc1", "ld_fc2", "ld_bfc2"))
        hb_ready = sem("hb_ready")
        h_rows, h_hi, h_lo, w3_hi, w3_lo, wo_hi, wo_lo, key_hi, key_lo = (
            sem(n) for n in ("h_rows", "h_hi", "h_lo", "w3_hi", "w3_lo", "wo_hi", "wo_lo", "key_hi", "key_lo"))
        qk_full, qk_hi, qk_lo, v_full, v_added, v_hi, v_lo, o_full, o_added = (
            sem(n) for n in ("qk_full", "qk_hi", "qk_lo", "v_full", "v_added", "v_hi", "v_lo", "o_full",
                             "o_added"))
        s3_ready, s3_max, s3_shift, p3_ready, p3_inv, p3_scaled, p3_bias, p3_turned, pt3_hi, pt3_lo = (
            sem(n) for n in ("s3_ready", "s3_max", "s3_shift", "p3_ready", "p3_inv", "p3_scaled", "p3_bias",
                             "p3_turned", "pt3_hi", "pt3_lo"))
        c3_ready, c3_hi, c3_lo = sem("c3_ready"), sem("c3_hi"), sem("c3_lo")
        pb_clear, pb_one, aux_ready, waux_out, pb_turned, pbt_out, aux_rows = (
            sem(n) for n in ("pb_clear", "pb_one", "aux_ready", "waux_out", "pb_turned", "pbt_out", "aux_rows"))
        hm_ready, fc1_ready, gelu_out, fc2_ready = (
            sem(n) for n in ("hm_ready", "fc1_ready", "gelu_out", "fc2_ready"))
        stored = sem("stored")

        block = stack.enter_context(nc.Block())

        def lnw(li, col, c):
            return VEC[:, li, col + c:col + c + 1]

        def ln_dve(dve, n, src):
            for m in range(TILES):
                nc.vector.bn_stats(STAT[:, m, :], src[:, m, :]).then_inc(ln_stats, 1)
            for m in range(TILES):
                dve.wait_ge(ln_stats, TILES * n + m + 1)
                nc.vector.bn_aggr(MV[:, m, :], STAT[:, m, :]).then_inc(ln_mv, 1)
            dve.wait_ge(ln_mv, TILES * (n + 1))
            nc.vector.tensor_scalar(VE[:, 0, :], MV[:, :, 1], EPS, None, ALU.add).then_inc(ln_var, 1)
            dve.wait_ge(ln_root, n + 1)
            nc.vector.reciprocal(VE[:, 2, :], VE[:, 1, :]).then_inc(ln_inv, 1)
            dve.wait_ge(ln_inv, n + 1)
            for m in range(TILES):
                nc.vector.tensor_scalar(XNT[:, m, :], src[:, m, :], MV[:, m, 0:1], VE[:, 2, m:m + 1],
                                        ALU.subtract, ALU.mult).then_inc(ln_rows, 1)

        def ln_act(act, n):
            act.wait_ge(ln_var, n + 1)
            nc.scalar.activation(VE[:, 1, :], VE[:, 0, :], ACT.Sqrt).then_inc(ln_root, 1)

        def turn(pe, src, c, hf):
            for k in range(4):
                last = nc.tensor.transpose(banks[2 * c + hf][:, k * P:(k + 1) * P],
                                           src[:, 4 * hf + k, c * P:(c + 1) * P], IDENT)
            last.then_inc(turned, 1)

        def ln_turn(pe, n):
            for hf in range(2):
                pe.wait_ge(ln_rows, TILES * n + 4 * hf + 4)
                for c in range(C):
                    turn(pe, XNT, c, hf)

        TURN_ORDER = [(c, hf) for hf in range(2) for c in range(C)]

        def g_par(j):
            return j % 2

        def wait_pt(eng, i, j):
            h, b = 2 * i + j // 4, j % 4
            if b == 0:
                eng.wait_ge(pt_dve, h + 1)
            else:
                eng.wait_ge(pt_act, 3 * h + b)

        Q0, K0, Q1, K1_, V0, V1_ = ("qk", 0), ("qk", 1), ("qk", 2), ("qk", 3), ("v", 0), ("v", 1)
        NEXT = [[(*Q0, 1), (*K0, 1)], [(*V0, 1)], [(*Q1, 1), (*K1_, 1)], [(*V1_, 1)]]
        OUTS = [[("o", b - 3, 0)] for b in range(4)]
        ORDER = {
            "prologue": (0, [None, None], [[(*x, 0) for x in (Q0, K0, V0, Q1, K1_, V1_)]]),
            "first": (0, [(*K1_, 0), (*V1_, 0)], [NEXT[0], NEXT[1], NEXT[2], NEXT[3] + OUTS[3]]),
            "steady": (1, [(*V1_, 0), ("o", -4, 0)], [NEXT[b] + OUTS[b] for b in range(4)]),
            "last": (1, [(*V1_, 0), ("o", -4, 0)], OUTS),
            "end": (1, [("o", -1, 0), ("o", 0, 0)], [[("o", 1, 0), ("o", 2, 0), ("o", 3, 0)]]),
        }

        def products(case, b):
            bank, before, slots = ORDER[case]
            line = before + [x for y in slots for x in y]
            at = sum(len(y) for y in slots[:b])
            return [(*x, 6 + (bank + at + m) % 2, line[at + m]) for m, x in enumerate(slots[b])]

        def wait_taken(eng, H, product):
            if product is not None:
                kind, n, dh = product
                if kind == "qk":
                    eng.wait_ge(qk_lo, 4 * (H + dh) + n + 1)
                elif kind == "v":
                    eng.wait_ge(v_added, 2 * (H + dh) + n + 1)
                else:
                    eng.wait_ge(o_added, 4 * H + n + 1)

        def wait_loaded(eng, sems, H, par):
            eng.wait_ge(sems[par], 8 * (H - par) + 16)

        def attention_heads(eng, a, head):
            head(16 * a, 0, "first")
            head(16 * a + 1, 1, "steady")
            with eng.Fori(8 * a + 1, 8 * a + 7) as i:
                head(2 * i, 0, "steady")
                head(2 * i + 1, 1, "steady")
            head(16 * a + 14, 0, "steady")
            head(16 * a + 15, 1, "last")

        def lagged(case, b, lag):
            return not (case == "first" and b < lag)

        @block.sync
        def _(sp):
            sp.dma_start(CRAW, ctx_in.rearrange("b (h p) d -> p (b h) d", p=P)).then_inc(ld_c, 16)
            for dst, src in ((CONST[:, :, :], const_in), (VEC[:, :, :], vec_in), (VECA[:, :], veca_in),
                             (PREV[:, :, :], prev_in), (S0[:, :], s0_in)):
                sp.dma_start(dst, src).then_inc(ld_small, 16)
            sp.dma_start(W1L[:, :, :, :], w1l_in).then_inc(ld_w1l, 16)
            sp.dma_start(X[:, :, :], x_in.rearrange("b (h p) d -> p (b h) d", p=P)).then_inc(ld_x, 16)
            sp.dma_start(WRK[:, :], wrk_in[0]).then_inc(ld_wrk, 16)

            def to_scan(src, dst, name):
                for b in range(B):
                    for c in range(C):
                        p0 = 32 * b + 16 * c
                        sp.dma_start(dst[p0:p0 + 16, :, :], src[:, 4 * c + b, :]).then_inc(moved[name], 16)

            def rwkv_moves(li):
                for n, (src, dst, name) in enumerate(((WT, WS, "w"), (KT, KS, "k"), (VT, VS, "v"),
                                                      (RT, RS, "r"))):
                    if name == "w":
                        sp.wait_ge(decay_e, 4 * (li + 1))
                    else:
                        sp.wait_ge(proj_out, 18 * li + 2 + 4 * (n + 1))
                    to_scan(src, dst, name)
                sp.wait_ge(att_out, 4 * (li + 1))
                for b in range(B):
                    for c in range(C):
                        p0 = 32 * b + 16 * c
                        sp.dma_start(ATT[:, 4 * c + b, :], AS[p0:p0 + 16, :, :]).then_inc(moved["a"], 16)

            rwkv_moves(0)
            sp.wait_ge(x_sum, 8)
            sp.dma_start(MU8[:, :], mask_in.to_broadcast([P, B * T])).then_inc(ld_mask, 16)
            sp.dma_start(WRK[:, :], wrk_in[1]).then_inc(ld_wrk, 16)
            rwkv_moves(1)

            def load_head(H, par):
                sp.dma_start(W3[:, par, :, :], w3_in[bass.ds(H, 1), :, :, :].rearrange("o p w e -> p (o w) e")
                             ).then_inc(ld_w3[par], 16)
                sp.dma_start(BV[:, par, :], bv_in[bass.ds(H, 1), :].to_broadcast([P, D3])).then_inc(ld_bv[par], 16)

            def load_aux(a):
                sp.dma_start(WOALL, w3_in[H3 * a:H3 * (a + 1), :, 3, :].rearrange("h p e -> p h e")).then_inc(ld_wo, 16)
                sp.dma_start(BVD[:, :, :], biasv_in[a]).then_inc(ld_aux, 16)
                sp.wait_ge(waux_out, a + 1)
                sp.dma_start(WAUX[16:17, :], rows_in[a:a + 1, :]).then_inc(ld_bo, 16)

            def next_head(H, par):
                sp.wait_ge(w3_lo, H + 1)
                sp.wait_ge(wo_lo, H + 1)
                sp.wait_ge(v_added, 2 * H + 2)
                load_head(H + 2, par)

            sp.wait_ge(x_sum, 20)
            load_head(0, 0)
            load_head(1, 1)
            load_aux(0)
            sp.dma_start(FC1, fc1_in).then_inc(ld_fc1, 16)
            sp.dma_start(BFC2[:, :], rows_in[2:3, :].to_broadcast([P, E])).then_inc(ld_bfc2, 16)
            with sp.Fori(0, 8) as i:
                next_head(2 * i, 0)
                next_head(2 * i + 1, 1)
            sp.wait_ge(x_sum, 24)
            load_aux(1)
            with sp.Fori(8, 15) as i:
                next_head(2 * i, 0)
                next_head(2 * i + 1, 1)
            sp.dma_start(FC2, fc2_in).then_inc(ld_fc2, 16)
            for pair in range(4):
                sp.wait_ge(x_sum, 30 + pair)
                sp.dma_start(out.rearrange("b (h p) d -> p (b h) d", p=P)[:, 2 * pair:2 * pair + 2, :],
                             X[:, 2 * pair:2 * pair + 2, :]).then_inc(stored, 16)
            sp.wait_ge(stored, 64)

        @block.tensor
        def _(pe):
            def proj(bank, w, col, rhs, hf, m=0, stride=E):
                for c in range(C):
                    last = nc.tensor.matmul(banks[bank][:, :], w[:, col + stride * c + P * m:col + stride * c + P * m + P],
                                            rhs[:, 4 * c + 2 * hf:4 * c + 2 * hf + 2, :], start=(c == 0),
                                            stop=(c == C - 1))
                return last

            def rows(bank, w, rhs, pair):
                for k in range(2):
                    m = 2 * pair + k
                    for c in range(C):
                        last = nc.tensor.matmul(banks[bank][:, k * E:(k + 1) * E],
                                                rhs[:, 4 * c + m // 2, (m % 2) * P:(m % 2) * P + P],
                                                w[:, c * E:(c + 1) * E], start=(c == 0), stop=(c == C - 1))
                return last

            def context():
                pe.wait_ge(ld_c, 16)
                pe.wait_ge(ld_small, 80)
                for c, hf in TURN_ORDER:
                    turn(pe, CRAW, c, hf)
                pe.wait_ge(ct_hi, 4)
                pe.wait_ge(ct_lo, 4)
                ln_turn(pe, 0)
                pe.wait_ge(ld_w1l, 16)
                pe.wait_ge(at_ready, 4)
                for m in range(C):
                    for hf in range(2):
                        proj(4 + 2 * m + hf, W1L[:, 1, :, :].rearrange("p c e -> p (c e)"), 0, AT, hf, m).then_inc(k1_proj, 1)
                for pair in range(4):
                    rows(pair, W1L[:, 2, :, :].rearrange("p c e -> p (c e)"), AT, pair).then_inc(v1_proj, 1)

            def rwkv(li, n_ln, xs):
                pe.wait_ge(ld_wrk, 16 * (li + 1))
                ln_turn(pe, n_ln)
                for m in range(2):
                    for hf in range(2):
                        pe.wait_ge(xmix_ready, 2 * (li + 1))
                        proj(4 + 2 * m + hf, WRK, W1, X5[2], hf, m).then_inc(m1_ready, 1)
                pe.wait_ge(m1_tanh, 4 * (li + 1))

                def mix(n):
                    j = MIX[n]
                    for q in range(4):
                        c, hf = q // 2, q % 2
                        if n:
                            pe.wait_ge(mix_scaled, 20 * li + 4 * n + q - 3)
                        nc.tensor.matmul(banks[q][:, :], WRK[:, W2 + 256 * j + P * c:W2 + 256 * j + P * c + P],
                                         M1[:, j // 4, hf * HALF:(hf + 1) * HALF], start=True,
                                         stop=True).then_inc(mix_ready, 1)

                def project(n, col):
                    pe.wait_ge(x5_ready, 20 * li + 4 * (n + 1))
                    for q in range(4):
                        if n == 1:
                            pe.wait_ge(decay_e, 4 * li + q + 1)
                        else:
                            pe.wait_ge(proj_out, 18 * li + 2 + 4 * (n - 1) + q + 1)
                        proj(4 + q, WRK, col, X5[n % 3], q % 2, q // 2).then_inc(proj_ready, 1)

                mix(0)
                mix(1)
                pe.wait_ge(x5_ready, 20 * li + 4)
                for hf in range(2):
                    proj(4 + hf, WRK, DW1, X5[0], hf, 0, P).then_inc(proj_ready, 1)
                mix(2)
                pe.wait_ge(proj_out, 18 * li + 2)
                for q in range(4):
                    c, hf = q // 2, q % 2
                    nc.tensor.matmul(banks[4 + q][:, :], WRK[:, DW2 + P * c:DW2 + P * c + P],
                                     DT[:, hf * HALF:(hf + 1) * HALF], start=True, stop=True).then_inc(proj_ready, 1)
                project(1, WK)
                mix(3)
                project(2, WV)
                mix(4)
                project(3, WR)
                project(4, WG)
                for k in range(9):
                    for q in range(4):
                        if k == 0:
                            pe.wait_ge(bonus_ready, li + 1)
                            src = T1
                        else:
                            pe.wait_ge(read_out, 8 * li + k)
                            src = MK[(k - 1) % 2]
                        last = nc.tensor.matmul(banks[q][:, :], IDENT, src[:, 2 * q:2 * q + 2, :],
                                                start=(k == 0), stop=(k == 8), skip_group_check=True)
                    last.then_inc(summed, 1)
                for q in range(4):
                    c, hf = q // 2, q % 2
                    if q == 0:
                        pe.wait_ge(moved["a"], 128 * (li + 1))
                        pe.wait_ge(g_ready, 4 * (li + 1))
                    nc.tensor.matmul(banks[4 + q][:, :], CENTER, ATT[:, 4 * c + 2 * hf:4 * c + 2 * hf + 2, :],
                                     start=True, stop=True).then_inc(centered, 1)
                for q in range(4):
                    c, hf = q // 2, q % 2
                    pe.wait_ge(squared, 4 * li + q + 1)
                    nc.tensor.matmul(banks[q][:, :], MEAN8, SQ[:, 4 * c + 2 * hf:4 * c + 2 * hf + 2, :],
                                     start=True, stop=True).then_inc(gvar, 1)
                pe.wait_ge(groot, 4 * (li + 1))
                for pair in range(4):
                    pe.wait_ge(y_ready, 4 * (li + 1))
                    rows(pair, WRK[:, WO:WO + 512], YT, pair).then_inc(wo_ready, 1)
                pe.wait_ge(x_sum, xs + 4)
                ln_turn(pe, n_ln + 1)
                for q in range(4):
                    pe.wait_ge(xkr_ready, 4 * li + 2)
                    proj(4 + q, WRK, FK, XK, q % 2, q // 2).then_inc(fk_ready, 1)
                pe.wait_ge(xkr_ready, 4 * li + 4)
                for pair in range(4):
                    rows(pair, WRK[:, FR:FR + 512], XR, pair).then_inc(fr_ready, 1)
                pe.wait_ge(fk_sq, 4 * (li + 1))
                for pair in range(4):
                    rows(4 + pair, WRK[:, FV:FV + 512], KK2, pair).then_inc(fv_ready, 1)

            def unit_scores(i, j, c):
                g, h, b = 8 * i + j, 2 * i + j // 4, j % 4
                if b == 0:
                    pe.wait_ge(km_lo, h + 1)
                if not (isinstance(i, int) and g < 2):
                    pe.wait_ge(sc_max, g - 1)
                for tt in range(2):
                    qs = slice((2 * b + tt) * P, (2 * b + tt) * P + P)
                    ks = slice(b * T, (b + 1) * T)
                    for n, (q, k) in enumerate(((Q1h, KMh), (Q1h, KMl), (Q1l, KMh))):
                        last = nc.tensor.matmul(banks[g_par(j)][:, tt * T:(tt + 1) * T], q[:, c, qs],
                                                k[:, (j // 4) % 2, ks], start=(n == 0), stop=(n == 2))
                last.then_inc(sc_ready, 1)

            def unit_turn(i, j):
                g = 8 * i + j
                pe.wait_ge(p1_ready, g + 1)
                if not (isinstance(g, int) and g < 2):
                    wait_pt(pe, i, j - 2)
                for ss in range(2):
                    for tt in range(2):
                        last = nc.tensor.transpose(banks[2 + g_par(j)][:, ss * T + tt * P:ss * T + (tt + 1) * P],
                                                   P1[:, g_par(j), tt, ss * P:(ss + 1) * P], IDENT)
                last.then_inc(p1_turned, 1)

            def unit_values(i, j):
                g, h, b = 8 * i + j, 2 * i + j // 4, j % 4
                wait_pt(pe, i, j)
                if b == 0 and not (isinstance(h, int) and h < 2):
                    pe.wait_ge(o_out, h - 1)
                for tt in range(2):
                    for ss in range(2):
                        last = nc.tensor.matmul(banks[4 + (j // 4) % 2][:, (2 * b + tt) * D1:(2 * b + tt + 1) * D1],
                                                PT1[:, g_par(j), ss, tt * P:(tt + 1) * P],
                                                V1[:, 2 * b + ss, bass.ds(D1 * h, D1)], start=(ss == 0),
                                                stop=(ss == 1))
                last.then_inc(pv_done, 1)

            def audio():
                pe.wait_ge(x_sum, 8)
                for c, hf in TURN_ORDER:
                    turn(pe, X, c, hf)
                pe.wait_ge(xt_ready, 4)
                for q in range(4):
                    proj(4 + q, W1L[:, 0, :, :].rearrange("p c e -> p (c e)"), 0,
                         XT1[:, :, :].rearrange("p c (b t) -> p (c b) t", b=B), q % 2, q // 2).then_inc(q1_proj, 1)
                pe.wait_ge(q1_lo, 4)

                def body(i, c):
                    for j in range(8):
                        unit_scores(i, j, c)
                        if not (isinstance(i, int) and 8 * i + j < 1):
                            unit_turn(i, j - 1)
                        if not (isinstance(i, int) and 8 * i + j < 2):
                            unit_values(i, j - 2)

                body(0, 0)
                for c in range(2):
                    with pe.Fori(1 if c == 0 else 4, 4 * c + 4) as i:
                        body(i, c)
                unit_turn(8, -1)
                unit_values(8, -2)
                unit_values(8, -1)
                pe.wait_ge(o_out, H1)
                for c, hf in TURN_ORDER:
                    turn(pe, AO, c, hf)
                pe.wait_ge(ao_turned, 4)
                for pair in range(4):
                    rows(4 + pair, W1L[:, 3, :, :].rearrange("p c e -> p (c e)"),
                         AOT[:, :, :].rearrange("p c (b t) -> p (c b) t", b=B), pair).then_inc(out1_ready, 1)

            context()
            rwkv(0, 1, 0)
            audio()
            rwkv(1, 3, 12)

            def three(out_, lh, ll, rh, rl, first, last):
                nc.tensor.matmul(out_, lh, rh, start=first, stop=False)
                nc.tensor.matmul(out_, lh, rl, start=False, stop=False)
                return nc.tensor.matmul(out_, ll, rh, start=False, stop=last)

            def product(H, par, kind, n, dh, bank, before):
                wait_taken(pe, H, before)
                pr = (par + dh) % 2
                if kind == "qk":
                    hf, w = n // 2, n % 2
                    pe.wait_ge(w3_lo, H + dh + 1)
                    rh, rl = ((Hh, Hl), (CTh, CTl))[w]
                    for c in range(C):
                        cs, ts = slice(c * D3, (c + 1) * D3), slice(hf * HALF, (hf + 1) * HALF)
                        last = three(banks[bank][:, :], W3h[:, pr, w, cs], W3l[:, pr, w, cs], rh[:, c, ts],
                                     rl[:, c, ts], c == 0, c == C - 1)
                    last.then_inc(qk_full, 1)
                elif kind == "v":
                    pe.wait_ge(w3_lo, H + dh + 1)
                    for k in range(4):
                        for c in range(C):
                            ts, cs = slice((4 * n + k) * P, (4 * n + k + 1) * P), slice(c * D3, (c + 1) * D3)
                            last = three(banks[bank][:, k * D3:(k + 1) * D3], CTh[:, c, ts], CTl[:, c, ts],
                                         W3h[:, pr, 2, cs], W3l[:, pr, 2, cs], c == 0, c == C - 1)
                    last.then_inc(v_full, 1)
                else:
                    pr = par if n >= 0 else 1 - par
                    pe.wait_ge(c3_lo, 4 * H + n + 1)
                    pe.wait_ge(wo_lo, H + 1 if n >= 0 else H)
                    for tt in range(2):
                        ts = slice((2 * (n % 4) + tt) * P, (2 * (n % 4) + tt + 1) * P)
                        last = three(banks[bank][:, tt * E:(tt + 1) * E], C3h[:, pr, ts], C3l[:, pr, ts],
                                     W3h[:, pr, 3, :], W3l[:, pr, 3, :], True, True)
                    last.then_inc(o_full, 1)

            def scores3(H, par, b):
                pe.wait_ge(qk_lo, 4 * H + 2 * (b // 2) + 2)
                pe.wait_ge(key_lo, H + 1)
                for tt in range(2):
                    if not (isinstance(H, int) and 4 * H + b < 1):
                        pe.wait_ge(p3_ready, 8 * H + 2 * b - 1 + tt)
                    ts = slice((2 * b + tt) * P, (2 * b + tt + 1) * P)
                    three(banks[tt][:, 0:KEYS], Q3h[:, par, ts], Q3l[:, par, ts], K3h[:, par, b, :],
                          K3l[:, par, b, :], True, True).then_inc(s3_ready, 1)

            def turn3(H, par, b):
                pe.wait_ge(p3_scaled, 8 * H + 2 * b + 2)
                if not (isinstance(H, int) and 4 * H + b < 2):
                    pe.wait_ge(pt3_lo, 4 * H + b - 1)
                for ss in range(2):
                    for tt in range(2):
                        last = nc.tensor.transpose(banks[2 + b % 2][:, ss * T + tt * P:ss * T + (tt + 1) * P],
                                                   P3[:, b % 2, tt, ss * P:(ss + 1) * P], IDENT)
                last.then_inc(p3_turned, 1)

            def values3(H, par, b):
                pe.wait_ge(pt3_lo, 4 * H + b + 1)
                pe.wait_ge(v_lo, 2 * H + b // 2 + 1)
                if not (isinstance(H, int) and 4 * H + b < 2):
                    pe.wait_ge(c3_lo, 4 * H + b - 1)
                pr = par if b >= 0 else 1 - par
                for ss in range(2):
                    m = 2 * (b % 4) + ss
                    last = three(banks[4 + b % 2][:, 0:T], V3h[:, pr, m, :], V3l[:, pr, m, :],
                                 PT3h[:, b % 2, ss, :], PT3l[:, b % 2, ss, :], ss == 0, ss == 1)
                last.then_inc(c3_ready, 1)

            def head(H, par, case):
                for b in range(4):
                    scores3(H, par, b)
                    if lagged(case, b, 1):
                        turn3(H, par, b - 1)
                    todo = products(case, b)
                    for x in todo:
                        if x[0] != "o":
                            product(H, par, *x)
                    if lagged(case, b, 2):
                        values3(H, par, b - 2)
                    for x in todo:
                        if x[0] == "o":
                            product(H, par, *x)

            def bias_products(a):
                pe.wait_ge(ld_wo, 16 * (a + 1))
                pe.wait_ge(ld_aux, 16 * (a + 1))
                for h in range(H3):
                    last = nc.tensor.matmul(banks[4][0:32, 0:E], BVD[:, h, :], WOALL[:, h, :], start=(h == 0),
                                            stop=(h == H3 - 1))
                last.then_inc(aux_ready, 1)

            def bias_rows(a):
                pe.wait_ge(p3_bias, 64 * (a + 1))
                pe.wait_ge(pt3_lo, 64 * (a + 1))
                for m in range(TILES):
                    last = nc.tensor.transpose(banks[2 + m // 4][0:32, (m % 4) * P:(m % 4 + 1) * P], PB[:, m, :], IDENT)
                    if m % 4 == 3:
                        last.then_inc(pb_turned, 1)
                pe.wait_ge(pbt_out, 2 * (a + 1))
                pe.wait_ge(ld_bo, 16 * (a + 1))
                pe.wait_ge(c3_lo, 64 * (a + 1))
                for pair in range(4):
                    for k in range(2):
                        m = 2 * pair + k
                        last = nc.tensor.matmul(banks[(0, 1, 4, 5)[pair]][:, k * E:(k + 1) * E],
                                                PBT[0:32, m * P:(m + 1) * P], WAUX[0:32, :], start=True, stop=True)
                    last.then_inc(aux_rows, 1)

            for a in range(2):
                H0 = 16 * a
                pe.wait_ge(x_sum, 20 + 4 * a)
                bias_products(a)
                ln_turn(pe, 5 + a)
                pe.wait_ge(h_lo, 4 * (a + 1))
                for x in products("prologue", 0):
                    product(H0, 0, *x)
                attention_heads(pe, a, head)
                H, ends = H0 + 15, products("end", 0)
                turn3(H, 1, 3)
                values3(H, 1, 2)
                product(H, 1, *ends[0])
                values3(H, 1, 3)
                product(H, 1, *ends[1])
                product(H, 1, *ends[2])
                bias_rows(a)

            pe.wait_ge(x_sum, 28)
            ln_turn(pe, 7)
            pe.wait_ge(ld_fc1, 16)
            pe.wait_ge(hm_ready, 4)
            for hf in range(2):
                for f in range(FT):
                    n = FT * hf + f
                    if n >= 4:
                        pe.wait_ge(gelu_out, n - 3)
                    for c in range(C):
                        last = nc.tensor.matmul(banks[4 + n % 4][:, :], FC1[:, c, f * P:(f + 1) * P],
                                                HM3[:, c, hf * HALF:(hf + 1) * HALF], start=(c == 0),
                                                stop=(c == C - 1))
                    last.then_inc(fc1_ready, 1)
            pe.wait_ge(ld_fc2, 16)
            for pair in range(4):
                pe.wait_ge(gelu_out, FT * (pair // 2 + 1))
                for k in range(2):
                    m = 2 * pair + k
                    for f in range(FT):
                        last = nc.tensor.matmul(banks[pair][:, k * E:(k + 1) * E], G3[:, f, m * P:(m + 1) * P],
                                                FC2[:, f, :], start=(f == 0), stop=(f == FT - 1))
                last.then_inc(fc2_ready, 1)

        @block.scalar
        def _(act):
            def context():
                act.wait_ge(ld_small, 80)
                for i, (c, hf) in enumerate(TURN_ORDER):
                    act.wait_ge(turned, i + 1)
                    nc.scalar.copy(CTh[:, c, hf * HALF:(hf + 1) * HALF], banks[2 * c + hf][:, :]).then_inc(ct_hi, 1)
                ln_act(act, 0)
                for i, (c, hf) in enumerate(TURN_ORDER):
                    act.wait_ge(turned, 4 + i + 1)
                    nc.scalar.activation(AT[:, 4 * c + 2 * hf:4 * c + 2 * hf + 2, :],
                                         banks[2 * c + hf][:, :].rearrange("p (b t) -> p b t", b=2), ACT.Identity,
                                         scale=VECA[:, G1 + c:G1 + c + 1],
                                         bias=VECA[:, B1 + c:B1 + c + 1]).then_inc(at_ready, 1)
                for q in range(4):
                    act.wait_ge(k1_proj, q + 1)
                    nc.scalar.copy(K1[:, q // 2, (q % 2) * HALF:(q % 2 + 1) * HALF], banks[4 + q][:, :]).then_inc(k1_hi, 1)
                for pair in range(4):
                    act.wait_ge(v1_proj, pair + 1)
                    nc.scalar.copy(V1[:, 2 * pair:2 * pair + 2, :],
                                   banks[pair][:, :].rearrange("p (m d) -> p m d", m=2)).then_inc(v1_ready, 1)

            def shifted_rows(li, n_ln, n_turn, w, b, prev):
                ln_act(act, n_ln)
                nc.scalar.copy(XN[:, :, 0], PREV[:, prev, :]).then_inc(xn_ready, 1)
                for i, (c, hf) in enumerate(TURN_ORDER):
                    act.wait_ge(turned, 4 * n_turn + i + 1)
                    nc.scalar.activation(XN[:, 4 * c + 2 * hf:4 * c + 2 * hf + 2, 1:T + 1],
                                         banks[2 * c + hf][:, :].rearrange("p (b t) -> p b t", b=2), ACT.Identity,
                                         scale=lnw(li, w, c), bias=lnw(li, b, c)).then_inc(xn_ready, 1)

            def take(q, dst, func=ACT.Copy, sem_=None, **kw):
                c, hf = q // 2, q % 2
                return nc.scalar.activation(dst[:, 4 * c + 2 * hf:4 * c + 2 * hf + 2, :],
                                            banks[4 + q][:, :].rearrange("p (b t) -> p b t", b=2), func, **kw)

            def rwkv(li, n_ln, n_turn):
                shifted_rows(li, n_ln, n_turn, LN1W, LN1B, 1)
                for q in range(4):
                    act.wait_ge(m1_ready, 4 * li + q + 1)
                    nc.scalar.activation(M1[:, q // 2, (q % 2) * HALF:(q % 2 + 1) * HALF], banks[4 + q][:, :],
                                         ACT.Tanh).then_inc(m1_tanh, 1)
                for hf in range(2):
                    act.wait_ge(proj_ready, 22 * li + hf + 1)
                    nc.scalar.activation(DT[:, hf * HALF:(hf + 1) * HALF], banks[4 + hf][:, :],
                                         ACT.Tanh).then_inc(proj_out, 1)
                for q in range(4):
                    act.wait_ge(proj_ready, 22 * li + 2 + q + 1)
                    take(q, WT, ACT.Exp, bias=lnw(li, TD, q // 2)).then_inc(proj_out, 1)
                for q in range(4):
                    act.wait_ge(proj_out, 18 * li + 2 + q + 1)
                    v = WT[:, 4 * (q // 2) + 2 * (q % 2):4 * (q // 2) + 2 * (q % 2) + 2, :]
                    nc.scalar.activation(v, v, ACT.Exp, scale=-1.0).then_inc(decay_e, 1)
                for n, dst in ((1, KT), (2, VT), (3, RT)):
                    for q in range(4):
                        act.wait_ge(proj_ready, 22 * li + 2 + 4 * n + q + 1)
                        take(q, dst).then_inc(proj_out, 1)
                for q in range(4):
                    act.wait_ge(proj_ready, 22 * li + 18 + q + 1)
                    take(q, TH, ACT.Tanh, scale=0.5).then_inc(gate_th, 1)
                for k in range(S):
                    if k >= 2:
                        act.wait_ge(read_out, 8 * li + k - 1)
                    else:
                        act.wait_ge(moved["v" if k else "k"], 128 * (li + 1))
                        act.wait_ge(moved["r"], 128 * (li + 1))
                    nc.scalar.copy(SS[k % 2][:, :, 0], S0[:, S * k:S * k + S]).then_inc(state0, 1)
                for q in range(4):
                    act.wait_ge(summed, 9 * (li + 1))
                    nc.scalar.copy(AS[:, 2 * q:2 * q + 2, :],
                                   banks[q][:, :].rearrange("p (b t) -> p b t", b=2)).then_inc(att_out, 1)
                for q in range(4):
                    act.wait_ge(centered, 4 * li + q + 1)
                    take(q, SQ, ACT.Square).then_inc(squared, 1)
                for q in range(4):
                    act.wait_ge(gvar, 4 * li + q + 1)
                    act.wait_ge(eps_set, 1)
                    c, hf = q // 2, q % 2
                    nc.scalar.activation(SD[:, 4 * c + 2 * hf:4 * c + 2 * hf + 2, :],
                                         banks[q][:, :].rearrange("p (b t) -> p b t", b=2), ACT.Sqrt,
                                         bias=EPSC[:, 0:1]).then_inc(groot, 1)
                shifted_rows(li, n_ln + 1, n_turn + 1, LN2W, LN2B, 0)
                for q in range(4):
                    act.wait_ge(fk_pos, 4 * li + q + 1)
                    c, hf = q // 2, q % 2
                    sl = slice(4 * c + 2 * hf, 4 * c + 2 * hf + 2)
                    nc.scalar.activation(KK2[:, sl, :], KK[:, sl, :], ACT.Square).then_inc(fk_sq, 1)
                for pair in range(4):
                    act.wait_ge(fr_ready, 4 * li + pair + 1)
                    nc.scalar.activation(RR[:, 2 * pair:2 * pair + 2, :],
                                         banks[pair][:, :].rearrange("p (b t) -> p b t", b=2), ACT.Tanh,
                                         scale=0.5).then_inc(fr_th, 1)

            def audio():
                for i, (c, hf) in enumerate(TURN_ORDER):
                    act.wait_ge(turned, 16 + i + 1)
                    nc.scalar.copy(XT1[:, c, hf * HALF:(hf + 1) * HALF], banks[2 * c + hf][:, :]).then_inc(xt_ready, 1)
                nc.scalar.activation(GT[:, :], VECA[:, GATE:GATE + 1], ACT.Tanh).then_inc(gate_done, 1)
                for q in range(4):
                    act.wait_ge(q1_proj, q + 1)
                    nc.scalar.copy(Q1h[:, q // 2, (q % 2) * HALF:(q % 2 + 1) * HALF], banks[4 + q][:, :]).then_inc(q1_hi, 1)

                def weights(i, j):
                    g, b = 8 * i + j, j % 4
                    act.wait_ge(sc_max, g + 1)
                    if not (isinstance(g, int) and g < 2):
                        act.wait_ge(p1_turned, g - 1)
                    if b == 0 and not (isinstance(g, int) and g < 8):
                        act.wait_ge(o_inv, 2 * i + j // 4 - 1)
                    for tt in range(2):
                        last = nc.scalar.activation(P1[:, g_par(j), tt, :], SM[:, g_par(j), tt, :], ACT.Exp,
                                                    scale=D1 ** -0.5, bias=NS1[:, g_par(j), tt:tt + 1],
                                                    accum_out=RS1[:, (j // 4) % 2, 2 * b + tt:2 * b + tt + 1])
                    last.then_inc(p1_ready, 1)

                def take_turned(i, j):
                    g = 8 * i + j
                    act.wait_ge(p1_turned, g + 1)
                    if not (isinstance(g, int) and g < 2):
                        act.wait_ge(pv_done, g - 1)
                    nc.scalar.copy(PT1[:, g_par(j), :, :],
                                   banks[2 + g_par(j)][:, :].rearrange("p (s t) -> p s t", s=2)).then_inc(pt_act, 1)

                def body(i):
                    for j in range(8):
                        weights(i, j)
                        if (j - 1) % 4 and not (isinstance(i, int) and 8 * i + j < 1):
                            take_turned(i, j - 1)

                body(0)
                with act.Fori(1, 8) as i:
                    body(i)
                take_turned(8, -1)
                for i, (c, hf) in enumerate(TURN_ORDER):
                    act.wait_ge(turned, 20 + i + 1)
                    nc.scalar.copy(AOT[:, c, hf * HALF:(hf + 1) * HALF], banks[2 * c + hf][:, :]).then_inc(ao_turned, 1)

            context()
            rwkv(0, 1, 2)
            audio()
            rwkv(1, 3, 6)

            def split_high(H, par, wo):
                wait_loaded(act, ld_w3, H, par)
                ws = slice(3, 4) if wo else slice(0, 3)
                nc.scalar.copy(W3h[:, par, ws, :], W3[:, par, ws, :]).then_inc(wo_hi if wo else w3_hi, 1)

            def key_bias(H, par):
                act.wait_ge(hb_ready, H + 1)
                nc.scalar.copy(K3h[:, par, :, T:KEYS],
                               HB[:, par, 2:3].unsqueeze(2).to_broadcast([P, B, 2])).then_inc(key_hi, 1)

            def take_high(H, par, kind, n, dh, bank, before):
                pr = (par + dh) % 2
                if kind == "qk":
                    hf = n // 2
                    act.wait_ge(hb_ready, H + dh + 1)
                    act.wait_ge(qk_full, 4 * (H + dh) + n + 1)
                    if n % 2 == 0:
                        nc.scalar.activation(Q3h[:, pr, hf * HALF:(hf + 1) * HALF], banks[bank][:, :], ACT.Identity,
                                             bias=HB[:, pr, 0:1]).then_inc(qk_hi, 1)
                    else:
                        nc.scalar.activation(K3h[:, pr, 2 * hf:2 * hf + 2, 0:T],
                                             banks[bank][:, :].rearrange("p (b t) -> p b t", b=2), ACT.Identity,
                                             bias=HB[:, pr, 1:2]).then_inc(qk_hi, 1)
                elif kind == "v":
                    act.wait_ge(v_added, 2 * (H + dh) + n + 1)
                    nc.scalar.copy(V3h[:, pr, 4 * n:4 * n + 4, :], V3[:, 4 * n:4 * n + 4, :]).then_inc(v_hi, 1)

            def turned_high(H, par, b):
                act.wait_ge(p3_turned, 4 * H + b + 1)
                nc.scalar.copy(PT3h[:, b % 2, :, :],
                               banks[2 + b % 2][:, :].rearrange("p (s t) -> p s t", s=2)).then_inc(pt3_hi, 1)

            def weights3(H, par, b):
                act.wait_ge(s3_shift, 4 * H + b + 1)
                if not (isinstance(H, int) and 4 * H + b < 2):
                    act.wait_ge(p3_bias, 4 * H + b - 1)
                for tt in range(2):
                    nc.scalar.activation(P3[:, b % 2, tt, 0:T + 1], banks[tt][:, 0:T + 1], ACT.Exp,
                                         scale=D3 ** -0.5, bias=NS3[:, b % 2, tt:tt + 1],
                                         accum_out=RS3[:, b % 2, tt:tt + 1]).then_inc(p3_ready, 1)

            def context_high(H, par, b):
                pr = par if b >= 0 else 1 - par
                act.wait_ge(c3_ready, 4 * H + b + 1)
                nc.scalar.copy(C3h[:, pr, (b % 4) * T:(b % 4 + 1) * T], banks[4 + b % 2][:, 0:T]).then_inc(c3_hi, 1)

            def head(H, par, case):
                for b in range(4):
                    if lagged(case, b, 1):
                        turned_high(H, par, b - 1)
                    weights3(H, par, b)
                    for x in products(case, b):
                        take_high(H, par, *x)
                    if b == 1 and case != "last":
                        key_bias(H + 1, 1 - par)
                    if lagged(case, b, 2):
                        context_high(H, par, b - 2)
                    if b == 0 and not (isinstance(H, int) and H >= 30):
                        act.wait_ge(v_added, 2 * H + 2)
                        split_high(H + 2, par, False)
                    if b == 3 and not (isinstance(H, int) and H >= 31):
                        if not (isinstance(H, int) and H == 0):
                            act.wait_ge(o_full, 4 * H)
                        split_high(H + 1, 1 - par, True)

            for a in range(2):
                if a == 0:
                    split_high(0, 0, False)
                    split_high(1, 1, False)
                    split_high(0, 0, True)
                act.wait_ge(aux_ready, a + 1)
                nc.scalar.copy(WAUX[0:32, :], banks[4][0:32, 0:E]).then_inc(waux_out, 1)
                key_bias(16 * a, 0)
                ln_act(act, 5 + a)
                for i, (c, hf) in enumerate(TURN_ORDER):
                    act.wait_ge(turned, 32 + 4 * a + i + 1)
                    v = slice(hf * HALF, (hf + 1) * HALF)
                    nc.scalar.activation(HF[:, c, v], banks[2 * c + hf][:, :], ACT.Identity,
                                         scale=VECA[:, LN3 + 4 * a + c:LN3 + 4 * a + c + 1],
                                         bias=VECA[:, LN3 + 4 * a + 2 + c:LN3 + 4 * a + 3 + c]).then_inc(h_rows, 1)
                    act.wait_ge(h_rows, 4 * a + i + 1)
                    nc.scalar.copy(Hh[:, c, v], HF[:, c, v]).then_inc(h_hi, 1)
                for x in products("prologue", 0):
                    take_high(16 * a, 0, *x)
                attention_heads(act, a, head)
                turned_high(16 * a + 15, 1, 3)
                context_high(16 * a + 15, 1, 2)
                context_high(16 * a + 15, 1, 3)
                for k in range(2):
                    act.wait_ge(pb_turned, 2 * a + k + 1)
                    nc.scalar.copy(PBT[0:32, k * HALF:(k + 1) * HALF], banks[2 + k][0:32, :]).then_inc(pbt_out, 1)

            ln_act(act, 7)
            for i, (c, hf) in enumerate(TURN_ORDER):
                act.wait_ge(turned, 40 + i + 1)
                nc.scalar.activation(HM3[:, c, hf * HALF:(hf + 1) * HALF], banks[2 * c + hf][:, :], ACT.Identity,
                                     scale=VECA[:, LN3 + 8 + c:LN3 + 9 + c],
                                     bias=VECA[:, LN3 + 10 + c:LN3 + 11 + c]).then_inc(hm_ready, 1)
            for n in range(2 * FT):
                hf, f = n // FT, n % FT
                act.wait_ge(fc1_ready, n + 1)
                nc.scalar.activation(G3[:, f, hf * HALF:(hf + 1) * HALF], banks[4 + n % 4][:, :], ACT.Gelu,
                                     bias=VECA[:, BFC1 + f:BFC1 + f + 1]).then_inc(gelu_out, 1)

        @block.vector
        def _(dve):
            def context():
                nc.vector.memset(EPSC[:, :], EPS).then_inc(eps_set, 1)
                dve.wait_ge(ld_c, 16)
                ln_dve(dve, 0, CRAW)
                for i, (c, hf) in enumerate(TURN_ORDER):
                    dve.wait_ge(ct_hi, i + 1)
                    v = slice(hf * HALF, (hf + 1) * HALF)
                    nc.vector.tensor_tensor(CTl[:, c, v], banks[2 * c + hf][:, :], CTh[:, c, v].bitcast(F32),
                                            ALU.subtract).then_inc(ct_lo, 1)

            def add_rows(sem_, n0, first_bank):
                for pair in range(4):
                    dve.wait_ge(sem_, n0 + pair + 1)
                    nc.vector.tensor_tensor(X[:, 2 * pair:2 * pair + 2, :],
                                            banks[first_bank + pair][:, :].rearrange("p (m d) -> p m d", m=2),
                                            X[:, 2 * pair:2 * pair + 2, :], ALU.add).then_inc(x_sum, 1)

            def rwkv(li, n_ln, xs):
                ln_dve(dve, n_ln, X)
                dve.wait_ge(xn_ready, 10 * li + 5)
                nc.vector.tensor_tensor(SX, XN[:, :, 0:T], XN[:, :, 1:T + 1], ALU.subtract).then_inc(sx_ready, 1)
                dve.wait_ge(sx_ready, 2 * li + 1)
                for c in range(C):
                    v = slice(4 * c, 4 * c + 4)
                    nc.vector.scalar_tensor_tensor(X5[2][:, v, :], SX[:, v, :], lnw(li, MAAX, c),
                                                   XN[:, v, 1:T + 1], ALU.mult, ALU.add).then_inc(xmix_ready, 1)
                for n in range(5):
                    for q in range(4):
                        c, hf = q // 2, q % 2
                        v = slice(4 * c + 2 * hf, 4 * c + 2 * hf + 2)
                        dve.wait_ge(mix_ready, 20 * li + 4 * n + q + 1)
                        if n == 3:
                            dve.wait_ge(proj_ready, 22 * li + 2)
                        if n == 4:
                            dve.wait_ge(proj_ready, 22 * li + 10)
                        nc.vector.scalar_tensor_tensor(X5[n % 3][:, v, :],
                                                       banks[q][:, :].rearrange("p (b t) -> p b t", b=2),
                                                       lnw(li, STACK + 2 * MIX[n], c), SX[:, v, :], ALU.add,
                                                       ALU.mult).then_inc(mix_scaled, 1)
                for q in range(4):
                    c, hf = q // 2, q % 2
                    v = slice(4 * c + 2 * hf, 4 * c + 2 * hf + 2)
                    dve.wait_ge(gate_th, 4 * li + q + 1)
                    nc.vector.scalar_tensor_tensor(G2[:, v, :], TH[:, v, :], 1.0,
                                                   banks[4 + q][:, :].rearrange("p (b t) -> p b t", b=2), ALU.add,
                                                   ALU.mult).then_inc(g_ready, 1)
                for name in "kr":
                    dve.wait_ge(moved[name], 128 * (li + 1))
                for k in range(S):
                    nc.vector.scalar_tensor_tensor(RK[:, k, :], KS[:, k, :], VEC[:, li, UCOL + k:UCOL + k + 1],
                                                   RS[:, k, :], ALU.mult, ALU.mult).then_inc(coef_rk, 1)
                dve.wait_ge(coef_rk, 8 * (li + 1))
                nc.vector.tensor_reduce(CF[:, :], RK.rearrange("p k t -> p t k"), AX_X, ALU.add).then_inc(coef_ready, 1)
                dve.wait_ge(coef_ready, li + 1)
                dve.wait_ge(moved["v"], 128 * (li + 1))
                nc.vector.tensor_tensor(T1, VS, CF[:, :].unsqueeze(1).to_broadcast([P, S, T]),
                                        ALU.mult).then_inc(bonus_ready, 1)
                dve.wait_ge(moved["w"], 128 * (li + 1))
                for k in range(S):
                    if k < S - POOL_K:
                        if k >= 2:
                            dve.wait_ge(scanned, 64 * li + 8 * (k - 1))
                        nc.vector.tensor_tensor(AK[k % 2], VS, KS[:, k, :].unsqueeze(1).to_broadcast([P, S, T]),
                                                ALU.mult).then_inc(outer_dve, 1)
                        dve.wait_ge(outer_dve, (S - POOL_K) * li + k + 1)
                    else:
                        dve.wait_ge(outer_pool, POOL_K * li + k - (S - POOL_K) + 1)
                    dve.wait_ge(state0, 8 * li + k + 1)
                    for d in range(S):
                        nc.vector.tensor_tensor_scan(SS[k % 2][:, d, 1:T + 1], WS[:, k, :], AK[k % 2][:, d, :],
                                                     S0[:, S * k + d:S * k + d + 1], ALU.mult,
                                                     ALU.add).then_inc(scanned, 1)
                    dve.wait_ge(scanned, 64 * li + 8 * (k + 1))
                    if k >= 2:
                        dve.wait_ge(summed, 9 * li + k)
                    nc.vector.tensor_tensor(MK[k % 2], SS[k % 2][:, :, 0:T],
                                            RS[:, k, :].unsqueeze(1).to_broadcast([P, S, T]),
                                            ALU.mult).then_inc(read_out, 1)
                for q in range(4):
                    c, hf = q // 2, q % 2
                    v = slice(4 * c + 2 * hf, 4 * c + 2 * hf + 2)
                    dve.wait_ge(groot, 4 * li + q + 1)
                    nc.vector.reciprocal(SQ[:, v, :], SD[:, v, :]).then_inc(ginv, 1)
                    dve.wait_ge(ginv, 4 * li + q + 1)
                    nc.vector.tensor_tensor(YT[:, v, :], banks[4 + q][:, :].rearrange("p (b t) -> p b t", b=2),
                                            SQ[:, v, :], ALU.mult).then_inc(gnorm, 1)
                    dve.wait_ge(gnorm, 4 * li + q + 1)
                    nc.vector.tensor_scalar(SD[:, v, :], YT[:, v, :], lnw(li, GNW, c), lnw(li, GNB, c),
                                            ALU.mult, ALU.add).then_inc(gaff, 1)
                    dve.wait_ge(gaff, 4 * li + q + 1)
                    nc.vector.scalar_tensor_tensor(YT[:, v, :], SD[:, v, :], 0.5, G2[:, v, :], ALU.mult,
                                                   ALU.mult).then_inc(y_ready, 1)
                add_rows(wo_ready, 4 * li, 0)
                dve.wait_ge(x_sum, xs + 4)
                ln_dve(dve, n_ln + 1, X)
                dve.wait_ge(xn_ready, 10 * li + 10)
                nc.vector.tensor_tensor(SX, XN[:, :, 0:T], XN[:, :, 1:T + 1], ALU.subtract).then_inc(sx_ready, 1)
                dve.wait_ge(sx_ready, 2 * li + 2)
                for dst, col in ((XK, FMK), (XR, FMR)):
                    for c in range(C):
                        v = slice(4 * c, 4 * c + 4)
                        nc.vector.scalar_tensor_tensor(dst[:, v, :], SX[:, v, :], lnw(li, col, c),
                                                       XN[:, v, 1:T + 1], ALU.mult, ALU.add).then_inc(xkr_ready, 1)
                for q in range(4):
                    c, hf = q // 2, q % 2
                    v = slice(4 * c + 2 * hf, 4 * c + 2 * hf + 2)
                    dve.wait_ge(fk_ready, 4 * li + q + 1)
                    nc.vector.tensor_scalar(KK[:, v, :], banks[4 + q][:, :].rearrange("p (b t) -> p b t", b=2), 0.0,
                                            None, ALU.max).then_inc(fk_pos, 1)
                for pair in range(4):
                    v = slice(2 * pair, 2 * pair + 2)
                    dve.wait_ge(fv_ready, 4 * li + pair + 1)
                    dve.wait_ge(fr_th, 4 * li + pair + 1)
                    nc.vector.scalar_tensor_tensor(FT1[:, v, :], RR[:, v, :], 1.0,
                                                   banks[4 + pair][:, :].rearrange("p (b t) -> p b t", b=2), ALU.add,
                                                   ALU.mult).then_inc(fv_mul, 1)
                    dve.wait_ge(fv_mul, 4 * li + pair + 1)
                    nc.vector.scalar_tensor_tensor(X[:, v, :], FT1[:, v, :], 0.5, X[:, v, :], ALU.mult,
                                                   ALU.add).then_inc(x_sum, 1)

            def audio():
                dve.wait_ge(ld_mask, 16)
                nc.vector.tensor_copy(MASKB[:, :], MU8[:, :]).then_inc(mask_f, 1)
                dve.wait_ge(mask_f, 1)
                nc.vector.reciprocal(MASKB[:, :], MASKB[:, :]).then_inc(mask_r, 1)
                dve.wait_ge(mask_r, 1)
                nc.vector.tensor_scalar(MASKB[:, :], MASKB[:, :], -1.0, 1.0, ALU.mult, ALU.add).then_inc(mask_b, 1)
                dve.wait_ge(mask_b, 1)
                for q in range(4):
                    v = slice((q % 2) * HALF, (q % 2 + 1) * HALF)
                    dve.wait_ge(q1_hi, q + 1)
                    nc.vector.tensor_tensor(Q1l[:, q // 2, v], banks[4 + q][:, :], Q1h[:, q // 2, v].bitcast(F32),
                                            ALU.subtract).then_inc(q1_lo, 1)

                def keys_low(h, par, c):
                    dve.wait_ge(km_hi, h + 1)
                    nc.vector.scalar_tensor_tensor(KMl[:, par, :], K1[:, c, :],
                                                   VECA[:, bass.ds(HMASK + h - 8 * c, 1)],
                                                   KMh[:, par, :].bitcast(F32), ALU.mult,
                                                   ALU.subtract).then_inc(km_lo, 1)

                def head_out(i, jh):
                    h, par = 2 * i + jh, jh % 2
                    dve.wait_ge(pv_done, 4 * h + 4)
                    nc.vector.reciprocal(RI1[:, par, :], RS1[:, par, :]).then_inc(o_inv, 1)
                    dve.wait_ge(o_inv, h + 1)
                    nc.vector.tensor_tensor(AO[:, :, bass.ds(D1 * h, D1)],
                                            banks[4 + par][:, 0:TILES * D1].rearrange("p (m d) -> p m d", m=TILES),
                                            RI1[:, par, :].unsqueeze(2).to_broadcast([P, TILES, D1]),
                                            ALU.mult).then_inc(o_out, 1)

                def body(i, c, c_next, last=False):
                    for j in range(8):
                        g, b = 8 * i + j, j % 4
                        dve.wait_ge(sc_ready, g + 1)
                        if not (isinstance(g, int) and g < 2):
                            dve.wait_ge(p1_ready, g - 1)
                        nc.vector.memset(CARRY[:, :], 0.0)
                        for tt in range(2):
                            nc.vector.tensor_tensor_reduce(SM[:, g_par(j), tt, :],
                                                           banks[g_par(j)][:, tt * T:(tt + 1) * T],
                                                           MASKB[:, b * T:(b + 1) * T], 1.0, MOST_NEGATIVE,
                                                           ALU.add, ALU.max,
                                                           NM1[:, g_par(j), tt:tt + 1]).then_inc(sc_masked, 1)
                        dve.wait_ge(sc_masked, 2 * g + 2)
                        nc.vector.tensor_scalar(NS1[:, g_par(j), :], NM1[:, g_par(j), :], -D1 ** -0.5, None,
                                                ALU.mult).then_inc(sc_max, 1)
                        if b == 1:
                            dve.wait_ge(p1_turned, g)
                            if not (isinstance(g, int) and g < 3):
                                dve.wait_ge(pv_done, g - 2)
                            nc.vector.tensor_copy(PT1[:, g_par(j - 1), :, :],
                                                  banks[2 + g_par(j - 1)][:, :].rearrange("p (s t) -> p s t", s=2)
                                                  ).then_inc(pt_dve, 1)
                            if not (last and j == 5):
                                keys_low(2 * i + j // 4 + 1, (j // 4 + 1) % 2, c if j == 1 else c_next)
                        if b == 2 and not (isinstance(i, int) and 2 * i + j // 4 < 1):
                            head_out(i, j // 4 - 1)

                keys_low(0, 0, 0)
                body(0, 0, 0)
                for c in range(2):
                    with dve.Fori(1 if c == 0 else 4, 4 * c + 3) as i:
                        body(i, c, c)
                    body(4 * c + 3, c, 1, c == 1)
                head_out(8, -1)
                dve.wait_ge(gate_done, 1)
                for pair in range(4):
                    dve.wait_ge(out1_ready, pair + 1)
                    nc.vector.scalar_tensor_tensor(X[:, 2 * pair:2 * pair + 2, :],
                                                   banks[4 + pair][:, :].rearrange("p (m d) -> p m d", m=2),
                                                   GT[:, 0:1], X[:, 2 * pair:2 * pair + 2, :], ALU.mult,
                                                   ALU.add).then_inc(x_sum, 1)
                dve.wait_ge(x_sum, 12)

            context()
            dve.wait_ge(ld_x, 16)
            dve.wait_ge(ld_small, 80)
            dve.wait_ge(turned, 8)
            rwkv(0, 1, 0)
            audio()
            rwkv(1, 3, 12)

            def take_low(H, par, kind, n, dh, bank, before):
                pr = (par + dh) % 2
                if kind == "qk":
                    hf = n // 2
                    dve.wait_ge(qk_hi, 4 * (H + dh) + n + 1)
                    if n % 2 == 0:
                        v = slice(hf * HALF, (hf + 1) * HALF)
                        nc.vector.scalar_tensor_tensor(Q3l[:, pr, v], banks[bank][:, :],
                                                       HB[:, pr, 0:1],
                                                       Q3h[:, pr, v].bitcast(F32), ALU.add,
                                                       ALU.subtract).then_inc(qk_lo, 1)
                    else:
                        v = slice(2 * hf, 2 * hf + 2)
                        nc.vector.scalar_tensor_tensor(K3l[:, pr, v, 0:T],
                                                       banks[bank][:, :].rearrange("p (b t) -> p b t", b=2),
                                                       HB[:, pr, 1:2],
                                                       K3h[:, pr, v, 0:T].bitcast(F32), ALU.add,
                                                       ALU.subtract).then_inc(qk_lo, 1)
                elif kind == "v":
                    dve.wait_ge(v_full, 2 * (H + dh) + n + 1)
                    wait_loaded(dve, ld_bv, H + dh, pr)
                    if not (isinstance(H, int) and H + dh < 1):
                        dve.wait_ge(v_lo, 2 * (H + dh) + n - 1)
                    nc.vector.tensor_tensor(V3[:, 4 * n:4 * n + 4, :],
                                            banks[bank][:, :].rearrange("p (m d) -> p m d", m=4),
                                            BV[:, pr, :].unsqueeze(1).to_broadcast([P, 4, D3]),
                                            ALU.add).then_inc(v_added, 1)
                else:
                    v = slice(2 * (n % 4), 2 * (n % 4) + 2)
                    dve.wait_ge(o_full, 4 * H + n + 1)
                    nc.vector.tensor_tensor(X[:, v, :], banks[bank][:, :].rearrange("p (m d) -> p m d", m=2),
                                            X[:, v, :], ALU.add).then_inc(o_added, 1)

            def row_max(H, par, b):
                for tt in range(2):
                    dve.wait_ge(s3_ready, 8 * H + 2 * b + tt + 1)
                    nc.vector.tensor_reduce(NM3[:, b % 2, tt:tt + 1], banks[tt][:, 0:T + 1], AX_X,
                                            ALU.max).then_inc(s3_max, 1)
                dve.wait_ge(s3_max, 8 * H + 2 * b + 2)
                nc.vector.tensor_scalar(NS3[:, b % 2, :], NM3[:, b % 2, :], -D3 ** -0.5, None,
                                        ALU.mult).then_inc(s3_shift, 1)

            def turned_low(H, par, b):
                dve.wait_ge(pt3_hi, 4 * H + b + 1)
                nc.vector.tensor_tensor(PT3l[:, b % 2, :, :],
                                        banks[2 + b % 2][:, :].rearrange("p (s t) -> p s t", s=2),
                                        PT3h[:, b % 2, :, :].bitcast(F32), ALU.subtract).then_inc(pt3_lo, 1)

            def invert(H, par, b):
                dve.wait_ge(p3_ready, 8 * H + 2 * b + 2)
                nc.vector.reciprocal(RI3[:, b % 2, :], RS3[:, b % 2, :]).then_inc(p3_inv, 1)

            def keep_bias(H, par, b, a):
                dve.wait_ge(p3_scaled, 8 * H + 2 * b + 2)
                nc.vector.tensor_scalar(PB[:, 2 * b:2 * b + 2, bass.ds(H - 16 * a, 1)], P3[:, b % 2, :, T:T + 1], 1.0,
                                        None, ALU.mult).then_inc(p3_bias, 1)

            def context_low(H, par, b):
                pr = par if b >= 0 else 1 - par
                v = slice((b % 4) * T, (b % 4 + 1) * T)
                dve.wait_ge(c3_hi, 4 * H + b + 1)
                nc.vector.tensor_tensor(C3l[:, pr, v], banks[4 + b % 2][:, 0:T], C3h[:, pr, v].bitcast(F32),
                                        ALU.subtract).then_inc(c3_lo, 1)

            def head_biases(H, par):
                nc.vector.tensor_scalar(HB[:, par, :], VECA[:, BQ:HMASK].rearrange("p (w h) -> p w h", w=3)
                                        [:, :, bass.ds(H, 1)], 1.0, None, ALU.mult).then_inc(hb_ready, 1)

            def key_bias_low(H, par):
                dve.wait_ge(key_hi, H + 1)
                nc.vector.tensor_tensor(K3l[:, par, :, T:KEYS],
                                        HB[:, par, 2:3].unsqueeze(2).to_broadcast([P, B, 2]),
                                        K3h[:, par, :, T:KEYS].bitcast(F32), ALU.subtract).then_inc(key_lo, 1)

            for a in range(2):
                def head(H, par, case):
                    for b in range(4):
                        row_max(H, par, b)
                        if lagged(case, b, 1):
                            turned_low(H, par, b - 1)
                        todo = [x for x in products(case, b) if x[0] != "o"]
                        if todo:
                            take_low(H, par, *todo[0])
                        invert(H, par, b)
                        for x in todo[1:]:
                            take_low(H, par, *x)
                        if b == 1 and case != "last":
                            dve.wait_ge(hb_ready, H + 2)
                            key_bias_low(H + 1, 1 - par)
                        keep_bias(H, par, b, a)
                        if b == 0 and not (isinstance(H, int) and H >= 30):
                            dve.wait_ge(qk_lo, 4 * H + 4)
                            dve.wait_ge(key_hi, H + 1)
                            dve.wait_ge(key_lo, H + 1)
                            head_biases(H + 2, par)
                        if lagged(case, b, 2):
                            context_low(H, par, b - 2)
                        for x in products(case, b):
                            if x[0] == "o":
                                take_low(H, par, *x)

                dve.wait_ge(x_sum, 20 + 4 * a)
                if a == 0:
                    head_biases(0, 0)
                    head_biases(1, 1)
                ln_dve(dve, 5 + a, X)
                key_bias_low(16 * a, 0)
                nc.vector.memset(PB[:, :, :], 0.0).then_inc(pb_clear, 1)
                dve.wait_ge(pb_clear, a + 1)
                nc.vector.memset(PB[:, :, 16:17], 1.0).then_inc(pb_one, 1)
                for i, (c, hf) in enumerate(TURN_ORDER):
                    dve.wait_ge(h_hi, 4 * a + i + 1)
                    v = slice(hf * HALF, (hf + 1) * HALF)
                    nc.vector.tensor_tensor(Hl[:, c, v], HF[:, c, v], Hh[:, c, v].bitcast(F32),
                                            ALU.subtract).then_inc(h_lo, 1)
                for x in products("prologue", 0):
                    take_low(16 * a, 0, *x)
                dve.wait_ge(pb_one, a + 1)
                attention_heads(dve, a, head)
                H, ends = 16 * a + 15, products("end", 0)
                turned_low(H, 1, 3)
                context_low(H, 1, 2)
                take_low(H, 1, *ends[0])
                context_low(H, 1, 3)
                take_low(H, 1, *ends[1])
                take_low(H, 1, *ends[2])
                dve.wait_ge(o_added, 64 * (a + 1))
                for pair in range(4):
                    dve.wait_ge(aux_rows, 4 * a + pair + 1)
                    nc.vector.tensor_tensor(X[:, 2 * pair:2 * pair + 2, :],
                                            banks[(0, 1, 4, 5)[pair]][:, :].rearrange("p (m d) -> p m d", m=2),
                                            X[:, 2 * pair:2 * pair + 2, :], ALU.add).then_inc(x_sum, 1)

            dve.wait_ge(x_sum, 28)
            ln_dve(dve, 7, X)
            dve.wait_ge(ln_rows, 64)
            dve.wait_ge(ld_bfc2, 16)
            nc.vector.tensor_tensor(X[:, :, :], X[:, :, :], BFC2[:, :].unsqueeze(1).to_broadcast([P, TILES, E]),
                                    ALU.add).then_inc(x_sum, 1)
            dve.wait_ge(x_sum, 29)
            add_rows(fc2_ready, 0, 0)

        @block.gpsimd
        def _(pool):
            def rwkv(li):
                for n in range(5):
                    for q in range(4):
                        c, hf = q // 2, q % 2
                        v = slice(4 * c + 2 * hf, 4 * c + 2 * hf + 2)
                        pool.wait_ge(mix_scaled, 20 * li + 4 * n + q + 1)
                        nc.gpsimd.tensor_tensor(X5[n % 3][:, v, :], X5[n % 3][:, v, :], XN[:, v, 1:T + 1],
                                                ALU.add).then_inc(x5_ready, 1)
                for name in "kv":
                    pool.wait_ge(moved[name], 128 * (li + 1))
                for k in range(S - POOL_K, S):
                    pool.wait_ge(scanned, 64 * li + 8 * (k - 1))
                    nc.gpsimd.tensor_tensor(AK[k % 2], VS, KS[:, k, :].unsqueeze(1).to_broadcast([P, S, T]),
                                            ALU.mult).then_inc(outer_pool, 1)

            def audio():
                def keys_high(h, par, c):
                    if not (isinstance(h, int) and h < 2):
                        pool.wait_ge(sc_ready, 4 * h - 4)
                    nc.gpsimd.tensor_tensor(KMh[:, par, :], K1[:, c, :],
                                            VECA[:, bass.ds(HMASK + h - 8 * c, 1)].to_broadcast([P, NTOK]),
                                            ALU.mult).then_inc(km_hi, 1)

                pool.wait_ge(x_sum, 8)
                keys_high(0, 0, 0)
                keys_high(1, 1, 0)
                for c in range(2):
                    with pool.Fori(1 if c == 0 else 4, 4 * c + 4) as i:
                        keys_high(2 * i, 0, c)
                        keys_high(2 * i + 1, 1, c)

            rwkv(0)
            audio()
            rwkv(1)

            def split_low(H, par, wo):
                hi, lo = (wo_hi, wo_lo) if wo else (w3_hi, w3_lo)
                ws = slice(3, 4) if wo else slice(0, 3)
                pool.wait_ge(hi, H + 1)
                nc.gpsimd.tensor_tensor(W3l[:, par, ws, :], W3[:, par, ws, :], W3h[:, par, ws, :].bitcast(F32),
                                        ALU.subtract).then_inc(lo, 1)

            def values_low(H, par, n):
                pool.wait_ge(v_hi, 2 * H + n + 1)
                nc.gpsimd.tensor_tensor(V3l[:, par, 4 * n:4 * n + 4, :], V3[:, 4 * n:4 * n + 4, :],
                                        V3h[:, par, 4 * n:4 * n + 4, :].bitcast(F32), ALU.subtract).then_inc(v_lo, 1)

            def scale(H, par, b):
                pool.wait_ge(p3_inv, 4 * H + b + 1)
                for tt in range(2):
                    nc.gpsimd.tensor_tensor(P3[:, b % 2, tt, 0:T + 1], P3[:, b % 2, tt, 0:T + 1],
                                            RI3[:, b % 2, tt:tt + 1].to_broadcast([P, T + 1]),
                                            ALU.mult).then_inc(p3_scaled, 1)

            def head(H, par, case):
                for b in range(4):
                    scale(H, par, b)
                    if b % 2 and case != "last":
                        values_low(H + 1, 1 - par, b // 2)
                    if b == 0 and not (isinstance(H, int) and H >= 30):
                        split_low(H + 2, par, False)
                    if b == 3 and not (isinstance(H, int) and H >= 31):
                        split_low(H + 1, 1 - par, True)

            split_low(0, 0, False)
            split_low(1, 1, False)
            split_low(0, 0, True)
            for a in range(2):
                values_low(16 * a, 0, 0)
                values_low(16 * a, 0, 1)
                attention_heads(pool, a, head)


def kernel(**inputs):
    import numpy as np
    import concourse.bacc as _bacc
    from concourse.bass_utils import run_bass_kernel_spmd as _run

    a = {k: np.asarray(v) for k, v in inputs.items()}

    def cols(v):
        return v.reshape(-1, P).T

    def wt(w):
        return w.reshape(C, P, -1).transpose(1, 0, 2).reshape(P, -1)

    def padded(w, shape):
        z = np.zeros(shape, np.float32)
        z[:w.shape[0], :w.shape[1]] = w
        return z

    def bias_columns(v):
        z = np.zeros((P, H3, 32), np.float32)
        for h in range(H3):
            z[:, h, h] = v[h]
        return z

    def rwkv_weights(p):
        w2 = np.zeros((P, 5, E), np.float32)
        for j in range(5):
            w2[32 * (j % 4):32 * (j % 4) + 32, j] = a[p + "maa_w2"][j]
        parts = [wt(padded(a[p + "maa_w1"], (E, 256))), w2.reshape(P, -1), wt(padded(a[p + "decay_w1"], (E, P))),
                 padded(a[p + "decay_w2"], (P, E))]
        parts += [wt(a[p + n].T) for n in ("Wk", "Wv", "Wr", "Wg", "Wo", "ffn_Wk", "ffn_Wr", "ffn_Wv")]
        return np.concatenate(parts, 1)

    def rwkv_vectors(p):
        parts = [cols(a[p + n]) for n in ("ln1_w", "ln1_b", "ln2_w", "ln2_b", "maa_x")]
        parts += [cols(a[p + "maa_stack"].reshape(-1))]
        parts += [cols(a[p + n]) for n in ("time_decay", "gn_w", "gn_b", "ffn_maa_k", "ffn_maa_r")]
        return np.concatenate(parts + [np.tile(a[p + "faaaa"], (B, 1))], 1)

    q = "L3_xattn_"
    head_of = np.arange(P)[:, None] // D1 == np.arange(HPC)[None, :]
    veca = [cols(a["L1_xattn_ln_gamma"]), cols(a["L1_xattn_ln_beta"]), np.tile(a["L1_xattn_gate"], (P, 1))]
    veca += [cols(a[q + n]) for n in ("ln1_scale", "ln1_offset", "ln2_scale", "ln2_offset", "ln_mlp_scale",
                                      "ln_mlp_offset", "b_fc1", "bq1", "bq2", "bk1", "bk2")]
    veca += [a[q + n].reshape(H3, D3).T for n in ("bias_k1", "bias_k2")]
    veca += [head_of.astype(np.float32)]
    same = (np.arange(P)[:, None] // S == np.arange(P)[None, :] // S).astype(np.float32) / S
    const = np.stack([np.eye(P, dtype=np.float32), np.eye(P, dtype=np.float32) - same, same], 1)
    ctx = a["ctx_2048"]
    prev = ctx[:, 0:2, :].reshape(B, 2, C, P).transpose(3, 1, 2, 0).reshape(P, 2, C * B)
    w3 = [[np.concatenate([a[q + n + s].reshape(C, P, H3, D3).transpose(2, 1, 0, 3) for n in ("wq", "wk", "wv")]
                          + [a[q + "wo" + s].reshape(H3, P, C, P)], 2).reshape(H3, P, 4, E)] for s in "12"]
    arrays = {
        "x": a["x"], "ctx": ctx, "mask": a["mask_BxS2_bf1"].reshape(1, B * T).view(np.uint8),
        "prev": prev, "s0": ctx[:, 2:10, :].reshape(P, S * S), "const": const,
        "wrk": np.stack([rwkv_weights("L0_xattn_"), rwkv_weights("L2_xattn_")]),
        "vec": np.stack([rwkv_vectors("L0_xattn_"), rwkv_vectors("L2_xattn_")], 1),
        "veca": np.concatenate(veca, 1),
        "w1l": np.stack([wt(a["L1_xattn_" + n].T) for n in ("Wq", "Wk", "Wv", "Wo")], 1).reshape(P, 4, C, E),
        "w3": np.concatenate([w[0] for w in w3]),
        "rows": np.stack([a[q + "bo1"], a[q + "bo2"], a[q + "b_fc2"]]),
        "bv": np.stack([a[q + "bv1"], a[q + "bv2"]]).reshape(2 * H3, D3),
        "biasv": np.stack([bias_columns(a[q + "bias_v" + s].reshape(H3, D3)) for s in "12"]),
        "fc1": a[q + "w_fc1"].reshape(C, P, F3).transpose(1, 0, 2),
        "fc2": a[q + "w_fc2"].reshape(FT, P, E).transpose(1, 0, 2),
    }
    nc = _bacc.Bacc("TRN2", target_bir_lowering=False, num_devices=1)
    args = []
    for name in arrays:
        arrays[name] = np.ascontiguousarray(arrays[name])
        args.append(nc.dram_tensor(f"in_{name}", arrays[name].shape, mybir.dt.from_np(arrays[name].dtype),
                                   kind="ExternalInput").ap())
    args.append(nc.dram_tensor("out_x", (B, T, E), F32, kind="ExternalOutput").ap())
    build_program(nc, *args)
    r = _run(nc, [{f"in_{k}": v for k, v in arrays.items()}], core_ids=[0])
    return r.results[0]["out_x"]
```

```python
from contextlib import ExitStack

import concourse.bass as bass
from concourse import mybir

F32 = mybir.dt.float32
F32R = mybir.dt.float32r
U8 = mybir.dt.uint8
ALU = mybir.AluOpType
ACT = mybir.ActivationFunctionType
AX_X = mybir.AxisListType.X

P = 128
B, T, E = 4, 256, 256
NTOK = B * T
C = E // P
TILES = NTOK // P
HALF = 512
S = 8
EPS = 1e-5
H1, D1 = 16, 16
HPC = P // D1
H3, D3 = 16, 128
KEYS = T + 2
F3 = 1024
FT = F3 // P

W1, W2, DW1, DW2 = 0, 2 * 256, 2 * 256 + 5 * 256, 2 * 256 + 5 * 256 + 2 * 128
WK, WV, WR, WG, WO, FK, FR, FV = (DW2 + 256 + 512 * i for i in range(8))
NW = FV + 512
LN1W, LN1B, LN2W, LN2B, MAAX, STACK, TD, GNW, GNB, FMK, FMR = 0, 2, 4, 6, 8, 10, 20, 22, 24, 26, 28
UCOL = 30
NV = UCOL + S
G1, B1, GATE, LN3, BFC1 = 0, 2, 4, 5, 17
BQ, BK, BIASK = (BFC1 + FT + 32 * i for i in range(3))
HMASK = BIASK + 32
NVA = HMASK + HPC
MOST_NEGATIVE = -3.0e38
MIX = [1, 0, 2, 3, 4]
POOL_K = 3


def build_program(nc, x_in, ctx_in, mask_in, prev_in, s0_in, const_in, wrk_in, vec_in, veca_in,
                  w1l_in, w3_in, wv_in, rows_in, bv_in, biasv_in, fc1_in, fc2_in, out):
    with ExitStack() as stack:
        def sem(name):
            return stack.enter_context(nc.semaphore(name))

        def sb(name, shape, dt=F32, where=stack):
            return where.enter_context(nc.sbuf_tensor(name, shape, dt))

        X = sb("X", [P, TILES, E])
        XNT = sb("XNT", [P, TILES, E])
        STAT = sb("STAT", [P, TILES, 6])
        MV = sb("MV", [P, TILES, 2])
        VE = sb("VE", [P, 3, TILES])
        CONST = sb("CONST", [P, 3, P])
        IDENT, CENTER, MEAN8 = CONST[:, 0, :], CONST[:, 1, :], CONST[:, 2, :]
        EPSC = sb("EPSC", [P, 1])
        VEC = sb("VEC", [P, 2, NV])
        VECA = sb("VECA", [P, NVA])
        PREV = sb("PREV", [P, 2, TILES])
        S0 = sb("S0", [P, S * S])
        CTh = sb("CTh", [P, C, NTOK], F32R)
        CTl = sb("CTl", [P, C, NTOK], F32R)
        KV1 = sb("KV1", [P, 2, 2048])
        K1 = KV1[:, 0, :].rearrange("p (c t) -> p c t", c=C)
        V1 = KV1[:, 1, :].rearrange("p (m d) -> p m d", m=TILES)
        W1L = sb("W1L", [P, 4, C, E])
        BFC2 = sb("BFC2", [P, E])
        CF = sb("CF", [P, T])

        with ExitStack() as scope:
            AR = sb("AR", [P, 14 * 2048 + 2056], F32, scope)
            WRK = sb("WRK", [P, NW], F32, scope)
        with ExitStack() as scope:
            Q1h = sb("Q1h", [P, C, NTOK], F32R, scope)
            Q1l = sb("Q1l", [P, C, NTOK], F32R, scope)
            KMh = sb("KMh", [P, 2, NTOK], F32R, scope)
            KMl = sb("KMl", [P, 2, NTOK], F32R, scope)
            MU8 = sb("MU8", [P, B * T], U8, scope)
            MASKB = sb("MASKB", [P, B * T], F32, scope)
            P1R = sb("P1R", [P, 4 * 2 * T], F32, scope)
            PT1 = sb("PT1", [P, 2, 2, T], F32, scope)
            VM = sb("VM", [P, 2, TILES, P], F32, scope)
            ZV = sb("ZV", [P, TILES, D1], F32, scope)
            NM1 = sb("NM1", [P, 2, 2], F32, scope)
            NS1 = sb("NS1", [P, 2, 2], F32, scope)
            RS1 = sb("RS1", [P, 2, 2], F32, scope)
            RI1 = sb("RI1", [P, 2, 2], F32, scope)
            GT = sb("GT", [P, 1], F32, scope)
            CARRY = sb("CARRY", [P, 1], F32, scope)
        P1 = P1R[:, :].rearrange("p (n k t) -> p n k t", n=4, k=2)
        XT1 = P1R[:, :].rearrange("p (c t) -> p c t", c=C)
        AOT = XT1
        with ExitStack() as scope:
            HF = sb("HF", [P, C, NTOK], F32, scope)
            Hh = sb("Hh", [P, C, NTOK], F32R, scope)
            Hl = sb("Hl", [P, C, NTOK], F32R, scope)
            WQK = sb("WQK", [P, 2, E], F32, scope)
            WQKh = sb("WQKh", [P, 2, 2, E], F32R, scope)
            WQKl = sb("WQKl", [P, 2, 2, E], F32R, scope)
            WO3 = sb("WO3", [P, E], F32, scope)
            WOh = sb("WOh", [P, 2, E], F32R, scope)
            WOl = sb("WOl", [P, 2, E], F32R, scope)
            WV3 = sb("WV3", [P, C, 2 * D3], F32, scope)
            WVh = sb("WVh", [P, C, 2 * D3], F32R, scope)
            WVl = sb("WVl", [P, C, 2 * D3], F32R, scope)
            Q3h = sb("Q3h", [P, 2, NTOK], F32R, scope)
            Q3l = sb("Q3l", [P, 2, NTOK], F32R, scope)
            K3h = sb("K3h", [P, 2, B, KEYS], F32R, scope)
            K3l = sb("K3l", [P, 2, B, KEYS], F32R, scope)
            V3 = sb("V3", [P, 2, 2, 2 * D3], F32, scope)
            V3h = sb("V3h", [P, TILES, 2 * D3], F32R, scope)
            V3l = sb("V3l", [P, TILES, 2 * D3], F32R, scope)
            HB = sb("HB", [P, 2, 3], F32, scope)
            BV = sb("BV", [P, 2 * D3], F32, scope)
            P3 = sb("P3", [P, 2, 2, KEYS], F32, scope)
            PT3h = sb("PT3h", [P, 2, 2, T], F32R, scope)
            PT3l = sb("PT3l", [P, 2, 2, T], F32R, scope)
            C3h = sb("C3h", [P, 2, NTOK], F32R, scope)
            C3l = sb("C3l", [P, 2, NTOK], F32R, scope)
            NM3 = sb("NM3", [P, 2, 2], F32, scope)
            NS3 = sb("NS3", [P, 2, 2], F32, scope)
            RS3 = sb("RS3", [P, 2, 2], F32, scope)
            RI3 = sb("RI3", [P, 2, 2], F32, scope)
            PB = sb("PB", [P, TILES, 32], F32, scope)
            PBT = sb("PBT", [32, NTOK], F32, scope)
            BVD = sb("BVD", [P, H3, 32], F32, scope)
            WAUX = sb("WAUX", [32, E], F32, scope)
        WOALL = KV1[:, :, :].rearrange("p k (h e) -> p (k h) e", e=E)
        with ExitStack() as scope:
            HM3 = sb("HM3", [P, C, NTOK], F32, scope)
            G3 = sb("G3", [P, FT, NTOK], F32, scope)
        FC1 = W1L[:, :, :, :].rearrange("p w c e -> p (w c e)").rearrange("p (c f) -> p c f", c=C)
        FC2 = KV1[:, 0, :].rearrange("p (f e) -> p f e", f=FT)

        def slot(i, n=1):
            return AR[:, i * 2048:(i + n) * 2048]

        def fm(i):
            return slot(i).rearrange("p (a t) -> p a t", a=8)

        XN = AR[:, 14 * 2048:14 * 2048 + 2056].rearrange("p (a t) -> p a t", a=8)
        SX = fm(1)
        X5 = [fm(2), fm(3), fm(4)]
        KT, VT, RT, WT = (fm(i) for i in (5, 6, 7, 8))
        KS, VS, RS, WS = (fm(i) for i in (9, 10, 11, 12))
        M1 = slot(11).rearrange("p (m t) -> p m t", m=2)
        DT = slot(13)[:, 0:NTOK]
        TH = fm(0)
        G2 = fm(13)
        RK, T1 = fm(4), fm(1)
        AK = [fm(2), fm(3)]
        MK = [fm(8), fm(0)]
        SS = [AR[:, 5 * 2048 + 2056 * i:5 * 2048 + 2056 * (i + 1)].rearrange("p (d t) -> p d t", d=S)
              for i in (0, 1)]
        AS, ATT, SQ, SD, YT = (fm(i) for i in (4, 9, 10, 11, 12))
        XK, XR, KK, KK2, RR, FT1 = (fm(i) for i in (2, 3, 4, 5, 6, 7))
        CRAW = slot(9).rearrange("p (m d) -> p m d", m=TILES)
        AT = fm(12)

        banks = [stack.enter_context(nc.psum_tensor(f"bank{i}", [P, 512], F32)) for i in range(8)]

        ld_x, ld_c, ld_small, ld_wrk, ld_w1l, ld_mask = (sem(n) for n in (
            "ld_x", "ld_c", "ld_small", "ld_wrk", "ld_w1l", "ld_mask"))
        eps_set, gate_done = sem("eps_set"), sem("gate_done")
        ln_stats, ln_mv, ln_var, ln_root, ln_inv, ln_rows = (sem(n) for n in (
            "ln_stats", "ln_mv", "ln_var", "ln_root", "ln_inv", "ln_rows"))
        turned = sem("turned")
        x_sum = sem("x_sum")
        ct_hi, ct_lo, at_ready, k1_proj, k1_hi, k1_lo, v1_proj, v1_ready, mask_f, mask_r, mask_b = (
            sem(n) for n in ("ct_hi", "ct_lo", "at_ready", "k1_proj", "k1_hi", "k1_lo", "v1_proj",
                             "v1_ready", "mask_f", "mask_r", "mask_b"))
        xn_ready, sx_ready, xmix_ready, m1_ready, m1_tanh, mix_ready, mix_scaled, x5_ready = (
            sem(n) for n in ("xn_ready", "sx_ready", "xmix_ready", "m1_ready", "m1_tanh", "mix_ready",
                             "mix_scaled", "x5_ready"))
        proj_ready, proj_out, decay_e, gate_th, g_ready = (
            sem(n) for n in ("proj_ready", "proj_out", "decay_e", "gate_th", "g_ready"))
        moved = {n: sem(f"moved_{n}") for n in "wkvra"}
        coef_rk, coef_ready, bonus_ready, state0, outer_dve, outer_pool, scanned, read_out, summed = (
            sem(n) for n in ("coef_rk", "coef_ready", "bonus_ready", "state0", "outer_dve", "outer_pool",
                             "scanned", "read_out", "summed"))
        att_out, centered, squared, gvar, groot, ginv, gnorm, gaff, y_ready, wo_ready = (
            sem(n) for n in ("att_out", "centered", "squared", "gvar", "groot", "ginv", "gnorm", "gaff",
                             "y_ready", "wo_ready"))
        xkr_ready, fk_ready, fk_pos, fk_sq, fr_ready, fr_th, fv_ready, fv_mul = (
            sem(n) for n in ("xkr_ready", "fk_ready", "fk_pos", "fk_sq", "fr_ready", "fr_th", "fv_ready",
                             "fv_mul"))
        xt_ready, q1_proj, q1_hi, q1_lo, km_hi, km_lo, vm_clear, vm_ready = (
            sem(n) for n in ("xt_ready", "q1_proj", "q1_hi", "q1_lo", "km_hi", "km_lo", "vm_clear", "vm_ready"))
        sc_ready, sc_masked, sc_max, p1_ready, p1_inv, p1_scaled, p1_turned, pt_out, pv_done = (
            sem(n) for n in ("sc_ready", "sc_masked", "sc_max", "p1_ready", "p1_inv", "p1_scaled", "p1_turned",
                             "pt_out", "pv_done"))
        ao_turned, out1_ready = sem("ao_turned"), sem("out1_ready")
        ld_wqk, ld_wo3, ld_wv, ld_bv = (sem(n) for n in ("ld_wqk", "ld_wo3", "ld_wv", "ld_bv"))
        ld_wo, ld_aux, ld_bo, ld_fc1, ld_fc2, ld_bfc2 = (
            sem(n) for n in ("ld_wo", "ld_aux", "ld_bo", "ld_fc1", "ld_fc2", "ld_bfc2"))
        hb_ready = sem("hb_ready")
        h_rows, h_hi, h_lo, wqk_hi, wqk_lo, wo_hi, wo_lo, wv_hi, wv_lo, key_hi, key_lo = (
            sem(n) for n in ("h_rows", "h_hi", "h_lo", "wqk_hi", "wqk_lo", "wo_hi", "wo_lo", "wv_hi", "wv_lo",
                             "key_hi", "key_lo"))
        qk_full, qk_hi, qk_lo, v_full, v_added, v_hi, v_lo, o_full, o_added = (
            sem(n) for n in ("qk_full", "qk_hi", "qk_lo", "v_full", "v_added", "v_hi", "v_lo", "o_full",
                             "o_added"))
        s3_ready, s3_max, s3_shift, p3_ready, p3_inv, p3_scaled, p3_bias, p3_turned, pt3_hi, pt3_lo = (
            sem(n) for n in ("s3_ready", "s3_max", "s3_shift", "p3_ready", "p3_inv", "p3_scaled", "p3_bias",
                             "p3_turned", "pt3_hi", "pt3_lo"))
        c3_ready, c3_hi, c3_lo = sem("c3_ready"), sem("c3_hi"), sem("c3_lo")
        pb_clear, pb_one, aux_ready, waux_out, pb_turned, pbt_out, aux_rows = (
            sem(n) for n in ("pb_clear", "pb_one", "aux_ready", "waux_out", "pb_turned", "pbt_out", "aux_rows"))
        hm_ready, fc1_ready, gelu_out, fc2_ready = (
            sem(n) for n in ("hm_ready", "fc1_ready", "gelu_out", "fc2_ready"))
        stored = sem("stored")

        block = stack.enter_context(nc.Block())

        def lnw(li, col, c):
            return VEC[:, li, col + c:col + c + 1]

        def ln_dve(dve, n, src):
            for m in range(TILES):
                nc.vector.bn_stats(STAT[:, m, :], src[:, m, :]).then_inc(ln_stats, 1)
            for m in range(TILES):
                dve.wait_ge(ln_stats, TILES * n + m + 1)
                nc.vector.bn_aggr(MV[:, m, :], STAT[:, m, :]).then_inc(ln_mv, 1)
            dve.wait_ge(ln_mv, TILES * (n + 1))
            nc.vector.tensor_scalar(VE[:, 0, :], MV[:, :, 1], EPS, None, ALU.add).then_inc(ln_var, 1)
            dve.wait_ge(ln_root, n + 1)
            nc.vector.reciprocal(VE[:, 2, :], VE[:, 1, :]).then_inc(ln_inv, 1)
            dve.wait_ge(ln_inv, n + 1)
            for m in range(TILES):
                nc.vector.tensor_scalar(XNT[:, m, :], src[:, m, :], MV[:, m, 0:1], VE[:, 2, m:m + 1],
                                        ALU.subtract, ALU.mult).then_inc(ln_rows, 1)

        def ln_act(act, n):
            act.wait_ge(ln_var, n + 1)
            nc.scalar.activation(VE[:, 1, :], VE[:, 0, :], ACT.Sqrt).then_inc(ln_root, 1)

        def turn(pe, src, c, hf):
            for k in range(4):
                last = nc.tensor.transpose(banks[2 * c + hf][:, k * P:(k + 1) * P],
                                           src[:, 4 * hf + k, c * P:(c + 1) * P], IDENT)
            last.then_inc(turned, 1)

        def ln_turn(pe, n):
            for hf in range(2):
                pe.wait_ge(ln_rows, TILES * n + 4 * hf + 4)
                for c in range(C):
                    turn(pe, XNT, c, hf)

        TURN_ORDER = [(c, hf) for hf in range(2) for c in range(C)]

        def g_par(j):
            return j % 2

        PRODUCT_BANKS = (3, 5, 6, 7)
        PROJ = [[("v", 1), ("qk", 4)], [("v", 2), ("qk", 5)], [("v", 3), ("qk", 6)], [("qk", 7)], [("qk", 8)],
                [("qk", 9)], [("qk", 10)], [("v", 4), ("qk", 11)]]
        PROLOGUE = [("qk", 0), ("qk", 1), ("v", 0), ("qk", 2), ("qk", 3)]

        def slots(case):
            return [[x for x in PROJ[s] if case != "last" or s < 4]
                    + ([("o", s - 3)] if case != "first" or s >= 3 else []) for s in range(8)]

        def flat(case):
            return [x for y in slots(case) for x in y]

        def earlier(line):
            step = {"qk": 8, "v": 4, "o": 8}
            return [(k, n - step[k]) for k, n in line]

        def products(case, s):
            if case == "prologue":
                at, before, line = 0, [None] * 4, PROLOGUE
                todo = PROLOGUE
            elif case == "end":
                at, before = len(PROLOGUE + flat("first") + flat("last")), flat("last")[-4:]
                line = todo = [("o", 5), ("o", 6), ("o", 7)]
            else:
                at = len(PROLOGUE) + (0 if case == "first" else len(flat("first")))
                before = PROLOGUE[-4:] if case == "first" else earlier(flat("steady")[-4:])
                line, todo = flat(case), slots(case)[s]
                k = sum(len(y) for y in slots(case)[:s])
                return [(*x, PRODUCT_BANKS[(at + k + m) % 4], (before + line)[k + m]) for m, x in enumerate(todo)]
            return [(*x, PRODUCT_BANKS[(at + m) % 4], (before + line)[m]) for m, x in enumerate(todo)]

        def wait_taken(eng, I, product):
            if product is not None:
                kind, n = product
                if kind == "qk":
                    eng.wait_ge(qk_lo, 8 * I + n + 1)
                elif kind == "v":
                    eng.wait_ge(v_added, 4 * I + n + 1)
                else:
                    eng.wait_ge(o_added, 8 * I + n + 1)

        def attention_pairs(eng, a, pair):
            pair(8 * a, "first")
            with eng.Fori(8 * a + 1, 8 * a + 7) as i:
                pair(i, "steady")
            pair(8 * a + 7, "last")

        def lagged(case, s, lag):
            return not (case == "first" and s < lag)

        @block.sync
        def _(sp):
            sp.dma_start(CRAW, ctx_in.rearrange("b (h p) d -> p (b h) d", p=P)).then_inc(ld_c, 16)
            for dst, src in ((CONST[:, :, :], const_in), (VEC[:, :, :], vec_in), (VECA[:, :], veca_in),
                             (PREV[:, :, :], prev_in), (S0[:, :], s0_in)):
                sp.dma_start(dst, src).then_inc(ld_small, 16)
            sp.dma_start(W1L[:, :, :, :], w1l_in).then_inc(ld_w1l, 16)
            sp.dma_start(X[:, :, :], x_in.rearrange("b (h p) d -> p (b h) d", p=P)).then_inc(ld_x, 16)
            sp.dma_start(WRK[:, :], wrk_in[0]).then_inc(ld_wrk, 16)

            def to_scan(src, dst, name):
                for b in range(B):
                    for c in range(C):
                        p0 = 32 * b + 16 * c
                        sp.dma_start(dst[p0:p0 + 16, :, :], src[:, 4 * c + b, :]).then_inc(moved[name], 16)

            def rwkv_moves(li):
                for n, (src, dst, name) in enumerate(((WT, WS, "w"), (KT, KS, "k"), (VT, VS, "v"),
                                                      (RT, RS, "r"))):
                    if name == "w":
                        sp.wait_ge(decay_e, 4 * (li + 1))
                    else:
                        sp.wait_ge(proj_out, 18 * li + 2 + 4 * (n + 1))
                    to_scan(src, dst, name)
                sp.wait_ge(att_out, 4 * (li + 1))
                for b in range(B):
                    for c in range(C):
                        p0 = 32 * b + 16 * c
                        sp.dma_start(ATT[:, 4 * c + b, :], AS[p0:p0 + 16, :, :]).then_inc(moved["a"], 16)

            rwkv_moves(0)
            sp.wait_ge(x_sum, 8)
            sp.dma_start(MU8[:, :], mask_in.to_broadcast([P, B * T])).then_inc(ld_mask, 16)
            sp.dma_start(WRK[:, :], wrk_in[1]).then_inc(ld_wrk, 16)
            rwkv_moves(1)

            def load_qk(H):
                sp.dma_start(WQK[:, :, :], w3_in[bass.ds(H, 1), :, 0:2, :].rearrange("o p w e -> p (o w) e")
                             ).then_inc(ld_wqk, 16)

            def load_wo(H):
                sp.dma_start(WO3[:, :], w3_in[bass.ds(H, 1), :, 2, :].rearrange("o p e -> p (o e)")).then_inc(ld_wo3, 16)

            def load_wv(I):
                sp.dma_start(WV3[:, :, :], wv_in[bass.ds(I, 1), :, :, :].rearrange("o p c e -> p (o c) e")
                             ).then_inc(ld_wv, 16)

            def load_bv(I):
                sp.dma_start(BV[:, :], bv_in[bass.ds(I, 1), :].to_broadcast([P, 2 * D3])).then_inc(ld_bv, 16)

            def load_aux(a):
                sp.dma_start(WOALL, w3_in[H3 * a:H3 * (a + 1), :, 2, :].rearrange("h p e -> p h e")).then_inc(ld_wo, 16)
                sp.dma_start(BVD[:, :, :], biasv_in[a]).then_inc(ld_aux, 16)
                sp.wait_ge(waux_out, a + 1)
                sp.dma_start(WAUX[16:17, :], rows_in[a:a + 1, :]).then_inc(ld_bo, 16)

            def pair_loads(I):
                sp.wait_ge(wqk_lo, 2 * I + 3)
                load_qk(2 * I + 3)
                sp.wait_ge(wo_lo, 2 * I + 1)
                load_wo(2 * I + 1)
                sp.wait_ge(v_added, 4 * I + 4)
                load_bv(I + 1)
                sp.wait_ge(wv_lo, I + 2)
                load_wv(I + 2)
                sp.wait_ge(wqk_lo, 2 * I + 4)
                load_qk(2 * I + 4)
                sp.wait_ge(wo_lo, 2 * I + 2)
                load_wo(2 * I + 2)

            sp.wait_ge(x_sum, 20)
            load_qk(0)
            load_wv(0)
            load_bv(0)
            load_wo(0)
            sp.wait_ge(wqk_lo, 1)
            load_qk(1)
            sp.wait_ge(wv_lo, 1)
            load_wv(1)
            load_aux(0)
            sp.dma_start(FC1, fc1_in).then_inc(ld_fc1, 16)
            sp.dma_start(BFC2[:, :], rows_in[2:3, :].to_broadcast([P, E])).then_inc(ld_bfc2, 16)
            sp.wait_ge(wqk_lo, 2)
            load_qk(2)
            with sp.Fori(0, 8) as i:
                pair_loads(i)
            sp.wait_ge(x_sum, 24)
            load_aux(1)
            with sp.Fori(8, 14) as i:
                pair_loads(i)
            sp.wait_ge(wqk_lo, 31)
            load_qk(31)
            sp.wait_ge(wo_lo, 29)
            load_wo(29)
            sp.wait_ge(v_added, 60)
            load_bv(15)
            sp.wait_ge(wo_lo, 30)
            load_wo(30)
            sp.wait_ge(wo_lo, 31)
            load_wo(31)
            sp.dma_start(FC2, fc2_in).then_inc(ld_fc2, 16)
            for pair in range(4):
                sp.wait_ge(x_sum, 30 + pair)
                sp.dma_start(out.rearrange("b (h p) d -> p (b h) d", p=P)[:, 2 * pair:2 * pair + 2, :],
                             X[:, 2 * pair:2 * pair + 2, :]).then_inc(stored, 16)
            sp.wait_ge(stored, 64)

        @block.tensor
        def _(pe):
            def proj(bank, w, col, rhs, hf, m=0, stride=E):
                for c in range(C):
                    last = nc.tensor.matmul(banks[bank][:, :], w[:, col + stride * c + P * m:col + stride * c + P * m + P],
                                            rhs[:, 4 * c + 2 * hf:4 * c + 2 * hf + 2, :], start=(c == 0),
                                            stop=(c == C - 1))
                return last

            def rows(bank, w, rhs, pair):
                for k in range(2):
                    m = 2 * pair + k
                    for c in range(C):
                        last = nc.tensor.matmul(banks[bank][:, k * E:(k + 1) * E],
                                                rhs[:, 4 * c + m // 2, (m % 2) * P:(m % 2) * P + P],
                                                w[:, c * E:(c + 1) * E], start=(c == 0), stop=(c == C - 1))
                return last

            def context():
                pe.wait_ge(ld_c, 16)
                pe.wait_ge(ld_small, 80)
                for c, hf in TURN_ORDER:
                    turn(pe, CRAW, c, hf)
                pe.wait_ge(ct_hi, 4)
                pe.wait_ge(ct_lo, 4)
                ln_turn(pe, 0)
                pe.wait_ge(ld_w1l, 16)
                pe.wait_ge(at_ready, 4)
                for m in range(C):
                    for hf in range(2):
                        proj(4 + 2 * m + hf, W1L[:, 1, :, :].rearrange("p c e -> p (c e)"), 0, AT, hf, m).then_inc(k1_proj, 1)
                for pair in range(4):
                    rows(pair, W1L[:, 2, :, :].rearrange("p c e -> p (c e)"), AT, pair).then_inc(v1_proj, 1)

            def rwkv(li, n_ln, xs):
                pe.wait_ge(ld_wrk, 16 * (li + 1))
                ln_turn(pe, n_ln)
                for m in range(2):
                    for hf in range(2):
                        pe.wait_ge(xmix_ready, 2 * (li + 1))
                        proj(4 + 2 * m + hf, WRK, W1, X5[2], hf, m).then_inc(m1_ready, 1)
                pe.wait_ge(m1_tanh, 4 * (li + 1))

                def mix(n):
                    j = MIX[n]
                    for q in range(4):
                        c, hf = q // 2, q % 2
                        if n:
                            pe.wait_ge(mix_scaled, 20 * li + 4 * n + q - 3)
                        nc.tensor.matmul(banks[q][:, :], WRK[:, W2 + 256 * j + P * c:W2 + 256 * j + P * c + P],
                                         M1[:, j // 4, hf * HALF:(hf + 1) * HALF], start=True,
                                         stop=True).then_inc(mix_ready, 1)

                def project(n, col):
                    pe.wait_ge(x5_ready, 20 * li + 4 * (n + 1))
                    for q in range(4):
                        if n == 1:
                            pe.wait_ge(decay_e, 4 * li + q + 1)
                        else:
                            pe.wait_ge(proj_out, 18 * li + 2 + 4 * (n - 1) + q + 1)
                        proj(4 + q, WRK, col, X5[n % 3], q % 2, q // 2).then_inc(proj_ready, 1)

                mix(0)
                mix(1)
                pe.wait_ge(x5_ready, 20 * li + 4)
                for hf in range(2):
                    proj(4 + hf, WRK, DW1, X5[0], hf, 0, P).then_inc(proj_ready, 1)
                mix(2)
                pe.wait_ge(proj_out, 18 * li + 2)
                for q in range(4):
                    c, hf = q // 2, q % 2
                    nc.tensor.matmul(banks[4 + q][:, :], WRK[:, DW2 + P * c:DW2 + P * c + P],
                                     DT[:, hf * HALF:(hf + 1) * HALF], start=True, stop=True).then_inc(proj_ready, 1)
                project(1, WK)
                mix(3)
                project(2, WV)
                mix(4)
                project(3, WR)
                project(4, WG)
                for k in range(9):
                    for q in range(4):
                        if k == 0:
                            pe.wait_ge(bonus_ready, li + 1)
                            src = T1
                        else:
                            pe.wait_ge(read_out, 8 * li + k)
                            src = MK[(k - 1) % 2]
                        last = nc.tensor.matmul(banks[q][:, :], IDENT, src[:, 2 * q:2 * q + 2, :],
                                                start=(k == 0), stop=(k == 8), skip_group_check=True)
                    last.then_inc(summed, 1)
                for q in range(4):
                    c, hf = q // 2, q % 2
                    if q == 0:
                        pe.wait_ge(moved["a"], 128 * (li + 1))
                        pe.wait_ge(g_ready, 4 * (li + 1))
                    nc.tensor.matmul(banks[4 + q][:, :], CENTER, ATT[:, 4 * c + 2 * hf:4 * c + 2 * hf + 2, :],
                                     start=True, stop=True).then_inc(centered, 1)
                for q in range(4):
                    c, hf = q // 2, q % 2
                    pe.wait_ge(squared, 4 * li + q + 1)
                    nc.tensor.matmul(banks[q][:, :], MEAN8, SQ[:, 4 * c + 2 * hf:4 * c + 2 * hf + 2, :],
                                     start=True, stop=True).then_inc(gvar, 1)
                pe.wait_ge(groot, 4 * (li + 1))
                for pair in range(4):
                    pe.wait_ge(y_ready, 4 * (li + 1))
                    rows(pair, WRK[:, WO:WO + 512], YT, pair).then_inc(wo_ready, 1)
                pe.wait_ge(x_sum, xs + 4)
                ln_turn(pe, n_ln + 1)
                for q in range(4):
                    pe.wait_ge(xkr_ready, 4 * li + 2)
                    proj(4 + q, WRK, FK, XK, q % 2, q // 2).then_inc(fk_ready, 1)
                pe.wait_ge(xkr_ready, 4 * li + 4)
                for pair in range(4):
                    rows(pair, WRK[:, FR:FR + 512], XR, pair).then_inc(fr_ready, 1)
                pe.wait_ge(fk_sq, 4 * (li + 1))
                for pair in range(4):
                    rows(4 + pair, WRK[:, FV:FV + 512], KK2, pair).then_inc(fv_ready, 1)

            def unit_scores(i, j, c):
                g, h, b = 8 * i + j, 2 * i + j // 4, j % 4
                if b in (0, 2):
                    pe.wait_ge(km_lo, 2 * h + 1 + b // 2)
                if not (isinstance(i, int) and g < 2):
                    pe.wait_ge(sc_max, g - 1)
                for tt in range(2):
                    qs = slice((2 * b + tt) * P, (2 * b + tt) * P + P)
                    ks = slice(b * T, (b + 1) * T)
                    for n, (q, k) in enumerate(((Q1h, KMh), (Q1h, KMl), (Q1l, KMh))):
                        last = nc.tensor.matmul(banks[g_par(j)][:, tt * T:(tt + 1) * T], q[:, c, qs],
                                                k[:, (j // 4) % 2, ks], start=(n == 0), stop=(n == 2))
                last.then_inc(sc_ready, 1)

            def unit_turn(i, j):
                g = 8 * i + j
                pe.wait_ge(p1_scaled, g + 1)
                if not (isinstance(g, int) and g < 2):
                    pe.wait_ge(pt_out, g - 1)
                for ss in range(2):
                    for tt in range(2):
                        last = nc.tensor.transpose(banks[2 + g_par(j)][:, ss * T + tt * P:ss * T + (tt + 1) * P],
                                                   P1[:, j % 4, tt, ss * P:(ss + 1) * P], IDENT)
                last.then_inc(p1_turned, 1)

            def unit_values(i, j, c):
                g, h, b = 8 * i + j, 2 * i + j // 4, j % 4
                first = isinstance(h, int) and h % HPC == 0
                if b == 0:
                    pe.wait_ge(vm_ready, 2 * h + 2)
                pe.wait_ge(pt_out, g + 1)
                for ss in range(2):
                    last = nc.tensor.matmul(banks[4 + 2 * c + b // 2][:, (b % 2) * T:(b % 2 + 1) * T],
                                            VM[:, (j // 4) % 2, 2 * b + ss, :],
                                            PT1[:, g_par(j), ss, :], start=(first and b % 2 == 0 and ss == 0), stop=(ss == 1),
                                            skip_group_check=True)
                last.then_inc(pv_done, 1)

            def audio():
                pe.wait_ge(x_sum, 8)
                for c, hf in TURN_ORDER:
                    turn(pe, X, c, hf)
                pe.wait_ge(xt_ready, 4)
                for q in range(4):
                    proj(4 + q, W1L[:, 0, :, :].rearrange("p c e -> p (c e)"), 0,
                         XT1[:, :, :].rearrange("p c (b t) -> p (c b) t", b=B), q % 2, q // 2).then_inc(q1_proj, 1)
                pe.wait_ge(q1_lo, 4)

                def body(i, c):
                    c_before = 0 if isinstance(i, int) and i == 4 else c
                    for j in range(8):
                        unit_scores(i, j, c)
                        if not (isinstance(i, int) and 8 * i + j < 2):
                            unit_turn(i, j - 2)
                        if not (isinstance(i, int) and 8 * i + j < 3):
                            unit_values(i, j - 3, c_before if j < 3 else c)

                for c in range(C):
                    body(4 * c, c)
                    with pe.Fori(4 * c + 1, 4 * c + 4) as i:
                        body(i, c)
                unit_turn(8, -2)
                unit_values(8, -3, 1)
                unit_turn(8, -1)
                unit_values(8, -2, 1)
                unit_values(8, -1, 1)
                pe.wait_ge(ao_turned, 4)
                for pair in range(4):
                    rows(pair, W1L[:, 3, :, :].rearrange("p c e -> p (c e)"),
                         AOT[:, :, :].rearrange("p c (b t) -> p (c b) t", b=B), pair).then_inc(out1_ready, 1)

            context()
            rwkv(0, 1, 0)
            audio()
            rwkv(1, 3, 12)

            def three(out_, lh, ll, rh, rl, first, last):
                nc.tensor.matmul(out_, lh, rh, start=first, stop=False)
                nc.tensor.matmul(out_, lh, rl, start=False, stop=False)
                return nc.tensor.matmul(out_, ll, rh, start=False, stop=last)

            def product(I, kind, n, bank, before):
                wait_taken(pe, I, before)
                if kind == "qk":
                    pr, hf, w = (n // 4) % 2, (n // 2) % 2, n % 2
                    pe.wait_ge(wqk_lo, 2 * I + n // 4 + 1)
                    rh, rl = ((Hh, Hl), (CTh, CTl))[w]
                    for c in range(C):
                        cs, ts = slice(c * D3, (c + 1) * D3), slice(hf * HALF, (hf + 1) * HALF)
                        last = three(banks[bank][:, :], WQKh[:, pr, w, cs], WQKl[:, pr, w, cs], rh[:, c, ts],
                                     rl[:, c, ts], c == 0, c == C - 1)
                    last.then_inc(qk_full, 1)
                elif kind == "v":
                    pe.wait_ge(wv_lo, I + n // 4 + 1)
                    for k in range(2):
                        for c in range(C):
                            ts = slice((2 * (n % 4) + k) * P, (2 * (n % 4) + k + 1) * P)
                            last = three(banks[bank][:, k * 2 * D3:(k + 1) * 2 * D3], CTh[:, c, ts], CTl[:, c, ts],
                                         WVh[:, c, :], WVl[:, c, :], c == 0, c == C - 1)
                    last.then_inc(v_full, 1)
                else:
                    pr = (n // 4) % 2
                    pe.wait_ge(c3_lo, 8 * I + n + 1)
                    pe.wait_ge(wo_lo, 2 * I + n // 4 + 1)
                    for tt in range(2):
                        ts = slice((2 * (n % 4) + tt) * P, (2 * (n % 4) + tt + 1) * P)
                        last = three(banks[bank][:, tt * E:(tt + 1) * E], C3h[:, pr, ts], C3l[:, pr, ts],
                                     WOh[:, pr, :], WOl[:, pr, :], True, True)
                    last.then_inc(o_full, 1)

            def scores3(I, s):
                par, b, G = s // 4, s % 4, 8 * I + s
                pe.wait_ge(qk_lo, 8 * I + 4 * par + 2 * (b // 2) + 2)
                pe.wait_ge(key_lo, 2 * I + par + 1)
                for tt in range(2):
                    if not (isinstance(G, int) and G < 1):
                        pe.wait_ge(p3_ready, 2 * G - 1 + tt)
                    ts = slice((2 * b + tt) * P, (2 * b + tt + 1) * P)
                    three(banks[tt][:, 0:KEYS], Q3h[:, par, ts], Q3l[:, par, ts], K3h[:, par, b, :],
                          K3l[:, par, b, :], True, True).then_inc(s3_ready, 1)

            def turn3(I, s):
                G = 8 * I + s
                pe.wait_ge(p3_scaled, 2 * G + 2)
                if not (isinstance(G, int) and G < 1):
                    pe.wait_ge(pt3_lo, G)
                for ss in range(2):
                    for tt in range(2):
                        last = nc.tensor.transpose(banks[2][:, ss * T + tt * P:ss * T + (tt + 1) * P],
                                                   P3[:, s % 2, tt, ss * P:(ss + 1) * P], IDENT)
                last.then_inc(p3_turned, 1)

            def values3(I, s):
                G, b, ds_ = 8 * I + s, s % 4, slice((s // 4 % 2) * D3, (s // 4 % 2 + 1) * D3)
                pe.wait_ge(pt3_lo, G + 1)
                pe.wait_ge(v_lo, 4 * I + (b + 1 if s >= 0 else b - 3))
                if not (isinstance(G, int) and G < 1):
                    pe.wait_ge(c3_lo, G)
                for ss in range(2):
                    m = 2 * b + ss
                    last = three(banks[4][:, 0:T], V3h[:, m, ds_], V3l[:, m, ds_],
                                 PT3h[:, s % 2, ss, :], PT3l[:, s % 2, ss, :], ss == 0, ss == 1)
                last.then_inc(c3_ready, 1)

            def pair(I, case):
                for s in range(8):
                    todo = products(case, s)
                    proj_ = [x for x in todo if x[0] != "o"]
                    scores3(I, s)
                    if proj_:
                        product(I, *proj_[0])
                    if lagged(case, s, 1):
                        turn3(I, s - 1)
                    for x in proj_[1:]:
                        product(I, *x)
                    if lagged(case, s, 2):
                        values3(I, s - 2)
                    for x in todo:
                        if x[0] == "o":
                            product(I, *x)

            def bias_products(a):
                pe.wait_ge(ld_wo, 16 * (a + 1))
                pe.wait_ge(ld_aux, 16 * (a + 1))
                for h in range(H3):
                    last = nc.tensor.matmul(banks[4][0:32, 0:E], BVD[:, h, :], WOALL[:, h, :], start=(h == 0),
                                            stop=(h == H3 - 1))
                last.then_inc(aux_ready, 1)

            def bias_rows(a):
                pe.wait_ge(p3_bias, 64 * (a + 1))
                pe.wait_ge(pt3_lo, 64 * (a + 1))
                for m in range(TILES):
                    last = nc.tensor.transpose(banks[2 + m // 4][0:32, (m % 4) * P:(m % 4 + 1) * P], PB[:, m, :], IDENT)
                    if m % 4 == 3:
                        last.then_inc(pb_turned, 1)
                pe.wait_ge(pbt_out, 2 * (a + 1))
                pe.wait_ge(ld_bo, 16 * (a + 1))
                pe.wait_ge(c3_lo, 64 * (a + 1))
                for pair in range(4):
                    for k in range(2):
                        m = 2 * pair + k
                        last = nc.tensor.matmul(banks[(0, 1, 4, 5)[pair]][:, k * E:(k + 1) * E],
                                                PBT[0:32, m * P:(m + 1) * P], WAUX[0:32, :], start=True, stop=True)
                    last.then_inc(aux_rows, 1)

            for a in range(2):
                pe.wait_ge(x_sum, 20 + 4 * a)
                bias_products(a)
                ln_turn(pe, 5 + a)
                pe.wait_ge(h_lo, 4 * (a + 1))
                for x in products("prologue", 0):
                    product(8 * a, *x)
                attention_pairs(pe, a, pair)
                I, ends = 8 * a + 7, products("end", 0)
                turn3(I, 7)
                values3(I, 6)
                product(I, *ends[0])
                values3(I, 7)
                product(I, *ends[1])
                product(I, *ends[2])
                bias_rows(a)

            pe.wait_ge(x_sum, 28)
            ln_turn(pe, 7)
            pe.wait_ge(ld_fc1, 16)
            pe.wait_ge(hm_ready, 4)
            for hf in range(2):
                for f in range(FT):
                    n = FT * hf + f
                    if n >= 4:
                        pe.wait_ge(gelu_out, n - 3)
                    for c in range(C):
                        last = nc.tensor.matmul(banks[4 + n % 4][:, :], FC1[:, c, f * P:(f + 1) * P],
                                                HM3[:, c, hf * HALF:(hf + 1) * HALF], start=(c == 0),
                                                stop=(c == C - 1))
                    last.then_inc(fc1_ready, 1)
            pe.wait_ge(ld_fc2, 16)
            for pair in range(4):
                pe.wait_ge(gelu_out, FT * (pair // 2 + 1))
                for k in range(2):
                    m = 2 * pair + k
                    for f in range(FT):
                        last = nc.tensor.matmul(banks[pair][:, k * E:(k + 1) * E], G3[:, f, m * P:(m + 1) * P],
                                                FC2[:, f, :], start=(f == 0), stop=(f == FT - 1))
                last.then_inc(fc2_ready, 1)

        @block.scalar
        def _(act):
            def context():
                act.wait_ge(ld_small, 80)
                for i, (c, hf) in enumerate(TURN_ORDER):
                    act.wait_ge(turned, i + 1)
                    nc.scalar.copy(CTh[:, c, hf * HALF:(hf + 1) * HALF], banks[2 * c + hf][:, :]).then_inc(ct_hi, 1)
                ln_act(act, 0)
                for i, (c, hf) in enumerate(TURN_ORDER):
                    act.wait_ge(turned, 4 + i + 1)
                    nc.scalar.activation(AT[:, 4 * c + 2 * hf:4 * c + 2 * hf + 2, :],
                                         banks[2 * c + hf][:, :].rearrange("p (b t) -> p b t", b=2), ACT.Identity,
                                         scale=VECA[:, G1 + c:G1 + c + 1],
                                         bias=VECA[:, B1 + c:B1 + c + 1]).then_inc(at_ready, 1)
                for q in range(4):
                    act.wait_ge(k1_proj, q + 1)
                    nc.scalar.copy(K1[:, q // 2, (q % 2) * HALF:(q % 2 + 1) * HALF], banks[4 + q][:, :]).then_inc(k1_hi, 1)
                for pair in range(4):
                    act.wait_ge(v1_proj, pair + 1)
                    nc.scalar.copy(V1[:, 2 * pair:2 * pair + 2, :],
                                   banks[pair][:, :].rearrange("p (m d) -> p m d", m=2)).then_inc(v1_ready, 1)

            def shifted_rows(li, n_ln, n_turn, w, b, prev):
                ln_act(act, n_ln)
                nc.scalar.copy(XN[:, :, 0], PREV[:, prev, :]).then_inc(xn_ready, 1)
                for i, (c, hf) in enumerate(TURN_ORDER):
                    act.wait_ge(turned, 4 * n_turn + i + 1)
                    nc.scalar.activation(XN[:, 4 * c + 2 * hf:4 * c + 2 * hf + 2, 1:T + 1],
                                         banks[2 * c + hf][:, :].rearrange("p (b t) -> p b t", b=2), ACT.Identity,
                                         scale=lnw(li, w, c), bias=lnw(li, b, c)).then_inc(xn_ready, 1)

            def take(q, dst, func=ACT.Copy, sem_=None, **kw):
                c, hf = q // 2, q % 2
                return nc.scalar.activation(dst[:, 4 * c + 2 * hf:4 * c + 2 * hf + 2, :],
                                            banks[4 + q][:, :].rearrange("p (b t) -> p b t", b=2), func, **kw)

            def rwkv(li, n_ln, n_turn):
                shifted_rows(li, n_ln, n_turn, LN1W, LN1B, 1)
                for q in range(4):
                    act.wait_ge(m1_ready, 4 * li + q + 1)
                    nc.scalar.activation(M1[:, q // 2, (q % 2) * HALF:(q % 2 + 1) * HALF], banks[4 + q][:, :],
                                         ACT.Tanh).then_inc(m1_tanh, 1)
                for hf in range(2):
                    act.wait_ge(proj_ready, 22 * li + hf + 1)
                    nc.scalar.activation(DT[:, hf * HALF:(hf + 1) * HALF], banks[4 + hf][:, :],
                                         ACT.Tanh).then_inc(proj_out, 1)
                for q in range(4):
                    act.wait_ge(proj_ready, 22 * li + 2 + q + 1)
                    take(q, WT, ACT.Exp, bias=lnw(li, TD, q // 2)).then_inc(proj_out, 1)
                for q in range(4):
                    act.wait_ge(proj_out, 18 * li + 2 + q + 1)
                    v = WT[:, 4 * (q // 2) + 2 * (q % 2):4 * (q // 2) + 2 * (q % 2) + 2, :]
                    nc.scalar.activation(v, v, ACT.Exp, scale=-1.0).then_inc(decay_e, 1)
                for n, dst in ((1, KT), (2, VT), (3, RT)):
                    for q in range(4):
                        act.wait_ge(proj_ready, 22 * li + 2 + 4 * n + q + 1)
                        take(q, dst).then_inc(proj_out, 1)
                for q in range(4):
                    act.wait_ge(proj_ready, 22 * li + 18 + q + 1)
                    take(q, TH, ACT.Tanh, scale=0.5).then_inc(gate_th, 1)
                for k in range(S):
                    if k >= 2:
                        act.wait_ge(read_out, 8 * li + k - 1)
                    else:
                        act.wait_ge(moved["v" if k else "k"], 128 * (li + 1))
                        act.wait_ge(moved["r"], 128 * (li + 1))
                    nc.scalar.copy(SS[k % 2][:, :, 0], S0[:, S * k:S * k + S]).then_inc(state0, 1)
                for q in range(4):
                    act.wait_ge(summed, 9 * (li + 1))
                    nc.scalar.copy(AS[:, 2 * q:2 * q + 2, :],
                                   banks[q][:, :].rearrange("p (b t) -> p b t", b=2)).then_inc(att_out, 1)
                for q in range(4):
                    act.wait_ge(centered, 4 * li + q + 1)
                    take(q, SQ, ACT.Square).then_inc(squared, 1)
                for q in range(4):
                    act.wait_ge(gvar, 4 * li + q + 1)
                    act.wait_ge(eps_set, 1)
                    c, hf = q // 2, q % 2
                    nc.scalar.activation(SD[:, 4 * c + 2 * hf:4 * c + 2 * hf + 2, :],
                                         banks[q][:, :].rearrange("p (b t) -> p b t", b=2), ACT.Sqrt,
                                         bias=EPSC[:, 0:1]).then_inc(groot, 1)
                shifted_rows(li, n_ln + 1, n_turn + 1, LN2W, LN2B, 0)
                for q in range(4):
                    act.wait_ge(fk_pos, 4 * li + q + 1)
                    c, hf = q // 2, q % 2
                    sl = slice(4 * c + 2 * hf, 4 * c + 2 * hf + 2)
                    nc.scalar.activation(KK2[:, sl, :], KK[:, sl, :], ACT.Square).then_inc(fk_sq, 1)
                for pair in range(4):
                    act.wait_ge(fr_ready, 4 * li + pair + 1)
                    nc.scalar.activation(RR[:, 2 * pair:2 * pair + 2, :],
                                         banks[pair][:, :].rearrange("p (b t) -> p b t", b=2), ACT.Tanh,
                                         scale=0.5).then_inc(fr_th, 1)

            def audio():
                for i, (c, hf) in enumerate(TURN_ORDER):
                    act.wait_ge(turned, 16 + i + 1)
                    nc.scalar.copy(XT1[:, c, hf * HALF:(hf + 1) * HALF], banks[2 * c + hf][:, :]).then_inc(xt_ready, 1)
                nc.scalar.activation(GT[:, :], VECA[:, GATE:GATE + 1], ACT.Tanh).then_inc(gate_done, 1)
                for q in range(4):
                    act.wait_ge(q1_proj, q + 1)
                    nc.scalar.copy(Q1h[:, q // 2, (q % 2) * HALF:(q % 2 + 1) * HALF], banks[4 + q][:, :]).then_inc(q1_hi, 1)

                def weights(i, j):
                    g = 8 * i + j
                    act.wait_ge(sc_max, g + 1)
                    for tt in range(2):
                        last = nc.scalar.activation(P1[:, j % 4, tt, :], P1[:, j % 4, tt, :], ACT.Exp,
                                                    scale=D1 ** -0.5, bias=NS1[:, g_par(j), tt:tt + 1],
                                                    accum_out=RS1[:, g_par(j), tt:tt + 1])
                    last.then_inc(p1_ready, 1)

                def take_turned(i, j):
                    g = 8 * i + j
                    act.wait_ge(p1_turned, g + 1)
                    if not (isinstance(g, int) and g < 2):
                        act.wait_ge(pv_done, g - 1)
                    nc.scalar.copy(PT1[:, g_par(j), :, :],
                                   banks[2 + g_par(j)][:, :].rearrange("p (s t) -> p s t", s=2)).then_inc(pt_out, 1)

                def body(i):
                    for j in range(8):
                        if not (isinstance(i, int) and 8 * i + j < 2):
                            take_turned(i, j - 2)
                        weights(i, j)

                body(0)
                with act.Fori(1, 8) as i:
                    body(i)
                take_turned(8, -2)
                take_turned(8, -1)
                for q in range(4):
                    act.wait_ge(pv_done, 4 * H1 - 2 + 2 * (q % 2) if q >= 2 else 2 * H1)
                    nc.scalar.copy(AOT[:, q // 2, (q % 2) * HALF:(q % 2 + 1) * HALF],
                                   banks[4 + q][:, :]).then_inc(ao_turned, 1)

            context()
            rwkv(0, 1, 2)
            audio()
            rwkv(1, 3, 5)

            def qk_high(H, par):
                act.wait_ge(ld_wqk, 16 * (H + 1))
                nc.scalar.copy(WQKh[:, par, :, :], WQK[:, :, :]).then_inc(wqk_hi, 1)

            def wo_high(H, par):
                act.wait_ge(ld_wo3, 16 * (H + 1))
                if not (isinstance(H, int) and H < 2):
                    act.wait_ge(o_full, 4 * H - 4)
                nc.scalar.copy(WOh[:, par, :], WO3[:, :]).then_inc(wo_hi, 1)

            def wv_high(I):
                act.wait_ge(ld_wv, 16 * (I + 1))
                nc.scalar.copy(WVh[:, :, :], WV3[:, :, :]).then_inc(wv_hi, 1)

            def key_bias(H, par):
                act.wait_ge(hb_ready, H + 1)
                nc.scalar.copy(K3h[:, par, :, T:KEYS],
                               HB[:, par, 2:3].unsqueeze(2).to_broadcast([P, B, 2])).then_inc(key_hi, 1)

            def take_high(I, kind, n, bank, before):
                if kind == "qk":
                    pr, hf = (n // 4) % 2, (n // 2) % 2
                    act.wait_ge(hb_ready, 2 * I + n // 4 + 1)
                    act.wait_ge(qk_full, 8 * I + n + 1)
                    if n % 2 == 0:
                        nc.scalar.activation(Q3h[:, pr, hf * HALF:(hf + 1) * HALF], banks[bank][:, :], ACT.Identity,
                                             bias=HB[:, pr, 0:1]).then_inc(qk_hi, 1)
                    else:
                        nc.scalar.activation(K3h[:, pr, 2 * hf:2 * hf + 2, 0:T],
                                             banks[bank][:, :].rearrange("p (b t) -> p b t", b=2), ACT.Identity,
                                             bias=HB[:, pr, 1:2]).then_inc(qk_hi, 1)
                elif kind == "v":
                    m = 2 * (n % 4)
                    act.wait_ge(v_added, 4 * I + n + 1)
                    nc.scalar.copy(V3h[:, m:m + 2, :], V3[:, n % 2, :, :]).then_inc(v_hi, 1)

            def turned_high(I, s):
                act.wait_ge(p3_turned, 8 * I + s + 1)
                nc.scalar.copy(PT3h[:, s % 2, :, :],
                               banks[2][:, :].rearrange("p (s t) -> p s t", s=2)).then_inc(pt3_hi, 1)

            def weights3(I, s):
                G = 8 * I + s
                act.wait_ge(s3_shift, G + 1)
                if not (isinstance(G, int) and G < 2):
                    act.wait_ge(p3_bias, G - 1)
                    act.wait_ge(p3_turned, G - 1)
                for tt in range(2):
                    nc.scalar.activation(P3[:, s % 2, tt, 0:T + 1], banks[tt][:, 0:T + 1], ACT.Exp,
                                         scale=D3 ** -0.5, bias=NS3[:, s % 2, tt:tt + 1],
                                         accum_out=RS3[:, s % 2, tt:tt + 1]).then_inc(p3_ready, 1)

            def context_high(I, s):
                act.wait_ge(c3_ready, 8 * I + s + 1)
                nc.scalar.copy(C3h[:, (s // 4) % 2, (s % 4) * T:(s % 4 + 1) * T], banks[4][:, 0:T]).then_inc(c3_hi, 1)

            def pair(I, case):
                final = isinstance(I, int) and I == 15
                for s in range(8):
                    todo = [x for x in products(case, s) if x[0] != "o"]
                    weights3(I, s)
                    if todo:
                        take_high(I, *todo[0])
                    if lagged(case, s, 1):
                        turned_high(I, s - 1)
                    for x in todo[1:]:
                        take_high(I, *x)
                    if lagged(case, s, 2):
                        context_high(I, s - 2)
                    if s == 0 and not final:
                        qk_high(2 * I + 2, 0)
                    if s == 4 and not final:
                        qk_high(2 * I + 3, 1)
                    if s % 4 == 1:
                        wo_high(2 * I + s // 4, s // 4)
                    if s == 1:
                        key_bias(2 * I + 1, 1)
                    if s == 5 and not final:
                        key_bias(2 * I + 2, 0)
                    if s == 3 and not final:
                        wv_high(I + 1)

            for a in range(2):
                if a == 0:
                    qk_high(0, 0)
                    wv_high(0)
                    key_bias(0, 0)
                act.wait_ge(aux_ready, a + 1)
                nc.scalar.copy(WAUX[0:32, :], banks[4][0:32, 0:E]).then_inc(waux_out, 1)
                if a == 0:
                    qk_high(1, 1)
                ln_act(act, 5 + a)
                for i, (c, hf) in enumerate(TURN_ORDER):
                    act.wait_ge(turned, 28 + 4 * a + i + 1)
                    v = slice(hf * HALF, (hf + 1) * HALF)
                    nc.scalar.activation(HF[:, c, v], banks[2 * c + hf][:, :], ACT.Identity,
                                         scale=VECA[:, LN3 + 4 * a + c:LN3 + 4 * a + c + 1],
                                         bias=VECA[:, LN3 + 4 * a + 2 + c:LN3 + 4 * a + 3 + c]).then_inc(h_rows, 1)
                    act.wait_ge(h_rows, 4 * a + i + 1)
                    nc.scalar.copy(Hh[:, c, v], HF[:, c, v]).then_inc(h_hi, 1)
                for x in products("prologue", 0):
                    take_high(8 * a, *x)
                attention_pairs(act, a, pair)
                turned_high(8 * a + 7, 7)
                context_high(8 * a + 7, 6)
                context_high(8 * a + 7, 7)
                for k in range(2):
                    act.wait_ge(pb_turned, 2 * a + k + 1)
                    nc.scalar.copy(PBT[0:32, k * HALF:(k + 1) * HALF], banks[2 + k][0:32, :]).then_inc(pbt_out, 1)

            ln_act(act, 7)
            for i, (c, hf) in enumerate(TURN_ORDER):
                act.wait_ge(turned, 36 + i + 1)
                nc.scalar.activation(HM3[:, c, hf * HALF:(hf + 1) * HALF], banks[2 * c + hf][:, :], ACT.Identity,
                                     scale=VECA[:, LN3 + 8 + c:LN3 + 9 + c],
                                     bias=VECA[:, LN3 + 10 + c:LN3 + 11 + c]).then_inc(hm_ready, 1)
            for n in range(2 * FT):
                hf, f = n // FT, n % FT
                act.wait_ge(fc1_ready, n + 1)
                nc.scalar.activation(G3[:, f, hf * HALF:(hf + 1) * HALF], banks[4 + n % 4][:, :], ACT.Gelu,
                                     bias=VECA[:, BFC1 + f:BFC1 + f + 1]).then_inc(gelu_out, 1)

        @block.vector
        def _(dve):
            def context():
                nc.vector.memset(EPSC[:, :], EPS).then_inc(eps_set, 1)
                dve.wait_ge(ld_c, 16)
                ln_dve(dve, 0, CRAW)
                for i, (c, hf) in enumerate(TURN_ORDER):
                    dve.wait_ge(ct_hi, i + 1)
                    v = slice(hf * HALF, (hf + 1) * HALF)
                    nc.vector.tensor_tensor(CTl[:, c, v], banks[2 * c + hf][:, :], CTh[:, c, v].bitcast(F32),
                                            ALU.subtract).then_inc(ct_lo, 1)

            def add_rows(sem_, n0, first_bank):
                for pair in range(4):
                    dve.wait_ge(sem_, n0 + pair + 1)
                    nc.vector.tensor_tensor(X[:, 2 * pair:2 * pair + 2, :],
                                            banks[first_bank + pair][:, :].rearrange("p (m d) -> p m d", m=2),
                                            X[:, 2 * pair:2 * pair + 2, :], ALU.add).then_inc(x_sum, 1)

            def rwkv(li, n_ln, xs):
                ln_dve(dve, n_ln, X)
                dve.wait_ge(xn_ready, 10 * li + 5)
                nc.vector.tensor_tensor(SX, XN[:, :, 0:T], XN[:, :, 1:T + 1], ALU.subtract).then_inc(sx_ready, 1)
                dve.wait_ge(sx_ready, 2 * li + 1)
                for c in range(C):
                    v = slice(4 * c, 4 * c + 4)
                    nc.vector.scalar_tensor_tensor(X5[2][:, v, :], SX[:, v, :], lnw(li, MAAX, c),
                                                   XN[:, v, 1:T + 1], ALU.mult, ALU.add).then_inc(xmix_ready, 1)
                for n in range(5):
                    for q in range(4):
                        c, hf = q // 2, q % 2
                        v = slice(4 * c + 2 * hf, 4 * c + 2 * hf + 2)
                        dve.wait_ge(mix_ready, 20 * li + 4 * n + q + 1)
                        if n == 3:
                            dve.wait_ge(proj_ready, 22 * li + 2)
                        if n == 4:
                            dve.wait_ge(proj_ready, 22 * li + 10)
                        nc.vector.scalar_tensor_tensor(X5[n % 3][:, v, :],
                                                       banks[q][:, :].rearrange("p (b t) -> p b t", b=2),
                                                       lnw(li, STACK + 2 * MIX[n], c), SX[:, v, :], ALU.add,
                                                       ALU.mult).then_inc(mix_scaled, 1)
                for q in range(4):
                    c, hf = q // 2, q % 2
                    v = slice(4 * c + 2 * hf, 4 * c + 2 * hf + 2)
                    dve.wait_ge(gate_th, 4 * li + q + 1)
                    nc.vector.scalar_tensor_tensor(G2[:, v, :], TH[:, v, :], 1.0,
                                                   banks[4 + q][:, :].rearrange("p (b t) -> p b t", b=2), ALU.add,
                                                   ALU.mult).then_inc(g_ready, 1)
                for name in "kr":
                    dve.wait_ge(moved[name], 128 * (li + 1))
                for k in range(S):
                    nc.vector.scalar_tensor_tensor(RK[:, k, :], KS[:, k, :], VEC[:, li, UCOL + k:UCOL + k + 1],
                                                   RS[:, k, :], ALU.mult, ALU.mult).then_inc(coef_rk, 1)
                dve.wait_ge(coef_rk, 8 * (li + 1))
                nc.vector.tensor_reduce(CF[:, :], RK.rearrange("p k t -> p t k"), AX_X, ALU.add).then_inc(coef_ready, 1)
                dve.wait_ge(coef_ready, li + 1)
                dve.wait_ge(moved["v"], 128 * (li + 1))
                nc.vector.tensor_tensor(T1, VS, CF[:, :].unsqueeze(1).to_broadcast([P, S, T]),
                                        ALU.mult).then_inc(bonus_ready, 1)
                dve.wait_ge(moved["w"], 128 * (li + 1))
                for k in range(S):
                    if k < S - POOL_K:
                        if k >= 2:
                            dve.wait_ge(scanned, 64 * li + 8 * (k - 1))
                        nc.vector.tensor_tensor(AK[k % 2], VS, KS[:, k, :].unsqueeze(1).to_broadcast([P, S, T]),
                                                ALU.mult).then_inc(outer_dve, 1)
                        dve.wait_ge(outer_dve, (S - POOL_K) * li + k + 1)
                    else:
                        dve.wait_ge(outer_pool, POOL_K * li + k - (S - POOL_K) + 1)
                    dve.wait_ge(state0, 8 * li + k + 1)
                    for d in range(S):
                        nc.vector.tensor_tensor_scan(SS[k % 2][:, d, 1:T + 1], WS[:, k, :], AK[k % 2][:, d, :],
                                                     S0[:, S * k + d:S * k + d + 1], ALU.mult,
                                                     ALU.add).then_inc(scanned, 1)
                    dve.wait_ge(scanned, 64 * li + 8 * (k + 1))
                    if k >= 2:
                        dve.wait_ge(summed, 9 * li + k)
                    nc.vector.tensor_tensor(MK[k % 2], SS[k % 2][:, :, 0:T],
                                            RS[:, k, :].unsqueeze(1).to_broadcast([P, S, T]),
                                            ALU.mult).then_inc(read_out, 1)
                for q in range(4):
                    c, hf = q // 2, q % 2
                    v = slice(4 * c + 2 * hf, 4 * c + 2 * hf + 2)
                    dve.wait_ge(groot, 4 * li + q + 1)
                    nc.vector.reciprocal(SQ[:, v, :], SD[:, v, :]).then_inc(ginv, 1)
                    dve.wait_ge(ginv, 4 * li + q + 1)
                    nc.vector.tensor_tensor(YT[:, v, :], banks[4 + q][:, :].rearrange("p (b t) -> p b t", b=2),
                                            SQ[:, v, :], ALU.mult).then_inc(gnorm, 1)
                    dve.wait_ge(gnorm, 4 * li + q + 1)
                    nc.vector.tensor_scalar(SD[:, v, :], YT[:, v, :], lnw(li, GNW, c), lnw(li, GNB, c),
                                            ALU.mult, ALU.add).then_inc(gaff, 1)
                    dve.wait_ge(gaff, 4 * li + q + 1)
                    nc.vector.scalar_tensor_tensor(YT[:, v, :], SD[:, v, :], 0.5, G2[:, v, :], ALU.mult,
                                                   ALU.mult).then_inc(y_ready, 1)
                add_rows(wo_ready, 4 * li, 0)
                dve.wait_ge(x_sum, xs + 4)
                ln_dve(dve, n_ln + 1, X)
                dve.wait_ge(xn_ready, 10 * li + 10)
                nc.vector.tensor_tensor(SX, XN[:, :, 0:T], XN[:, :, 1:T + 1], ALU.subtract).then_inc(sx_ready, 1)
                dve.wait_ge(sx_ready, 2 * li + 2)
                for dst, col in ((XK, FMK), (XR, FMR)):
                    for c in range(C):
                        v = slice(4 * c, 4 * c + 4)
                        nc.vector.scalar_tensor_tensor(dst[:, v, :], SX[:, v, :], lnw(li, col, c),
                                                       XN[:, v, 1:T + 1], ALU.mult, ALU.add).then_inc(xkr_ready, 1)
                for q in range(4):
                    c, hf = q // 2, q % 2
                    v = slice(4 * c + 2 * hf, 4 * c + 2 * hf + 2)
                    dve.wait_ge(fk_ready, 4 * li + q + 1)
                    nc.vector.tensor_scalar(KK[:, v, :], banks[4 + q][:, :].rearrange("p (b t) -> p b t", b=2), 0.0,
                                            None, ALU.max).then_inc(fk_pos, 1)
                for pair in range(4):
                    v = slice(2 * pair, 2 * pair + 2)
                    dve.wait_ge(fv_ready, 4 * li + pair + 1)
                    dve.wait_ge(fr_th, 4 * li + pair + 1)
                    nc.vector.scalar_tensor_tensor(FT1[:, v, :], RR[:, v, :], 1.0,
                                                   banks[4 + pair][:, :].rearrange("p (b t) -> p b t", b=2), ALU.add,
                                                   ALU.mult).then_inc(fv_mul, 1)
                    dve.wait_ge(fv_mul, 4 * li + pair + 1)
                    nc.vector.scalar_tensor_tensor(X[:, v, :], FT1[:, v, :], 0.5, X[:, v, :], ALU.mult,
                                                   ALU.add).then_inc(x_sum, 1)

            def audio():
                dve.wait_ge(ld_mask, 16)
                nc.vector.tensor_copy(MASKB[:, :], MU8[:, :]).then_inc(mask_f, 1)
                dve.wait_ge(mask_f, 1)
                nc.vector.reciprocal(MASKB[:, :], MASKB[:, :]).then_inc(mask_r, 1)
                dve.wait_ge(mask_r, 1)
                nc.vector.tensor_scalar(MASKB[:, :], MASKB[:, :], -1.0, 1.0, ALU.mult, ALU.add).then_inc(mask_b, 1)
                dve.wait_ge(mask_b, 1)
                for q in range(4):
                    v = slice((q % 2) * HALF, (q % 2 + 1) * HALF)
                    dve.wait_ge(q1_hi, q + 1)
                    nc.vector.tensor_tensor(Q1l[:, q // 2, v], banks[4 + q][:, :], Q1h[:, q // 2, v].bitcast(F32),
                                            ALU.subtract).then_inc(q1_lo, 1)

                nc.vector.memset(VM[:, :, :, :], 0.0).then_inc(vm_clear, 1)
                nc.vector.memset(ZV[:, :, :], 0.0).then_inc(vm_clear, 1)

                def values_in(h, par, c):
                    if not (isinstance(h, int) and h < 2):
                        dve.wait_ge(pv_done, 4 * h - 4)
                    else:
                        dve.wait_ge(vm_clear, 2)
                    for value, k in ((ZV[:, :, :], (h - 2) % HPC if isinstance(h, int) else h - 2 - HPC * c),
                                     (V1[:, :, bass.ds(D1 * h, D1)], h - HPC * c)):
                        nc.vector.tensor_scalar(VM[:, par, :, bass.ds(D1 * k, D1)], value, 1.0, None,
                                                ALU.mult).then_inc(vm_ready, 1)

                def keys_high(h, par, c):
                    nc.vector.tensor_scalar(KMh[:, par, :], K1[:, c, :], VECA[:, bass.ds(HMASK + h - 8 * c, 1)],
                                            None, ALU.mult).then_inc(km_hi, 1)

                def keys_low(h, par, c, hf):
                    v = slice(hf * HALF, (hf + 1) * HALF)
                    dve.wait_ge(km_hi, h + 1)
                    nc.vector.scalar_tensor_tensor(KMl[:, par, v], K1[:, c, v],
                                                   VECA[:, bass.ds(HMASK + h - 8 * c, 1)],
                                                   KMh[:, par, v].bitcast(F32), ALU.mult,
                                                   ALU.subtract).then_inc(km_lo, 1)

                def body(i, c, c_next, last=False):
                    for j in range(8):
                        g, b = 8 * i + j, j % 4
                        dve.wait_ge(sc_ready, g + 1)
                        if not (isinstance(g, int) and g < 4):
                            dve.wait_ge(p1_turned, g - 3)
                        nc.vector.memset(CARRY[:, :], 0.0)
                        for tt in range(2):
                            nc.vector.tensor_tensor_reduce(P1[:, j % 4, tt, :],
                                                           banks[g_par(j)][:, tt * T:(tt + 1) * T],
                                                           MASKB[:, b * T:(b + 1) * T], 1.0, MOST_NEGATIVE,
                                                           ALU.add, ALU.max,
                                                           NM1[:, g_par(j), tt:tt + 1]).then_inc(sc_masked, 1)
                        dve.wait_ge(sc_masked, 2 * g + 2)
                        nc.vector.tensor_scalar(NS1[:, g_par(j), :], NM1[:, g_par(j), :], -D1 ** -0.5, None,
                                                ALU.mult).then_inc(sc_max, 1)
                        if b == 0:
                            values_in(2 * i + j // 4, j // 4, c)
                        if b and not (last and j > 4):
                            h, par, c_ = 2 * i + j // 4 + 1, (j // 4 + 1) % 2, c if j < 4 else c_next
                            if b == 1:
                                keys_high(h, par, c_)
                            else:
                                keys_low(h, par, c_, b - 2)
                        dve.wait_ge(p1_ready, g + 1)
                        nc.vector.reciprocal(RI1[:, g_par(j), :], RS1[:, g_par(j), :]).then_inc(p1_inv, 1)

                keys_high(0, 0, 0)
                keys_low(0, 0, 0, 0)
                keys_low(0, 0, 0, 1)
                for c in range(C):
                    body(4 * c, c, c)
                    with dve.Fori(4 * c + 1, 4 * c + 3) as i:
                        body(i, c, c)
                    body(4 * c + 3, c, 1, c == 1)
                dve.wait_ge(gate_done, 1)
                for pair in range(4):
                    dve.wait_ge(out1_ready, pair + 1)
                    nc.vector.scalar_tensor_tensor(X[:, 2 * pair:2 * pair + 2, :],
                                                   banks[pair][:, :].rearrange("p (m d) -> p m d", m=2),
                                                   GT[:, 0:1], X[:, 2 * pair:2 * pair + 2, :], ALU.mult,
                                                   ALU.add).then_inc(x_sum, 1)
                dve.wait_ge(x_sum, 12)

            context()
            dve.wait_ge(ld_x, 16)
            dve.wait_ge(ld_small, 80)
            dve.wait_ge(turned, 8)
            rwkv(0, 1, 0)
            audio()
            rwkv(1, 3, 12)

            def take_low(I, kind, n, bank, before):
                if kind == "qk":
                    pr, hf = (n // 4) % 2, (n // 2) % 2
                    dve.wait_ge(qk_hi, 8 * I + n + 1)
                    if n % 2 == 0:
                        v = slice(hf * HALF, (hf + 1) * HALF)
                        nc.vector.scalar_tensor_tensor(Q3l[:, pr, v], banks[bank][:, :],
                                                       HB[:, pr, 0:1],
                                                       Q3h[:, pr, v].bitcast(F32), ALU.add,
                                                       ALU.subtract).then_inc(qk_lo, 1)
                    else:
                        v = slice(2 * hf, 2 * hf + 2)
                        nc.vector.scalar_tensor_tensor(K3l[:, pr, v, 0:T],
                                                       banks[bank][:, :].rearrange("p (b t) -> p b t", b=2),
                                                       HB[:, pr, 1:2],
                                                       K3h[:, pr, v, 0:T].bitcast(F32), ALU.add,
                                                       ALU.subtract).then_inc(qk_lo, 1)
                elif kind == "v":
                    dve.wait_ge(v_full, 4 * I + n + 1)
                    dve.wait_ge(ld_bv, 16 * (I + n // 4 + 1))
                    if not (isinstance(I, int) and 4 * I + n < 2):
                        dve.wait_ge(v_lo, 4 * I + n - 1)
                    nc.vector.tensor_tensor(V3[:, n % 2, :, :],
                                            banks[bank][:, :].rearrange("p (m d) -> p m d", m=2),
                                            BV[:, :].unsqueeze(1).to_broadcast([P, 2, 2 * D3]),
                                            ALU.add).then_inc(v_added, 1)
                else:
                    v = slice(2 * (n % 4), 2 * (n % 4) + 2)
                    dve.wait_ge(o_full, 8 * I + n + 1)
                    nc.vector.tensor_tensor(X[:, v, :], banks[bank][:, :].rearrange("p (m d) -> p m d", m=2),
                                            X[:, v, :], ALU.add).then_inc(o_added, 1)

            def row_max(I, s):
                G = 8 * I + s
                for tt in range(2):
                    dve.wait_ge(s3_ready, 2 * G + tt + 1)
                    nc.vector.tensor_reduce(NM3[:, s % 2, tt:tt + 1], banks[tt][:, 0:T + 1], AX_X,
                                            ALU.max).then_inc(s3_max, 1)
                dve.wait_ge(s3_max, 2 * G + 2)
                nc.vector.tensor_scalar(NS3[:, s % 2, :], NM3[:, s % 2, :], -D3 ** -0.5, None,
                                        ALU.mult).then_inc(s3_shift, 1)

            def turned_low(I, s):
                dve.wait_ge(pt3_hi, 8 * I + s + 1)
                nc.vector.tensor_tensor(PT3l[:, s % 2, :, :],
                                        banks[2][:, :].rearrange("p (s t) -> p s t", s=2),
                                        PT3h[:, s % 2, :, :].bitcast(F32), ALU.subtract).then_inc(pt3_lo, 1)

            def invert(I, s):
                dve.wait_ge(p3_ready, 16 * I + 2 * s + 2)
                nc.vector.reciprocal(RI3[:, s % 2, :], RS3[:, s % 2, :]).then_inc(p3_inv, 1)

            def keep_bias(I, s, a):
                b, h = s % 4, 2 * I - 16 * a + s // 4
                dve.wait_ge(p3_scaled, 16 * I + 2 * s + 2)
                nc.vector.tensor_scalar(PB[:, 2 * b:2 * b + 2, bass.ds(h, 1)], P3[:, s % 2, :, T:T + 1], 1.0,
                                        None, ALU.mult).then_inc(p3_bias, 1)

            def context_low(I, s):
                pr, v = (s // 4) % 2, slice((s % 4) * T, (s % 4 + 1) * T)
                dve.wait_ge(c3_hi, 8 * I + s + 1)
                nc.vector.tensor_tensor(C3l[:, pr, v], banks[4][:, 0:T], C3h[:, pr, v].bitcast(F32),
                                        ALU.subtract).then_inc(c3_lo, 1)

            def head_biases(H, par):
                nc.vector.tensor_scalar(HB[:, par, :], VECA[:, BQ:HMASK].rearrange("p (w h) -> p w h", w=3)
                                        [:, :, bass.ds(H, 1)], 1.0, None, ALU.mult).then_inc(hb_ready, 1)

            def key_bias_low(H, par):
                dve.wait_ge(key_hi, H + 1)
                nc.vector.tensor_tensor(K3l[:, par, :, T:KEYS],
                                        HB[:, par, 2:3].unsqueeze(2).to_broadcast([P, B, 2]),
                                        K3h[:, par, :, T:KEYS].bitcast(F32), ALU.subtract).then_inc(key_lo, 1)

            for a in range(2):
                def pair(I, case):
                    final = isinstance(I, int) and I == 15
                    for s in range(8):
                        todo = [x for x in products(case, s) if x[0] != "o"]
                        row_max(I, s)
                        if lagged(case, s, 1):
                            keep_bias(I, s - 1, a)
                        if lagged(case, s, 4):
                            n = s - 4
                            if s:
                                take_low(I, *[x for x in products(case, s - 1) if x[0] == "o"][0])
                            else:
                                take_low(I - 1, *[x for x in products("steady", 7) if x[0] == "o"][0])
                        if todo and todo[0][0] == "v":
                            take_low(I, *todo[0])
                        invert(I, s)
                        if todo and todo[0][0] == "qk":
                            take_low(I, *todo[0])
                        if lagged(case, s, 1):
                            turned_low(I, s - 1)
                        for x in todo[1:]:
                            take_low(I, *x)
                        if lagged(case, s, 2):
                            context_low(I, s - 2)
                        if s == 0 and not final:
                            dve.wait_ge(qk_lo, 8 * I + 4)
                            dve.wait_ge(key_hi, 2 * I + 1)
                            dve.wait_ge(key_lo, 2 * I + 1)
                            head_biases(2 * I + 2, 0)
                        if s == 1:
                            dve.wait_ge(hb_ready, 2 * I + 2)
                            key_bias_low(2 * I + 1, 1)
                        if s == 4 and not final:
                            dve.wait_ge(qk_lo, 8 * I + 8)
                            dve.wait_ge(key_lo, 2 * I + 2)
                            head_biases(2 * I + 3, 1)
                        if s == 5 and not final:
                            dve.wait_ge(hb_ready, 2 * I + 3)
                            key_bias_low(2 * I + 2, 0)

                dve.wait_ge(x_sum, 20 + 4 * a)
                if a == 0:
                    head_biases(0, 0)
                    head_biases(1, 1)
                    key_bias_low(0, 0)
                ln_dve(dve, 5 + a, X)
                nc.vector.memset(PB[:, :, :], 0.0).then_inc(pb_clear, 1)
                dve.wait_ge(pb_clear, a + 1)
                nc.vector.memset(PB[:, :, 16:17], 1.0).then_inc(pb_one, 1)
                for i, (c, hf) in enumerate(TURN_ORDER):
                    dve.wait_ge(h_hi, 4 * a + i + 1)
                    v = slice(hf * HALF, (hf + 1) * HALF)
                    nc.vector.tensor_tensor(Hl[:, c, v], HF[:, c, v], Hh[:, c, v].bitcast(F32),
                                            ALU.subtract).then_inc(h_lo, 1)
                for x in products("prologue", 0):
                    take_low(8 * a, *x)
                dve.wait_ge(pb_one, a + 1)
                attention_pairs(dve, a, pair)
                I, ends = 8 * a + 7, products("end", 0)
                keep_bias(I, 7, a)
                take_low(I, *products("last", 7)[0])
                turned_low(I, 7)
                context_low(I, 6)
                take_low(I, *ends[0])
                context_low(I, 7)
                take_low(I, *ends[1])
                take_low(I, *ends[2])
                dve.wait_ge(o_added, 64 * (a + 1))
                for pair in range(4):
                    dve.wait_ge(aux_rows, 4 * a + pair + 1)
                    nc.vector.tensor_tensor(X[:, 2 * pair:2 * pair + 2, :],
                                            banks[(0, 1, 4, 5)[pair]][:, :].rearrange("p (m d) -> p m d", m=2),
                                            X[:, 2 * pair:2 * pair + 2, :], ALU.add).then_inc(x_sum, 1)

            dve.wait_ge(x_sum, 28)
            ln_dve(dve, 7, X)
            dve.wait_ge(ln_rows, 64)
            dve.wait_ge(ld_bfc2, 16)
            nc.vector.tensor_tensor(X[:, :, :], X[:, :, :], BFC2[:, :].unsqueeze(1).to_broadcast([P, TILES, E]),
                                    ALU.add).then_inc(x_sum, 1)
            dve.wait_ge(x_sum, 29)
            add_rows(fc2_ready, 0, 0)

        @block.gpsimd
        def _(pool):
            def rwkv(li):
                for n in range(5):
                    for q in range(4):
                        c, hf = q // 2, q % 2
                        v = slice(4 * c + 2 * hf, 4 * c + 2 * hf + 2)
                        pool.wait_ge(mix_scaled, 20 * li + 4 * n + q + 1)
                        nc.gpsimd.tensor_tensor(X5[n % 3][:, v, :], X5[n % 3][:, v, :], XN[:, v, 1:T + 1],
                                                ALU.add).then_inc(x5_ready, 1)
                for name in "kv":
                    pool.wait_ge(moved[name], 128 * (li + 1))
                for k in range(S - POOL_K, S):
                    pool.wait_ge(scanned, 64 * li + 8 * (k - 1))
                    nc.gpsimd.tensor_tensor(AK[k % 2], VS, KS[:, k, :].unsqueeze(1).to_broadcast([P, S, T]),
                                            ALU.mult).then_inc(outer_pool, 1)

            def audio():
                def scale(i, j):
                    pool.wait_ge(p1_inv, 8 * i + j + 1)
                    nc.gpsimd.tensor_tensor(P1[:, j % 4, :, :], P1[:, j % 4, :, :],
                                            RI1[:, g_par(j), :].unsqueeze(2).to_broadcast([P, 2, T]),
                                            ALU.mult).then_inc(p1_scaled, 1)

                with pool.Fori(0, 8) as i:
                    for j in range(8):
                        scale(i, j)

            rwkv(0)
            audio()
            rwkv(1)

            def qk_low(H, par):
                pool.wait_ge(wqk_hi, H + 1)
                nc.gpsimd.tensor_tensor(WQKl[:, par, :, :], WQK[:, :, :], WQKh[:, par, :, :].bitcast(F32),
                                        ALU.subtract).then_inc(wqk_lo, 1)

            def wo_low(H, par):
                pool.wait_ge(wo_hi, H + 1)
                nc.gpsimd.tensor_tensor(WOl[:, par, :], WO3[:, :], WOh[:, par, :].bitcast(F32),
                                        ALU.subtract).then_inc(wo_lo, 1)

            def wv_low(I):
                pool.wait_ge(wv_hi, I + 1)
                nc.gpsimd.tensor_tensor(WVl[:, :, :], WV3[:, :, :], WVh[:, :, :].bitcast(F32),
                                        ALU.subtract).then_inc(wv_lo, 1)

            def values_low(I, n):
                m = 2 * (n % 4)
                pool.wait_ge(v_hi, 4 * I + n + 1)
                nc.gpsimd.tensor_tensor(V3l[:, m:m + 2, :], V3[:, n % 2, :, :],
                                        V3h[:, m:m + 2, :].bitcast(F32), ALU.subtract).then_inc(v_lo, 1)

            def scale(I, s):
                pool.wait_ge(p3_inv, 8 * I + s + 1)
                for tt in range(2):
                    nc.gpsimd.tensor_tensor(P3[:, s % 2, tt, 0:T + 1], P3[:, s % 2, tt, 0:T + 1],
                                            RI3[:, s % 2, tt:tt + 1].to_broadcast([P, T + 1]),
                                            ALU.mult).then_inc(p3_scaled, 1)

            def pair(I, case):
                final = isinstance(I, int) and I == 15
                for s in range(8):
                    scale(I, s)
                    for x in products(case, s):
                        if x[0] == "v":
                            values_low(I, x[1])
                    if s == 0 and not final:
                        qk_low(2 * I + 2, 0)
                    if s == 4 and not final:
                        qk_low(2 * I + 3, 1)
                    if s % 4 == 1:
                        wo_low(2 * I + s // 4, s // 4)
                    if s == 3 and not final:
                        wv_low(I + 1)

            qk_low(0, 0)
            wv_low(0)
            qk_low(1, 1)
            for a in range(2):
                values_low(8 * a, 0)
                attention_pairs(pool, a, pair)


def kernel(**inputs):
    import numpy as np
    import concourse.bacc as _bacc
    from concourse.bass_utils import run_bass_kernel_spmd as _run

    a = {k: np.asarray(v) for k, v in inputs.items()}

    def cols(v):
        return v.reshape(-1, P).T

    def wt(w):
        return w.reshape(C, P, -1).transpose(1, 0, 2).reshape(P, -1)

    def padded(w, shape):
        z = np.zeros(shape, np.float32)
        z[:w.shape[0], :w.shape[1]] = w
        return z

    def bias_columns(v):
        z = np.zeros((P, H3, 32), np.float32)
        for h in range(H3):
            z[:, h, h] = v[h]
        return z

    def rwkv_weights(p):
        w2 = np.zeros((P, 5, E), np.float32)
        for j in range(5):
            w2[32 * (j % 4):32 * (j % 4) + 32, j] = a[p + "maa_w2"][j]
        parts = [wt(padded(a[p + "maa_w1"], (E, 256))), w2.reshape(P, -1), wt(padded(a[p + "decay_w1"], (E, P))),
                 padded(a[p + "decay_w2"], (P, E))]
        parts += [wt(a[p + n].T) for n in ("Wk", "Wv", "Wr", "Wg", "Wo", "ffn_Wk", "ffn_Wr", "ffn_Wv")]
        return np.concatenate(parts, 1)

    def rwkv_vectors(p):
        parts = [cols(a[p + n]) for n in ("ln1_w", "ln1_b", "ln2_w", "ln2_b", "maa_x")]
        parts += [cols(a[p + "maa_stack"].reshape(-1))]
        parts += [cols(a[p + n]) for n in ("time_decay", "gn_w", "gn_b", "ffn_maa_k", "ffn_maa_r")]
        return np.concatenate(parts + [np.tile(a[p + "faaaa"], (B, 1))], 1)

    q = "L3_xattn_"
    head_of = np.arange(P)[:, None] // D1 == np.arange(HPC)[None, :]
    veca = [cols(a["L1_xattn_ln_gamma"]), cols(a["L1_xattn_ln_beta"]), np.tile(a["L1_xattn_gate"], (P, 1))]
    veca += [cols(a[q + n]) for n in ("ln1_scale", "ln1_offset", "ln2_scale", "ln2_offset", "ln_mlp_scale",
                                      "ln_mlp_offset", "b_fc1", "bq1", "bq2", "bk1", "bk2")]
    veca += [a[q + n].reshape(H3, D3).T for n in ("bias_k1", "bias_k2")]
    veca += [head_of.astype(np.float32)]
    same = (np.arange(P)[:, None] // S == np.arange(P)[None, :] // S).astype(np.float32) / S
    const = np.stack([np.eye(P, dtype=np.float32), np.eye(P, dtype=np.float32) - same, same], 1)
    ctx = a["ctx_2048"]
    prev = ctx[:, 0:2, :].reshape(B, 2, C, P).transpose(3, 1, 2, 0).reshape(P, 2, C * B)
    w3 = [np.concatenate([a[q + n + s].reshape(C, P, H3, D3).transpose(2, 1, 0, 3) for n in ("wq", "wk")]
                         + [a[q + "wo" + s].reshape(H3, P, C, P)], 2).reshape(H3, P, 3, E) for s in "12"]
    wv = [a[q + "wv" + s].reshape(C, P, H3 // 2, 2 * D3).transpose(2, 1, 0, 3) for s in "12"]
    arrays = {
        "x": a["x"], "ctx": ctx, "mask": a["mask_BxS2_bf1"].reshape(1, B * T).view(np.uint8),
        "prev": prev, "s0": ctx[:, 2:10, :].reshape(P, S * S), "const": const,
        "wrk": np.stack([rwkv_weights("L0_xattn_"), rwkv_weights("L2_xattn_")]),
        "vec": np.stack([rwkv_vectors("L0_xattn_"), rwkv_vectors("L2_xattn_")], 1),
        "veca": np.concatenate(veca, 1),
        "w1l": np.stack([wt(a["L1_xattn_" + n].T) for n in ("Wq", "Wk", "Wv", "Wo")], 1).reshape(P, 4, C, E),
        "w3": np.concatenate(w3),
        "wv": np.concatenate(wv),
        "rows": np.stack([a[q + "bo1"], a[q + "bo2"], a[q + "b_fc2"]]),
        "bv": np.stack([a[q + "bv1"], a[q + "bv2"]]).reshape(H3, 2 * D3),
        "biasv": np.stack([bias_columns(a[q + "bias_v" + s].reshape(H3, D3)) for s in "12"]),
        "fc1": a[q + "w_fc1"].reshape(C, P, F3).transpose(1, 0, 2),
        "fc2": a[q + "w_fc2"].reshape(FT, P, E).transpose(1, 0, 2),
    }
    nc = _bacc.Bacc("TRN2", target_bir_lowering=False, num_devices=1)
    args = []
    for name in arrays:
        arrays[name] = np.ascontiguousarray(arrays[name])
        args.append(nc.dram_tensor(f"in_{name}", arrays[name].shape, mybir.dt.from_np(arrays[name].dtype),
                                   kind="ExternalInput").ap())
    args.append(nc.dram_tensor("out_x", (B, T, E), F32, kind="ExternalOutput").ap())
    build_program(nc, *args)
    r = _run(nc, [{f"in_{k}": v for k, v in arrays.items()}], core_ids=[0])
    return r.results[0]["out_x"]
```

```python
from contextlib import ExitStack

import concourse.bass as bass
from concourse import mybir

F32 = mybir.dt.float32
F32R = mybir.dt.float32r
U8 = mybir.dt.uint8
ALU = mybir.AluOpType
ACT = mybir.ActivationFunctionType
AX_X = mybir.AxisListType.X

P = 128
B, T, E = 4, 256, 256
NTOK = B * T
C = E // P
TILES = NTOK // P
HALF = 512
S = 8
EPS = 1e-5
H1, D1 = 16, 16
HPC = P // D1
H3, D3 = 16, 128
KEYS = T + 2
F3 = 1024
FT = F3 // P

W1, W2, DW1, DW2 = 0, 2 * 256, 2 * 256 + 5 * 256, 2 * 256 + 5 * 256 + 2 * 128
WK, WV, WR, WG, WO, FK, FR, FV = (DW2 + 256 + 512 * i for i in range(8))
NW = FV + 512
LN1W, LN1B, LN2W, LN2B, MAAX, STACK, TD, GNW, GNB, FMK, FMR = 0, 2, 4, 6, 8, 10, 20, 22, 24, 26, 28
UCOL = 30
NV = UCOL + S
G1, B1, GATE, LN3, BFC1 = 0, 2, 4, 5, 17
BQ, BK, BIASK = (BFC1 + FT + 32 * i for i in range(3))
HMASK = BIASK + 32
NVA = HMASK + HPC
MOST_NEGATIVE = -3.0e38
MIX = [1, 0, 2, 3, 4]
QUARTERS = (0, 2, 1, 3)


def build_program(nc, x_in, ctx_in, mask_in, prev_in, s0_in, const_in, wrk_in, vec_in, veca_in,
                  w1l_in, w3_in, wv_in, rows_in, bv_in, biasv_in, fc1_in, fc2_in, out):
    with ExitStack() as stack:
        def sem(name):
            return stack.enter_context(nc.semaphore(name))

        def sb(name, shape, dt=F32, where=stack):
            return where.enter_context(nc.sbuf_tensor(name, shape, dt))

        X = sb("X", [P, TILES, E])
        XNT = sb("XNT", [P, TILES, E])
        STAT = sb("STAT", [P, TILES, 6])
        MV = sb("MV", [P, TILES, 2])
        VL = sb("VL", [P, TILES])
        VE = sb("VE", [P, TILES])
        CONST = sb("CONST", [P, 3, P])
        IDENT, CENTER, MEAN8 = CONST[:, 0, :], CONST[:, 1, :], CONST[:, 2, :]
        EPSC = sb("EPSC", [P, 1])
        VEC = sb("VEC", [P, 2, NV])
        VECA = sb("VECA", [P, NVA])
        PREV = sb("PREV", [P, 2, TILES])
        S0 = sb("S0", [P, S * S])
        CTh = sb("CTh", [P, C, NTOK], F32R)
        CTl = sb("CTl", [P, C, NTOK], F32R)
        with ExitStack() as scope:
            KV1 = sb("KV1", [P, 2, 2048], F32, scope)
        FC2S = sb("FC2S", [P, 2, FT, E], F32R)
        K1 = KV1[:, 0, :].rearrange("p (c t) -> p c t", c=C)
        V1 = KV1[:, 1, :].rearrange("p (m d) -> p m d", m=TILES)
        W1L = sb("W1L", [P, 4, C, E])
        BFC2 = sb("BFC2", [P, E])
        CF = sb("CF", [P, T])

        with ExitStack() as scope:
            AR = sb("AR", [P, 14 * 2048 + 16 + 2056], F32, scope)
            WRK = sb("WRK", [P, NW], F32, scope)
        with ExitStack() as scope:
            Q1h = sb("Q1h", [P, C, NTOK], F32R, scope)
            Q1l = sb("Q1l", [P, C, NTOK], F32R, scope)
            KMh = sb("KMh", [P, 2, NTOK], F32R, scope)
            KMl = sb("KMl", [P, 2, NTOK], F32R, scope)
            MU8 = sb("MU8", [P, B * T], U8, scope)
            MASKB = sb("MASKB", [P, B * T], F32, scope)
            P1R = sb("P1R", [P, 4 * 2 * T], F32, scope)
            PT1 = sb("PT1", [P, 2, 2, T], F32, scope)
            VM = sb("VM", [P, 2, TILES, P], F32, scope)
            ZV = sb("ZV", [P, TILES, D1], F32, scope)
            NM1 = sb("NM1", [P, 2, 2], F32, scope)
            NS1 = sb("NS1", [P, 2, 2], F32, scope)
            RS1 = sb("RS1", [P, 2, 2], F32, scope)
            RI1 = sb("RI1", [P, 2, 2], F32, scope)
            GT = sb("GT", [P, 1], F32, scope)
            CARRY = sb("CARRY", [P, 1], F32, scope)
        P1 = P1R[:, :].rearrange("p (n k t) -> p n k t", n=4, k=2)
        XT1 = P1R[:, :].rearrange("p (c t) -> p c t", c=C)
        AOT = XT1
        with ExitStack() as scope:
            WQK = sb("WQK", [P, 2, E], F32, scope)
            WV3 = sb("WV3", [P, C, 2 * D3], F32, scope)
            WQKh = sb("WQKh", [P, 2, 2, E], F32R, scope)
            Hh = sb("Hh", [P, C, NTOK], F32R, scope)
            C3h = sb("C3h", [P, 2, NTOK], F32R, scope)
            K3h = sb("K3h", [P, 2, B, KEYS], F32R, scope)
            K3l = sb("K3l", [P, 2, B, KEYS], F32R, scope)
            Q3h = sb("Q3h", [P, 2, NTOK], F32R, scope)
            Q3l = sb("Q3l", [P, 2, NTOK], F32R, scope)
            V3h = sb("V3h", [P, TILES, 2 * D3], F32R, scope)
            WQKl = sb("WQKl", [P, 2, 2, E], F32R, scope)
            WVh = sb("WVh", [P, C, 2 * D3], F32R, scope)
            WVl = sb("WVl", [P, C, 2 * D3], F32R, scope)
            Hl = sb("Hl", [P, C, NTOK], F32R, scope)
            WO3 = sb("WO3", [P, E], F32, scope)
            BV = sb("BV", [P, 2 * D3], F32, scope)
            HB = sb("HB", [P, 2, 3], F32, scope)
            WOh = sb("WOh", [P, 2, E], F32R, scope)
            WOl = sb("WOl", [P, 2, E], F32R, scope)
            V3 = sb("V3", [P, 2, 2, 2 * D3], F32, scope)
            V3l = sb("V3l", [P, TILES, 2 * D3], F32R, scope)
            P3 = sb("P3", [P, 2, 2, KEYS], F32, scope)
            PT3h = sb("PT3h", [P, 2, 2, T], F32R, scope)
            PT3l = sb("PT3l", [P, 2, 2, T], F32R, scope)
            C3l = sb("C3l", [P, 2, NTOK], F32R, scope)
            NM3 = sb("NM3", [P, 2, 2], F32, scope)
            NS3 = sb("NS3", [P, 2, 2], F32, scope)
            RS3 = sb("RS3", [P, 2, 2], F32, scope)
            RI3 = sb("RI3", [P, 2, 2], F32, scope)
            PB = sb("PB", [P, TILES, 32], F32, scope)
            PBT = sb("PBT", [32, NTOK], F32, scope)
            with ExitStack() as inner:
                HF = sb("HF", [P, C, NTOK], F32, inner)
            FC1l = sb("FC1l", [P, C, F3], F32R, scope)
            FC1h = sb("FC1h", [P, C, F3], F32R, scope)
        WOALL = KV1[:, :, :].rearrange("p k (h e) -> p (k h) e", e=E)
        AUX = W1L[:, :, :, :].rearrange("p w c e -> p (w c e)")
        BVD = AUX[:, 0:H3 * 32].rearrange("p (h k) -> p h k", h=H3)
        WAUX = [AUX[0:32, H3 * 32 + E * a:H3 * 32 + E * (a + 1)] for a in range(2)]
        with ExitStack() as scope:
            with ExitStack() as inner:
                HM3 = sb("HM3", [P, C, NTOK], F32, inner)
            HMl = sb("HMl", [P, C, NTOK], F32R, scope)
            HMh = sb("HMh", [P, C, NTOK], F32R, scope)
            with ExitStack() as inner:
                G3 = sb("G3", [P, FT, NTOK], F32, inner)
            G3l = sb("G3l", [P, FT, NTOK], F32R, scope)
            G3h = sb("G3h", [P, FT, NTOK], F32R, scope)
        FC1 = HF[:, :, :]
        FC2 = KV1[:, 0, :].rearrange("p (f e) -> p f e", f=FT)
        FC2l, FC2h = FC2S[:, 0, :, :], FC2S[:, 1, :, :]

        def mlp_weights(n):
            if n < 4:
                v = (slice(None), n // 2, slice((n % 2) * HALF, (n % 2 + 1) * HALF))
                return FC1[v], FC1h[v], FC1l[v]
            v = (slice(None), slice(2 * (n - 4), 2 * (n - 4) + 2), slice(None))
            return FC2[v], FC2h[v], FC2l[v]

        def slot(i):
            at = i * 2048 + (16 if i >= 7 else 0)
            return AR[:, at:at + 2048]

        def fm(i):
            return slot(i).rearrange("p (a t) -> p a t", a=8)

        XN = AR[:, 14 * 2048 + 16:14 * 2048 + 16 + 2056].rearrange("p (a t) -> p a t", a=8)
        SX = fm(1)
        X5 = [fm(2), fm(3), fm(4)]
        KT, VT, RT, WT = (fm(i) for i in (5, 6, 7, 8))
        KS, VS, RS, WS = (fm(i) for i in (9, 10, 11, 12))
        M1 = slot(11).rearrange("p (m t) -> p m t", m=2)
        DT = slot(13)[:, 0:NTOK]
        TH = fm(0)
        G2 = fm(13)
        RK, T1, GB = fm(4), fm(3), fm(3)
        AK = [fm(1), fm(14)]
        MK = [fm(8), fm(0)]
        SS = [AR[:, 5 * 2048 + 2056 * i:5 * 2048 + 2056 * (i + 1)].rearrange("p (d t) -> p d t", d=S)
              for i in (0, 1)]
        AS, ATT, SQ, SD, YT = (fm(i) for i in (4, 9, 10, 11, 12))
        XK, XR, KK, KK2, RR, FT1 = (fm(i) for i in (2, 3, 4, 5, 6, 7))
        CRAW = slot(9).rearrange("p (m d) -> p m d", m=TILES)
        AT = fm(2)
        XNC = V1

        banks = [stack.enter_context(nc.psum_tensor(f"bank{i}", [P, 512], F32)) for i in range(8)]

        ld_x0, ld_x1, ld_mixes, ld_c, ld_small, ld_wrk, ld_w1l, ld_mask = (sem(n) for n in (
            "ld_x0", "ld_x1", "ld_mixes", "ld_c", "ld_small", "ld_wrk", "ld_w1l", "ld_mask"))
        eps_set, root_table, gate_done = sem("eps_set"), sem("root_table"), sem("gate_done")
        ln_stats, ln_mv, ln_root, ln_inv, ln_rows = (sem(n) for n in ("ln_stats", "ln_mv", "ln_root", "ln_inv", "ln_rows"))
        turned = sem("turned")
        x_sum = sem("x_sum")
        ct_hi, ct_lo, at_ready, k1_proj, k1_out, v1_proj, v1_ready, mask_f, mask_b = (
            sem(n) for n in ("ct_hi", "ct_lo", "at_ready", "k1_proj", "k1_out", "v1_proj",
                             "v1_ready", "mask_f", "mask_b"))
        xn_ready, sx_first, sx_ready, xmix_ready, m1_ready, m1_tanh, mix_ready, mix_scaled, x5_ready = (
            sem(n) for n in ("xn_ready", "sx_first", "sx_ready", "xmix_ready", "m1_ready", "m1_tanh", "mix_ready",
                             "mix_scaled", "x5_ready"))
        proj_ready, proj_out, decay_e, gate_th, g_ready = (
            sem(n) for n in ("proj_ready", "proj_out", "decay_e", "gate_th", "g_ready"))
        moved = {n: sem(f"moved_{n}") for n in ("w", "k", "v", "r", "a0", "a1")}
        coef_ru, coef_rk, coef_sum, coef_ready, bonus_ready, state0, outer_dve, outer_pool, scanned, read_out, summed = (
            sem(n) for n in ("coef_ru", "coef_rk", "coef_sum", "coef_ready", "bonus_ready", "state0", "outer_dve", "outer_pool",
                             "scanned", "read_out", "summed"))
        att_out, centered, squared, gvar, glog, ginv, gate_offset, gscaled, y_ready, wo_ready = (
            sem(n) for n in ("att_out", "centered", "squared", "gvar", "glog", "ginv", "gate_offset", "gscaled", "y_ready",
                             "wo_ready"))
        xkr_ready, fk_ready, fk_pos, fk_sq, fr_ready, fr_th, fv_ready, fv_mul = (
            sem(n) for n in ("xkr_ready", "fk_ready", "fk_pos", "fk_sq", "fr_ready", "fr_th", "fv_ready",
                             "fv_mul"))
        xt_ready, q1_proj, q1_hi, q1_lo, km_hi, km_lo, vm_clear, vm_ready = (
            sem(n) for n in ("xt_ready", "q1_proj", "q1_hi", "q1_lo", "km_hi", "km_lo", "vm_clear", "vm_ready"))
        sc_ready, sc_masked, sc_max, p1_ready, p1_inv, p1_scaled, p1_turned, pt_out, pv_done = (
            sem(n) for n in ("sc_ready", "sc_masked", "sc_max", "p1_ready", "p1_inv", "p1_scaled", "p1_turned",
                             "pt_out", "pv_done"))
        ao_turned, out1_ready = sem("ao_turned"), sem("out1_ready")
        ld_wqk, ld_wo3, ld_wv, ld_bv = (sem(n) for n in ("ld_wqk", "ld_wo3", "ld_wv", "ld_bv"))
        ld_wo, ld_aux, ld_bo, ld_fc1, ld_fc2, ld_bfc2 = (
            sem(n) for n in ("ld_wo", "ld_aux", "ld_bo", "ld_fc1", "ld_fc2", "ld_bfc2"))
        hb_ready = sem("hb_ready")
        h_rows, h_hi, h_lo, wqk_hi, wqk_lo, wo_hi, wo_lo, wv_hi, wv_lo, key_hi, key_lo = (
            sem(n) for n in ("h_rows", "h_hi", "h_lo", "wqk_hi", "wqk_lo", "wo_hi", "wo_lo", "wv_hi", "wv_lo",
                             "key_hi", "key_lo"))
        qk_full, qk_hi, qk_lo, v_full, v_added, v_hi, v_lo, o_full, o_added = (
            sem(n) for n in ("qk_full", "qk_hi", "qk_lo", "v_full", "v_added", "v_hi", "v_lo", "o_full",
                             "o_added"))
        s3_ready, s3_max, s3_shift, p3_ready, p3_inv, p3_scaled, p3_bias, p3_turned, pt3_hi, pt3_lo = (
            sem(n) for n in ("s3_ready", "s3_max", "s3_shift", "p3_ready", "p3_inv", "p3_scaled", "p3_bias",
                             "p3_turned", "pt3_hi", "pt3_lo"))
        c3_ready, c3_hi, c3_lo = sem("c3_ready"), sem("c3_hi"), sem("c3_lo")
        pb_clear, pb_one, aux_ready, waux_out, pb_turned, pbt_out = (
            sem(n) for n in ("pb_clear", "pb_one", "aux_ready", "waux_out", "pb_turned", "pbt_out"))
        mlp_hi, mlp_lo, hm_ready, hm_hi, hm_lo, fc1_ready, gelu_out, g3_hi, g3_lo, fc2_ready = (
            sem(n) for n in ("mlp_hi", "mlp_lo", "hm_ready", "hm_hi", "hm_lo", "fc1_ready", "gelu_out", "g3_hi",
                             "g3_lo", "fc2_ready"))
        stored = sem("stored")

        block = stack.enter_context(nc.Block())

        def lnw(li, col, c):
            return VEC[:, li, col + c:col + c + 1]

        def ln_moments(dve, n, src, pairs):
            tiles = [2 * pair + k for pair in pairs for k in range(2)]
            for m in tiles:
                nc.vector.bn_stats(STAT[:, m, :], src[:, m, :]).then_inc(ln_stats, 1)
            for m in tiles:
                dve.wait_ge(ln_stats, TILES * n + m + 1)
                nc.vector.bn_aggr(MV[:, m, :], STAT[:, m, :]).then_inc(ln_mv, 1)

        def ln_normalise(dve, n, src, pairs, dst=None):
            dst = XNT if dst is None else dst
            for pair in pairs:
                t = slice(2 * pair, 2 * pair + 2)
                dve.wait_ge(ln_root, 4 * n + pair + 1)
                nc.vector.reciprocal(VE[:, t], VL[:, t]).then_inc(ln_inv, 1)
            for pair in pairs:
                dve.wait_ge(ln_inv, 4 * n + pair + 1)
                for m in (2 * pair, 2 * pair + 1):
                    nc.vector.tensor_scalar(dst[:, m, :], src[:, m, :], MV[:, m, 0:1], VE[:, m:m + 1],
                                            ALU.subtract, ALU.mult).then_inc(ln_rows, 1)

        def ln_dve(dve, n, src, pairs):
            ln_moments(dve, n, src, pairs)
            ln_normalise(dve, n, src, pairs)

        def ln_pair(dve, n, pair, x_count):
            dve.wait_ge(x_sum, x_count)
            ln_moments(dve, n, X, [pair])
            if pair % 2:
                ln_normalise(dve, n, X, [pair - 1, pair])

        def ln_act(act, n, pairs=(0, 1, 2, 3)):
            for pair in pairs:
                t = slice(2 * pair, 2 * pair + 2)
                act.wait_ge(ln_mv, TILES * n + 2 * pair + 2)
                nc.scalar.activation(VL[:, t], MV[:, t, 1], ACT.Sqrt, bias=EPSC[:, 0:1]).then_inc(ln_root, 1)

        def turn(pe, src, c, hf, where):
            for k in range(4):
                last = nc.tensor.transpose(banks[where[2 * c + hf]][:, k * P:(k + 1) * P],
                                           src[:, 4 * hf + k, c * P:(c + 1) * P], IDENT)
            last.then_inc(turned, 1)

        def ln_turn(pe, n, where, halves=(0, 1)):
            for hf in halves:
                pe.wait_ge(ln_rows, TILES * n + 4 * hf + 4)
                for c in range(C):
                    turn(pe, XNT, c, hf, where)

        LOW, HIGH, SPARE = (0, 1, 2, 3), (4, 5, 6, 7), (0, 1, 2, 4)
        TURN_ORDER = [(c, hf) for hf in range(2) for c in range(C)]

        def g_par(j):
            return j % 2

        PRODUCT_BANKS = (3, 5, 6, 7)
        PROJ = [[("v", 1), ("qk", 4)], [("v", 2), ("qk", 5)], [("v", 3), ("qk", 6)], [("qk", 7)], [("qk", 8)],
                [("qk", 9)], [("qk", 10)], [("v", 4), ("qk", 11)]]
        PROLOGUE = [("qk", 1), ("qk", 3), ("v", 0), ("qk", 0), ("qk", 2)]
        PLACE = {1: 0, 3: 1, 0: 2, 2: 3}

        def slots(case):
            return [[x for x in PROJ[s] if case != "last" or s < 4]
                    + ([("pb", s - 6)] if case == "last" and s >= 6 else [])
                    + ([("o", s - 3)] if case != "first" or s >= 3 else []) for s in range(8)]

        def flat(case):
            return [x for y in slots(case) for x in y]

        def earlier(line):
            step = {"qk": 8, "v": 4, "o": 8}
            return [(k, n - step[k]) for k, n in line]

        def products(case, s):
            if case == "prologue":
                at, before, line = 0, [None] * 4, PROLOGUE
                todo = PROLOGUE
            elif case == "end":
                at, before = len(PROLOGUE + flat("first") + flat("last")), flat("last")[-4:]
                line = todo = [("pb", 2), ("o", 5), ("pb", 3), ("o", 6), ("o", 7)]
            else:
                at = len(PROLOGUE) + (0 if case == "first" else len(flat("first")))
                before = PROLOGUE[-4:] if case == "first" else earlier(flat("steady")[-4:])
                line, todo = flat(case), slots(case)[s]
                k = sum(len(y) for y in slots(case)[:s])
                return [(*x, PRODUCT_BANKS[(at + k + m) % 4], (before + line)[k + m]) for m, x in enumerate(todo)]
            return [(*x, PRODUCT_BANKS[(at + m) % 4], (before + line)[m]) for m, x in enumerate(todo)]

        def wait_taken(eng, I, product):
            if product is not None:
                kind, n = product
                if kind == "pb":
                    eng.wait_ge(pbt_out, 4 * (I // 8) + n + 1)
                elif kind == "qk":
                    eng.wait_ge(qk_lo, 8 * I + n + 1)
                elif kind == "v":
                    eng.wait_ge(v_added, 4 * I + n + 1)
                else:
                    eng.wait_ge(o_added, 8 * I + n + 1)

        def attention_pairs(eng, a, pair):
            pair(8 * a, "first")
            with eng.Fori(8 * a + 1, 8 * a + 7) as i:
                pair(i, "steady")
            pair(8 * a + 7, "last")

        def lagged(case, s, lag):
            return not (case == "first" and s < lag)

        @block.sync
        def _(sp):
            for hf, loaded in enumerate((ld_x0, ld_x1)):
                sp.dma_start(X[:, 4 * hf:4 * hf + 4, :],
                             x_in.rearrange("b (h p) d -> p (b h) d", p=P)[:, 4 * hf:4 * hf + 4, :]).then_inc(loaded, 16)
            for dst, src in ((CONST[:, :, :], const_in), (VEC[:, :, :], vec_in), (VECA[:, :], veca_in),
                             (PREV[:, :, :], prev_in), (S0[:, :], s0_in)):
                sp.dma_start(dst, src).then_inc(ld_small, 16)
            sp.dma_start(WRK[:, 0:DW1], wrk_in[0, :, 0:DW1]).then_inc(ld_mixes, 16)
            sp.dma_start(CRAW, ctx_in.rearrange("b (h p) d -> p (b h) d", p=P)).then_inc(ld_c, 16)
            sp.dma_start(WRK[:, DW1:NW], wrk_in[0, :, DW1:NW]).then_inc(ld_wrk, 16)
            sp.dma_start(W1L[:, :, :, :], w1l_in).then_inc(ld_w1l, 16)

            def to_scan(src, dst, name, ready, n0):
                for hf in range(2):
                    sp.wait_ge(ready, n0 + 2 * hf + 2)
                    for b in (2 * hf, 2 * hf + 1):
                        for c in range(C):
                            p0 = 32 * b + 16 * c
                            sp.dma_start(dst[p0:p0 + 16, :, :], src[:, 4 * c + b, :]).then_inc(moved[name], 16)

            def rwkv_moves(li):
                to_scan(WT, WS, "w", decay_e, 4 * li)
                if li == 0:
                    sp.wait_ge(ln_rows, 2 * TILES)
                for n, (src, dst, name) in enumerate(((KT, KS, "k"), (VT, VS, "v"), (RT, RS, "r"))):
                    to_scan(src, dst, name, proj_out, 18 * li + 6 + 4 * n)
                if li == 1:
                    sp.wait_ge(aux_ready, 1)
                    load_aux(1)
                    load_output_bias(0)
                sp.wait_ge(att_out, 4 * (li + 1))
                for b in range(B):
                    for c in range(C):
                        p0 = 32 * b + 16 * c
                        sp.dma_start(ATT[:, 4 * c + b, :], AS[p0:p0 + 16, :, :]).then_inc(moved[f"a{b // 2}"], 16)

            rwkv_moves(0)
            sp.wait_ge(x_sum, 8)
            sp.dma_start(MU8[:, :], mask_in.to_broadcast([P, B * T])).then_inc(ld_mask, 16)
            sp.dma_start(WRK[:, :], wrk_in[1]).then_inc(ld_wrk, 16)
            def load_aux(a):
                sp.dma_start(WOALL, w3_in[H3 * a:H3 * (a + 1), :, 2, :].rearrange("h p e -> p h e")).then_inc(ld_wo, 16)
                sp.dma_start(BVD, biasv_in[a]).then_inc(ld_aux, 16)

            def load_output_bias(a):
                sp.wait_ge(waux_out, a + 1)
                sp.dma_start(WAUX[a][H3:H3 + 1, :], rows_in[a:a + 1, :]).then_inc(ld_bo, 16)

            sp.wait_ge(x_sum, 12)
            load_aux(0)
            rwkv_moves(1)

            def load_qk(H):
                sp.dma_start(WQK[:, :, :], w3_in[bass.ds(H, 1), :, 0:2, :].rearrange("o p w e -> p (o w) e")
                             ).then_inc(ld_wqk, 16)

            def load_wo(H):
                sp.dma_start(WO3[:, :], w3_in[bass.ds(H, 1), :, 2, :].rearrange("o p e -> p (o e)")).then_inc(ld_wo3, 16)

            def load_wv(I):
                sp.dma_start(WV3[:, :, :], wv_in[bass.ds(I, 1), :, :, :].rearrange("o p c e -> p (o c) e")
                             ).then_inc(ld_wv, 16)

            def load_bv(I):
                sp.dma_start(BV[:, :], bv_in[bass.ds(I, 1), :].to_broadcast([P, 2 * D3])).then_inc(ld_bv, 16)

            def pair_loads(I):
                sp.wait_ge(wqk_lo, 2 * I + 3)
                load_qk(2 * I + 3)
                sp.wait_ge(wo_lo, 2 * I + 1)
                load_wo(2 * I + 1)
                sp.wait_ge(v_added, 4 * I + 4)
                load_bv(I + 1)
                sp.wait_ge(wv_lo, I + 2)
                load_wv(I + 2)
                sp.wait_ge(wqk_lo, 2 * I + 4)
                load_qk(2 * I + 4)
                sp.wait_ge(wo_lo, 2 * I + 2)
                load_wo(2 * I + 2)

            sp.wait_ge(x_sum, 16)
            load_qk(0)
            load_wv(0)
            load_bv(0)
            load_wo(0)
            sp.wait_ge(wqk_lo, 1)
            load_qk(1)
            sp.wait_ge(wv_lo, 1)
            load_wv(1)
            load_output_bias(1)
            sp.dma_start(FC2, fc2_in).then_inc(ld_fc2, 16)
            sp.dma_start(BFC2[:, :], rows_in[2:3, :].to_broadcast([P, E])).then_inc(ld_bfc2, 16)
            sp.wait_ge(wqk_lo, 2)
            load_qk(2)
            with sp.Fori(0, 14) as i:
                pair_loads(i)
            sp.wait_ge(h_lo, 8)
            sp.dma_start(FC1, fc1_in).then_inc(ld_fc1, 16)
            sp.wait_ge(wqk_lo, 31)
            load_qk(31)
            sp.wait_ge(wo_lo, 29)
            load_wo(29)
            sp.wait_ge(v_added, 60)
            load_bv(15)
            sp.wait_ge(wo_lo, 30)
            load_wo(30)
            sp.wait_ge(wo_lo, 31)
            load_wo(31)
            for pair in range(4):
                sp.wait_ge(x_sum, 22 + pair)
                sp.dma_start(out.rearrange("b (h p) d -> p (b h) d", p=P)[:, 2 * pair:2 * pair + 2, :],
                             X[:, 2 * pair:2 * pair + 2, :]).then_inc(stored, 16)
            sp.wait_ge(stored, 64)

        @block.tensor
        def _(pe):
            def proj(bank, w, col, rhs, hf, m=0, stride=E):
                for c in range(C):
                    last = nc.tensor.matmul(banks[bank][:, :], w[:, col + stride * c + P * m:col + stride * c + P * m + P],
                                            rhs[:, 4 * c + 2 * hf:4 * c + 2 * hf + 2, :], start=(c == 0),
                                            stop=(c == C - 1))
                return last

            def rows(bank, w, rhs, pair, part=None):
                for k in range(2):
                    m = 2 * pair + k
                    for c in range(C):
                        last = nc.tensor.matmul(banks[bank][:, k * E:(k + 1) * E],
                                                rhs[:, 4 * c + m // 2, (m % 2) * P:(m % 2) * P + P],
                                                w[:, c * E:(c + 1) * E],
                                                start=(c == 0 if part is None else part + k + c == 0),
                                                stop=(c == C - 1 and part != 0),
                                                skip_group_check=part is not None)
                return last

            def context():
                pe.wait_ge(ld_c, 16)
                for c, hf in TURN_ORDER:
                    turn(pe, CRAW, c, hf, HIGH)

            def context_rows():
                pe.wait_ge(ln_rows, 2 * TILES)
                for c, hf in TURN_ORDER:
                    turn(pe, XNC, c, hf, LOW)

            def audio_keys(q):
                if q == 0:
                    pe.wait_ge(ld_w1l, 16)
                pe.wait_ge(at_ready, 4)
                proj(4 + q, W1L[:, 1, :, :].rearrange("p c e -> p (c e)"), 0, AT, q % 2, q // 2).then_inc(k1_proj, 1)

            def audio_values(pair):
                pe.wait_ge(k1_out, pair + 1)
                rows(4 + pair, W1L[:, 2, :, :].rearrange("p c e -> p (c e)"), AT, pair).then_inc(v1_proj, 1)

            def bias_products(a, bank):
                pe.wait_ge(ld_wo, 16 * (a + 1))
                pe.wait_ge(ld_aux, 16 * (a + 1))
                for h in range(H3):
                    last = nc.tensor.matmul(banks[bank][0:32, 0:E], BVD[:, h, :], WOALL[:, h, :], start=(h == 0),
                                            stop=(h == H3 - 1))
                last.then_inc(aux_ready, 1)

            def rwkv(li, lns, where):
                if li == 0:
                    pe.wait_ge(ld_small, 80)
                ln_turn(pe, lns[0], where)
                if li == 0:
                    pe.wait_ge(ld_mixes, 16)
                else:
                    pe.wait_ge(ld_wrk, 32)
                for i, q in enumerate(QUARTERS):
                    pe.wait_ge(xmix_ready, 4 * li + 2 * (q % 2) + 2)
                    proj(where[q], WRK, W1, X5[2], q % 2, q // 2).then_inc(m1_ready, 1)

                def mix(n):
                    j = MIX[n]
                    for i, q in enumerate(QUARTERS):
                        c, hf = q // 2, q % 2
                        if n:
                            pe.wait_ge(mix_scaled, 20 * li + 4 * n + i - 3)
                        else:
                            pe.wait_ge(m1_tanh, 4 * li + 2 * hf + 2)
                        nc.tensor.matmul(banks[q][:, :], WRK[:, W2 + 256 * j + P * c:W2 + 256 * j + P * c + P],
                                         M1[:, j // 4, hf * HALF:(hf + 1) * HALF], start=True,
                                         stop=True).then_inc(mix_ready, 1)

                def project(n, col):
                    for i, q in enumerate(QUARTERS):
                        pe.wait_ge(x5_ready, 20 * li + 4 * n + 2 * (q % 2) + 2)
                        if n == 1:
                            pe.wait_ge(decay_e, 4 * li + i + 1)
                        else:
                            pe.wait_ge(proj_out, 18 * li + 2 + 4 * (n - 1) + i + 1)
                        proj(4 + q, WRK, col, X5[n % 3], q % 2, q // 2).then_inc(proj_ready, 1)

                mix(0)
                if li == 0:
                    context()
                mix(1)
                if li == 0:
                    pe.wait_ge(ld_wrk, 16)
                    pe.wait_ge(ct_lo, 4)
                for hf in range(2):
                    pe.wait_ge(x5_ready, 20 * li + 2 * hf + 2)
                    proj(4 + hf, WRK, DW1, X5[0], hf, 0, P).then_inc(proj_ready, 1)
                mix(2)
                pe.wait_ge(proj_out, 18 * li + 2)
                for q in QUARTERS:
                    c, hf = q // 2, q % 2
                    nc.tensor.matmul(banks[4 + q][:, :], WRK[:, DW2 + P * c:DW2 + P * c + P],
                                     DT[:, hf * HALF:(hf + 1) * HALF], start=True, stop=True).then_inc(proj_ready, 1)
                project(1, WK)
                mix(3)
                project(2, WV)
                mix(4)
                project(3, WR)
                project(4, WG)
                if li == 1:
                    bias_products(0, 3)
                if li == 0:
                    context_rows()
                    for q in range(4):
                        if q == 0:
                            pe.wait_ge(g_ready, 4)
                        audio_keys(q)
                for n, k in enumerate((0, 1, 2, 3, 4, 5, "bonus", 6, 7)):
                    if k == "bonus":
                        pe.wait_ge(bonus_ready, li + 1)
                        src = T1
                    else:
                        pe.wait_ge(read_out, 8 * li + k + 1)
                        src = MK[k % 2]
                    for q in range(4):
                        if li == 1 and n == 0 and q == 3:
                            pe.wait_ge(waux_out, 1)
                        last = nc.tensor.matmul(banks[q][:, :], IDENT, src[:, 2 * q:2 * q + 2, :],
                                                start=(n == 0), stop=(n == 8), skip_group_check=True)
                    last.then_inc(summed, 1)
                    if k == 1:
                        pe.wait_ge(g_ready, 4 * (li + 1))
                        if li == 0:
                            pe.wait_ge(k1_out, 1)
                        pe.wait_ge(coef_rk, li + 1)
                        for kk in range(S):
                            last = nc.tensor.matmul(banks[4][:, 0:T], IDENT, RK[:, kk, :], start=(kk == 0),
                                                    stop=(kk == S - 1))
                        last.then_inc(coef_sum, 1)
                if li == 0:
                    pe.wait_ge(coef_ready, 1)
                    for pair in range(4):
                        audio_values(pair)
                    pe.wait_ge(v1_ready, 4)
                if li == 1:
                    bias_products(1, 7)
                for q in QUARTERS:
                    c, hf = q // 2, q % 2
                    if c == 0:
                        pe.wait_ge(moved[f"a{hf}"], 64 * (li + 1))
                    if q == 3 and li == 1:
                        pe.wait_ge(waux_out, 2)
                    nc.tensor.matmul(banks[4 + q][:, :], CENTER, ATT[:, 4 * c + 2 * hf:4 * c + 2 * hf + 2, :],
                                     start=True, stop=True).then_inc(centered, 1)
                for i, q in enumerate(QUARTERS):
                    c, hf = q // 2, q % 2
                    pe.wait_ge(squared, 4 * li + i + 1)
                    pe.wait_ge(gscaled, 4 * li + i + 1)
                    nc.tensor.matmul(banks[4 + q][:, :], MEAN8, SQ[:, 4 * c + 2 * hf:4 * c + 2 * hf + 2, :],
                                     start=True, stop=True).then_inc(gvar, 1)
                for part, pair in ((0, 0), (0, 1), (0, 2), (1, 0), (1, 1), (0, 3), (1, 2), (1, 3)):
                    if part == 0:
                        pe.wait_ge(gate_offset, 4 * li + 2 * (pair // 2) + 2)
                        rows(QUARTERS[pair], WRK[:, WO:WO + 512], GB, pair, part=0)
                        continue
                    pe.wait_ge(y_ready, 4 * li + 2 * (pair // 2) + 2)
                    rows(QUARTERS[pair], WRK[:, WO:WO + 512], YT, pair, part=1).then_inc(wo_ready, 1)
                ln_turn(pe, lns[1], HIGH)
                for q in QUARTERS:
                    pe.wait_ge(xkr_ready, 8 * li + 2 * (q % 2) + 2)
                    if q < 2:
                        pe.wait_ge(xn_ready, 10 * li + 8 + 2 * q)
                    proj(4 + q, WRK, FK, XK, q % 2, q // 2).then_inc(fk_ready, 1)
                for what, pair in (("r", 0), ("v", 0), ("r", 1), ("r", 2), ("v", 1), ("r", 3), ("v", 2), ("v", 3)):
                    if what == "r":
                        pe.wait_ge(xkr_ready, 8 * li + 4 + 2 * (pair // 2) + 2)
                        rows(pair, WRK[:, FR:FR + 512], XR, pair).then_inc(fr_ready, 1)
                    else:
                        pe.wait_ge(fk_pos, 4 * (li + 1))
                        pe.wait_ge(fk_sq, 4 * (li + 1))
                        rows(4 + pair, WRK[:, FV:FV + 512], KK2, pair).then_inc(fv_ready, 1)

            def unit_scores(i, j, c):
                g, h, b = 8 * i + j, 2 * i + j // 4, j % 4
                if b in (0, 2):
                    pe.wait_ge(km_lo, 2 * h + 1 + b // 2)
                if not (isinstance(i, int) and g < 2):
                    pe.wait_ge(sc_max, g - 1)
                for tt in range(2):
                    qs = slice((2 * b + tt) * P, (2 * b + tt) * P + P)
                    ks = slice(b * T, (b + 1) * T)
                    for n, (q, k) in enumerate(((Q1h, KMh), (Q1h, KMl), (Q1l, KMh))):
                        last = nc.tensor.matmul(banks[g_par(j)][:, tt * T:(tt + 1) * T], q[:, c, qs],
                                                k[:, (j // 4) % 2, ks], start=(n == 0), stop=(n == 2))
                last.then_inc(sc_ready, 1)

            def unit_turn(i, j):
                g = 8 * i + j
                pe.wait_ge(p1_scaled, g + 1)
                if not (isinstance(g, int) and g < 2):
                    pe.wait_ge(pt_out, g - 1)
                for ss in range(2):
                    for tt in range(2):
                        last = nc.tensor.transpose(banks[2 + g_par(j)][:, ss * T + tt * P:ss * T + (tt + 1) * P],
                                                   P1[:, j % 4, tt, ss * P:(ss + 1) * P], IDENT)
                last.then_inc(p1_turned, 1)

            def unit_values(i, j, c):
                g, h, b = 8 * i + j, 2 * i + j // 4, j % 4
                first = isinstance(h, int) and h % HPC == 0
                if b == 0:
                    pe.wait_ge(vm_ready, 2 * h + 2)
                pe.wait_ge(pt_out, g + 1)
                for ss in range(2):
                    last = nc.tensor.matmul(banks[4 + 2 * c + b // 2][:, (b % 2) * T:(b % 2 + 1) * T],
                                            VM[:, (j // 4) % 2, 2 * b + ss, :],
                                            PT1[:, g_par(j), ss, :], start=(first and b % 2 == 0 and ss == 0), stop=(ss == 1),
                                            skip_group_check=True)
                last.then_inc(pv_done, 1)

            def audio():
                pe.wait_ge(fr_th, 4)
                for c, hf in TURN_ORDER:
                    pe.wait_ge(x_sum, 6 + 2 * hf)
                    turn(pe, X, c, hf, LOW)
                pe.wait_ge(xt_ready, 4)
                for q in range(4):
                    proj(4 + q, W1L[:, 0, :, :].rearrange("p c e -> p (c e)"), 0,
                         XT1[:, :, :].rearrange("p c (b t) -> p (c b) t", b=B), q % 2, q // 2).then_inc(q1_proj, 1)
                pe.wait_ge(q1_lo, 4)

                def body(i, c):
                    c_before = 0 if isinstance(i, int) and i == 4 else c
                    for j in range(8):
                        unit_scores(i, j, c)
                        if not (isinstance(i, int) and 8 * i + j < 3):
                            unit_turn(i, j - 3)
                        if not (isinstance(i, int) and 8 * i + j < 4):
                            unit_values(i, j - 4, c_before if j < 4 else c)

                for c in range(C):
                    body(4 * c, c)
                    with pe.Fori(4 * c + 1, 4 * c + 4) as i:
                        body(i, c)
                for j in (-3, -2, -1):
                    unit_turn(8, j)
                    unit_values(8, j - 1, 1)
                unit_values(8, -1, 1)
                pe.wait_ge(ao_turned, 4)
                for pair in range(4):
                    rows(pair, W1L[:, 3, :, :].rearrange("p c e -> p (c e)"),
                         AOT[:, :, :].rearrange("p c (b t) -> p (c b) t", b=B), pair).then_inc(out1_ready, 1)

            rwkv(0, (0, 2), LOW)
            audio()
            rwkv(1, (3, 4), HIGH)

            def three(out_, lh, ll, rh, rl, first, last):
                nc.tensor.matmul(out_, lh, rh, start=first, stop=False)
                nc.tensor.matmul(out_, lh, rl, start=False, stop=False)
                return nc.tensor.matmul(out_, ll, rh, start=False, stop=last)

            def product(I, kind, n, bank, before, prologue=False):
                wait_taken(pe, I, before)
                if kind == "pb":
                    pe.wait_ge(p3_bias, 8 * I + 5 + n)
                    for k in range(2):
                        last = nc.tensor.transpose(banks[bank][0:32, k * P:(k + 1) * P], PB[:, 2 * n + k, :], IDENT)
                    last.then_inc(pb_turned, 1)
                elif kind == "qk":
                    pr, hf, w = (n // 4) % 2, (n // 2) % 2, n % 2
                    pe.wait_ge(wqk_lo, 2 * I + n // 4 + 1)
                    rh, rl = ((Hh, Hl), (CTh, CTl))[w]
                    for c in range(C):
                        cs, ts = slice(c * D3, (c + 1) * D3), slice(hf * HALF, (hf + 1) * HALF)
                        last = three(banks[bank][:, :], WQKh[:, pr, w, cs], WQKl[:, pr, w, cs], rh[:, c, ts],
                                     rl[:, c, ts], c == 0, c == C - 1)
                    last.then_inc(qk_full, 1)
                elif kind == "v":
                    pe.wait_ge(wv_lo, I + n // 4 + 1)
                    for k in range(2):
                        for c in range(C):
                            ts = slice((2 * (n % 4) + k) * P, (2 * (n % 4) + k + 1) * P)
                            last = three(banks[bank][:, k * 2 * D3:(k + 1) * 2 * D3], CTh[:, c, ts], CTl[:, c, ts],
                                         WVh[:, c, :], WVl[:, c, :], c == 0, c == C - 1)
                    last.then_inc(v_full, 1)
                else:
                    pr = (n // 4) % 2
                    pe.wait_ge(c3_lo, 8 * I + n + 1)
                    pe.wait_ge(wo_lo, 2 * I + n // 4 + 1)
                    a = I // 8 if isinstance(I, int) else 0
                    ends = isinstance(I, int) and I % 8 == 7 and n >= 4
                    if ends:
                        pe.wait_ge(pbt_out, 4 * a + n - 3)
                        pe.wait_ge(ld_bo, 32)
                    for tt in range(2):
                        ts = slice((2 * (n % 4) + tt) * P, (2 * (n % 4) + tt + 1) * P)
                        last = three(banks[bank][:, tt * E:(tt + 1) * E], C3h[:, pr, ts], C3l[:, pr, ts],
                                     WOh[:, pr, :], WOl[:, pr, :], True, not ends)
                        if ends:
                            last = nc.tensor.matmul(banks[bank][:, tt * E:(tt + 1) * E], PBT[0:32, ts], WAUX[a],
                                                    start=False, stop=True)
                    last.then_inc(o_full, 1)

            def scores3(I, s):
                par, b, G = s // 4, s % 4, 8 * I + s
                first = isinstance(I, int) and I % 8 == 0 and par == 0
                pe.wait_ge(qk_lo, 8 * I + 4 * par + (b // 2 + 3 if first else 2 * (b // 2) + 2))
                pe.wait_ge(key_lo, 2 * I + par + 1)
                for tt in range(2):
                    if not (isinstance(G, int) and G < 1):
                        pe.wait_ge(p3_ready, 2 * G - 1 + tt)
                    ts = slice((2 * b + tt) * P, (2 * b + tt + 1) * P)
                    three(banks[tt][:, 0:KEYS], Q3h[:, par, ts], Q3l[:, par, ts], K3h[:, par, b, :],
                          K3l[:, par, b, :], True, True).then_inc(s3_ready, 1)

            def turn3(I, s):
                G = 8 * I + s
                pe.wait_ge(p3_scaled, 2 * G + 2)
                if not (isinstance(G, int) and G < 1):
                    pe.wait_ge(pt3_lo, G)
                for ss in range(2):
                    for tt in range(2):
                        last = nc.tensor.transpose(banks[2][:, ss * T + tt * P:ss * T + (tt + 1) * P],
                                                   P3[:, s % 2, tt, ss * P:(ss + 1) * P], IDENT)
                last.then_inc(p3_turned, 1)

            def values3(I, s):
                G, b, ds_ = 8 * I + s, s % 4, slice((s // 4 % 2) * D3, (s // 4 % 2 + 1) * D3)
                pe.wait_ge(pt3_lo, G + 1)
                pe.wait_ge(v_lo, 4 * I + (b + 1 if s >= 0 else b - 3))
                if not (isinstance(G, int) and G < 1):
                    pe.wait_ge(c3_lo, G)
                for ss in range(2):
                    m = 2 * b + ss
                    last = three(banks[4][:, 0:T], V3h[:, m, ds_], V3l[:, m, ds_],
                                 PT3h[:, s % 2, ss, :], PT3l[:, s % 2, ss, :], ss == 0, ss == 1)
                last.then_inc(c3_ready, 1)

            def pair(I, case):
                for s in range(8):
                    todo = products(case, s)
                    proj_ = [x for x in todo if x[0] in ("qk", "v")]
                    scores3(I, s)
                    if proj_:
                        product(I, *proj_[0])
                    if lagged(case, s, 1):
                        turn3(I, s - 1)
                    for x in proj_[1:]:
                        product(I, *x)
                    if lagged(case, s, 2):
                        values3(I, s - 2)
                    for x in todo:
                        if x[0] in ("pb", "o"):
                            product(I, *x)

            for a in range(2):
                first = products("prologue", 0)
                if a == 0:
                    pe.wait_ge(fr_th, 8)
                ln_turn(pe, 5 + a, SPARE, [0])
                if a:
                    pe.wait_ge(o_added, 64)
                else:
                    pe.wait_ge(fv_mul, 6)
                for x in first[0:2]:
                    product(8 * a, *x)
                if a == 0:
                    pe.wait_ge(fv_mul, 8)
                product(8 * a, *first[2])
                ln_turn(pe, 5 + a, SPARE, [1])
                for hf, x in enumerate(first[3:]):
                    pe.wait_ge(h_lo, 4 * a + 2 * hf + 2)
                    product(8 * a, *x)
                attention_pairs(pe, a, pair)
                I, ends = 8 * a + 7, products("end", 0)
                turn3(I, 7)
                product(I, *ends[0])
                values3(I, 6)
                product(I, *ends[1])
                product(I, *ends[2])
                values3(I, 7)
                product(I, *ends[3])
                product(I, *ends[4])

            ln_turn(pe, 7, LOW, [0])
            pe.wait_ge(o_added, 128)
            pe.wait_ge(mlp_lo, 8)
            for hf in range(2):
                pe.wait_ge(hm_lo, 2 * hf + 2)
                v = slice(hf * HALF, (hf + 1) * HALF)
                for f in range(FT):
                    if hf == 0 and f == 1:
                        ln_turn(pe, 7, LOW, [1])
                    n, fs = FT * hf + f, slice(f * P, (f + 1) * P)
                    if n >= 4:
                        pe.wait_ge(g3_hi, n - 3)
                    for c in range(C):
                        last = three(banks[4 + n % 4][:, :], FC1h[:, c, fs], FC1l[:, c, fs], HMh[:, c, v],
                                     HMl[:, c, v], c == 0, c == C - 1)
                    last.then_inc(fc1_ready, 1)
            for pair in range(4):
                pe.wait_ge(g3_lo, FT * (pair // 2 + 1))
                for k in range(2):
                    ts = slice((2 * pair + k) * P, (2 * pair + k + 1) * P)
                    for f in range(FT):
                        last = three(banks[pair][:, k * E:(k + 1) * E], G3h[:, f, ts], G3l[:, f, ts],
                                     FC2h[:, f, :], FC2l[:, f, :], f == 0, f == FT - 1)
                last.then_inc(fc2_ready, 1)

        @block.scalar
        def _(act):
            def qk_high(H, par):
                act.wait_ge(ld_wqk, 16 * (H + 1))
                nc.scalar.copy(WQKh[:, par, :, :], WQK[:, :, :]).then_inc(wqk_hi, 1)

            def wv_high(I):
                act.wait_ge(ld_wv, 16 * (I + 1))
                nc.scalar.copy(WVh[:, :, :], WV3[:, :, :]).then_inc(wv_hi, 1)

            def context():
                for i, (c, hf) in enumerate(TURN_ORDER):
                    act.wait_ge(turned, 4 + i + 1)
                    nc.scalar.copy(CTh[:, c, hf * HALF:(hf + 1) * HALF], banks[4 + 2 * c + hf][:, :]).then_inc(ct_hi, 1)

            def context_rows():
                for i, (c, hf) in enumerate(TURN_ORDER):
                    act.wait_ge(turned, 8 + i + 1)
                    nc.scalar.activation(AT[:, 4 * c + 2 * hf:4 * c + 2 * hf + 2, :],
                                         banks[2 * c + hf][:, :].rearrange("p (b t) -> p b t", b=2), ACT.Identity,
                                         scale=VECA[:, G1 + c:G1 + c + 1],
                                         bias=VECA[:, B1 + c:B1 + c + 1]).then_inc(at_ready, 1)

            def audio_keys(q):
                act.wait_ge(k1_proj, q + 1)
                nc.scalar.copy(K1[:, q // 2, (q % 2) * HALF:(q % 2 + 1) * HALF], banks[4 + q][:, :]).then_inc(k1_out, 1)

            def audio_values(pair):
                act.wait_ge(v1_proj, pair + 1)
                nc.scalar.copy(V1[:, 2 * pair:2 * pair + 2, :],
                               banks[4 + pair][:, :].rearrange("p (m d) -> p m d", m=2)).then_inc(v1_ready, 1)

            def shifted_rows(li, n_ln, n_turn, w, b, prev, where):
                if n_ln:
                    ln_act(act, n_ln, (0, 1))
                act.wait_ge(turned, 4 * n_turn + 1)
                nc.scalar.copy(XN[:, :, 0], PREV[:, prev, :]).then_inc(xn_ready, 1)
                for i, (c, hf) in enumerate(TURN_ORDER):
                    if i == 2:
                        ln_act(act, n_ln, (2, 3))
                    act.wait_ge(turned, 4 * n_turn + i + 1)
                    nc.scalar.activation(XN[:, 4 * c + 2 * hf:4 * c + 2 * hf + 2, 1:T + 1],
                                         banks[where[2 * c + hf]][:, :].rearrange("p (b t) -> p b t", b=2),
                                         ACT.Identity, scale=lnw(li, w, c), bias=lnw(li, b, c)).then_inc(xn_ready, 1)

            def take(q, dst, func=ACT.Copy, sem_=None, **kw):
                c, hf = q // 2, q % 2
                return nc.scalar.activation(dst[:, 4 * c + 2 * hf:4 * c + 2 * hf + 2, :],
                                            banks[4 + q][:, :].rearrange("p (b t) -> p b t", b=2), func, **kw)

            def bias_rows(a, bank):
                act.wait_ge(aux_ready, a + 1)
                nc.scalar.copy(WAUX[a], banks[bank][0:32, 0:E]).then_inc(waux_out, 1)

            def rwkv(li, lns, turns, where):
                shifted_rows(li, lns[0], turns[0], LN1W, LN1B, 1, where)
                for i, q in enumerate(QUARTERS):
                    act.wait_ge(m1_ready, 4 * li + i + 1)
                    nc.scalar.activation(M1[:, q // 2, (q % 2) * HALF:(q % 2 + 1) * HALF], banks[where[q]][:, :],
                                         ACT.Tanh).then_inc(m1_tanh, 1)
                if li == 0:
                    context()
                    ln_act(act, 1)
                for hf in range(2):
                    act.wait_ge(proj_ready, 22 * li + hf + 1)
                    nc.scalar.activation(DT[:, hf * HALF:(hf + 1) * HALF], banks[4 + hf][:, :],
                                         ACT.Tanh).then_inc(proj_out, 1)
                for i, q in enumerate(QUARTERS):
                    act.wait_ge(proj_ready, 22 * li + 2 + i + 1)
                    take(q, WT, ACT.Exp, bias=lnw(li, TD, q // 2)).then_inc(proj_out, 1)
                for i, q in enumerate(QUARTERS):
                    act.wait_ge(proj_out, 18 * li + 2 + i + 1)
                    v = WT[:, 4 * (q // 2) + 2 * (q % 2):4 * (q // 2) + 2 * (q % 2) + 2, :]
                    nc.scalar.activation(v, v, ACT.Exp, scale=-1.0).then_inc(decay_e, 1)
                for n, dst in ((1, KT), (2, VT), (3, RT)):
                    for i, q in enumerate(QUARTERS):
                        act.wait_ge(proj_ready, 22 * li + 2 + 4 * n + i + 1)
                        take(q, dst).then_inc(proj_out, 1)
                for i, q in enumerate(QUARTERS):
                    act.wait_ge(proj_ready, 22 * li + 18 + i + 1)
                    take(q, TH, ACT.Tanh, scale=0.5).then_inc(gate_th, 1)
                def first_state(k):
                    nc.scalar.copy(SS[k % 2][:, :, 0], S0[:, S * k:S * k + S]).then_inc(state0, 1)

                if li == 0:
                    context_rows()
                act.wait_ge(moved["k"], 128 * (li + 1))
                act.wait_ge(moved["v"], 128 * (li + 1))
                act.wait_ge(moved["r"], 128 * (li + 1))
                first_state(0)
                first_state(1)
                for k in range(S):
                    nc.scalar.activation(RK[:, k, :], RS[:, k, :], ACT.Copy,
                                         scale=VEC[:, li, UCOL + k:UCOL + k + 1]).then_inc(coef_ru, 1)
                if li == 0:
                    for q in range(4):
                        audio_keys(q)
                else:
                    bias_rows(0, 3)
                for k in range(2, S):
                    act.wait_ge(read_out, 8 * li + k - 1)
                    first_state(k)
                    if k == 3:
                        act.wait_ge(coef_sum, li + 1)
                        nc.scalar.copy(CF[:, :], banks[4][:, 0:T]).then_inc(coef_ready, 1)
                for q in range(2):
                    act.wait_ge(summed, 9 * (li + 1))
                    nc.scalar.copy(AS[:, 2 * q:2 * q + 2, :],
                                   banks[q][:, :].rearrange("p (b t) -> p b t", b=2)).then_inc(att_out, 1)
                if li == 0:
                    for pair in range(4):
                        audio_values(pair)
                else:
                    bias_rows(1, 7)
                nc.scalar.activation(VL[:, 0:1], EPSC[:, 0:1], ACT.Ln)
                for i, q in enumerate(QUARTERS):
                    act.wait_ge(centered, 4 * li + i + 1)
                    take(q, SQ, ACT.Square).then_inc(squared, 1)
                for i, q in enumerate(QUARTERS):
                    c, hf = q // 2, q % 2
                    v = slice(4 * c + 2 * hf, 4 * c + 2 * hf + 2)
                    act.wait_ge(gvar, 4 * li + i + 1)
                    nc.scalar.activation(SD[:, v, :], banks[4 + q][:, :].rearrange("p (b t) -> p b t", b=2), ACT.Ln,
                                         bias=EPSC[:, 0:1]).then_inc(glog, 1)
                for i, q in enumerate(QUARTERS):
                    c, hf = q // 2, q % 2
                    v = slice(4 * c + 2 * hf, 4 * c + 2 * hf + 2)
                    act.wait_ge(glog, 4 * li + i + 1)
                    nc.scalar.activation(SD[:, v, :], SD[:, v, :], ACT.Exp, scale=-0.5).then_inc(ginv, 1)
                shifted_rows(li, lns[1], turns[1], LN2W, LN2B, 0, HIGH)
                if li == 1:
                    qk_high(0, 0)
                    wv_high(0)
                for i, q in enumerate(QUARTERS):
                    act.wait_ge(fk_pos, 4 * li + i + 1)
                    c, hf = q // 2, q % 2
                    sl = slice(4 * c + 2 * hf, 4 * c + 2 * hf + 2)
                    nc.scalar.activation(KK2[:, sl, :], KK[:, sl, :], ACT.Square).then_inc(fk_sq, 1)
                for pair in range(4):
                    act.wait_ge(fr_ready, 4 * li + pair + 1)
                    nc.scalar.activation(RR[:, 2 * pair:2 * pair + 2, :],
                                         banks[pair][:, :].rearrange("p (b t) -> p b t", b=2), ACT.Tanh,
                                         scale=0.5).then_inc(fr_th, 1)

            def audio():
                for i, (c, hf) in enumerate(TURN_ORDER):
                    act.wait_ge(turned, 16 + i + 1)
                    nc.scalar.copy(XT1[:, c, hf * HALF:(hf + 1) * HALF], banks[2 * c + hf][:, :]).then_inc(xt_ready, 1)
                nc.scalar.activation(GT[:, :], VECA[:, GATE:GATE + 1], ACT.Tanh).then_inc(gate_done, 1)
                for q in range(4):
                    act.wait_ge(q1_proj, q + 1)
                    nc.scalar.copy(Q1h[:, q // 2, (q % 2) * HALF:(q % 2 + 1) * HALF], banks[4 + q][:, :]).then_inc(q1_hi, 1)

                def weights(i, j):
                    g = 8 * i + j
                    act.wait_ge(sc_max, g + 1)
                    for tt in range(2):
                        last = nc.scalar.activation(P1[:, j % 4, tt, :], P1[:, j % 4, tt, :], ACT.Exp,
                                                    scale=D1 ** -0.5, bias=NS1[:, g_par(j), tt:tt + 1],
                                                    accum_out=RS1[:, g_par(j), tt:tt + 1])
                    last.then_inc(p1_ready, 1)

                def take_turned(i, j):
                    g = 8 * i + j
                    act.wait_ge(p1_turned, g + 1)
                    if not (isinstance(g, int) and g < 2):
                        act.wait_ge(pv_done, g - 1)
                    nc.scalar.copy(PT1[:, g_par(j), :, :],
                                   banks[2 + g_par(j)][:, :].rearrange("p (s t) -> p s t", s=2)).then_inc(pt_out, 1)

                def body(i):
                    for j in range(8):
                        if not (isinstance(i, int) and 8 * i + j < 3):
                            take_turned(i, j - 3)
                        weights(i, j)

                body(0)
                with act.Fori(1, 8) as i:
                    body(i)
                for j in (-3, -2, -1):
                    take_turned(8, j)
                for q in range(4):
                    act.wait_ge(pv_done, 4 * H1 - 2 + 2 * (q % 2) if q >= 2 else 2 * H1)
                    nc.scalar.copy(AOT[:, q // 2, (q % 2) * HALF:(q % 2 + 1) * HALF],
                                   banks[4 + q][:, :]).then_inc(ao_turned, 1)

            act.wait_ge(eps_set, 1)
            nc.scalar.activation(VL[:, 0:1], EPSC[:, 0:1], ACT.Sqrt).then_inc(root_table, 1)
            act.wait_ge(root_table, 1)
            ln_act(act, 0, (0, 1))
            act.wait_ge(ld_small, 80)
            rwkv(0, (0, 2), (0, 3), LOW)
            audio()
            rwkv(1, (3, 4), (5, 6), HIGH)

            def wo_high(H, par):
                act.wait_ge(ld_wo3, 16 * (H + 1))
                if not (isinstance(H, int) and H < 2):
                    act.wait_ge(o_full, 4 * H - 4)
                nc.scalar.copy(WOh[:, par, :], WO3[:, :]).then_inc(wo_hi, 1)

            def key_bias(H, par):
                act.wait_ge(hb_ready, H + 1)
                nc.scalar.copy(K3h[:, par, :, T:KEYS],
                               HB[:, par, 2:3].unsqueeze(2).to_broadcast([P, B, 2])).then_inc(key_hi, 1)

            def take_high(I, kind, n, bank, before):
                if kind == "qk":
                    pr, hf = (n // 4) % 2, (n // 2) % 2
                    act.wait_ge(hb_ready, 2 * I + n // 4 + 1)
                    act.wait_ge(qk_full, 8 * I + (PLACE[n] if n < 4 else n) + 1)
                    if n % 2 == 0:
                        nc.scalar.activation(Q3h[:, pr, hf * HALF:(hf + 1) * HALF], banks[bank][:, :], ACT.Identity,
                                             bias=HB[:, pr, 0:1]).then_inc(qk_hi, 1)
                    else:
                        nc.scalar.activation(K3h[:, pr, 2 * hf:2 * hf + 2, 0:T],
                                             banks[bank][:, :].rearrange("p (b t) -> p b t", b=2), ACT.Identity,
                                             bias=HB[:, pr, 1:2]).then_inc(qk_hi, 1)
                elif kind == "pb":
                    act.wait_ge(pb_turned, 4 * (I // 8) + n + 1)
                    nc.scalar.copy(PBT[0:32, n * T:(n + 1) * T], banks[bank][0:32, 0:T]).then_inc(pbt_out, 1)
                elif kind == "v":
                    m = 2 * (n % 4)
                    act.wait_ge(v_added, 4 * I + n + 1)
                    nc.scalar.copy(V3h[:, m:m + 2, :], V3[:, n % 2, :, :]).then_inc(v_hi, 1)

            def turned_high(I, s):
                act.wait_ge(p3_turned, 8 * I + s + 1)
                nc.scalar.copy(PT3h[:, s % 2, :, :],
                               banks[2][:, :].rearrange("p (s t) -> p s t", s=2)).then_inc(pt3_hi, 1)

            def weights3(I, s):
                G = 8 * I + s
                act.wait_ge(s3_shift, G + 1)
                if not (isinstance(G, int) and G < 2):
                    act.wait_ge(p3_bias, G - 1)
                    act.wait_ge(p3_turned, G - 1)
                for tt in range(2):
                    nc.scalar.activation(P3[:, s % 2, tt, 0:T + 1], banks[tt][:, 0:T + 1], ACT.Exp,
                                         scale=D3 ** -0.5, bias=NS3[:, s % 2, tt:tt + 1],
                                         accum_out=RS3[:, s % 2, tt:tt + 1]).then_inc(p3_ready, 1)

            def context_high(I, s):
                act.wait_ge(c3_ready, 8 * I + s + 1)
                nc.scalar.copy(C3h[:, (s // 4) % 2, (s % 4) * T:(s % 4 + 1) * T], banks[4][:, 0:T]).then_inc(c3_hi, 1)

            def pair(I, case):
                final = isinstance(I, int) and I == 15
                for s in range(8):
                    todo = [x for x in products(case, s) if x[0] in ("qk", "v")]
                    weights3(I, s)
                    if todo and todo[0][0] == "v":
                        take_high(I, *todo.pop(0))
                    if lagged(case, s, 1):
                        turned_high(I, s - 1)
                    if lagged(case, s, 2):
                        context_high(I, s - 2)
                    for x in todo:
                        take_high(I, *x)
                    for x in products(case, s):
                        if x[0] == "pb":
                            take_high(I, *x)
                    if s == 0 and not final:
                        qk_high(2 * I + 2, 0)
                    if s == 4 and not final:
                        qk_high(2 * I + 3, 1)
                    if s % 4 == 1:
                        wo_high(2 * I + s // 4, s // 4)
                    if s == 1:
                        key_bias(2 * I + 1, 1)
                    if s == 5 and not final:
                        key_bias(2 * I + 2, 0)
                    if s == 3 and not final:
                        wv_high(I + 1)
                    if final:
                        if s == 0:
                            act.wait_ge(ld_fc1, 16)
                        if s == 4:
                            act.wait_ge(ld_fc2, 16)
                        raw, high, _ = mlp_weights(s)
                        nc.scalar.copy(high, raw).then_inc(mlp_hi, 1)

            for a in range(2):
                if a == 0:
                    ln_act(act, 5, (0, 1))

                def h_row(i):
                    c, hf = TURN_ORDER[i]
                    act.wait_ge(turned, 28 + 4 * a + i + 1)
                    v = slice(hf * HALF, (hf + 1) * HALF)
                    nc.scalar.activation(HF[:, c, v], banks[SPARE[2 * c + hf]][:, :], ACT.Identity,
                                         scale=VECA[:, LN3 + 4 * a + c:LN3 + 4 * a + c + 1],
                                         bias=VECA[:, LN3 + 4 * a + 2 + c:LN3 + 4 * a + 3 + c]).then_inc(h_rows, 1)

                def h_high(i):
                    c, hf = TURN_ORDER[i]
                    v = slice(hf * HALF, (hf + 1) * HALF)
                    act.wait_ge(h_rows, 4 * a + i + 1)
                    nc.scalar.copy(Hh[:, c, v], HF[:, c, v]).then_inc(h_hi, 1)

                first = products("prologue", 0)
                if a == 0:
                    key_bias(0, 0)
                h_row(0)
                h_row(1)
                h_high(0)
                h_high(1)
                if a == 0:
                    ln_act(act, 5, (2, 3))
                take_high(8 * a, *first[0])
                h_row(2)
                h_row(3)
                h_high(2)
                h_high(3)
                take_high(8 * a, *first[1])
                for x in first[2:]:
                    take_high(8 * a, *x)
                if a == 0:
                    qk_high(1, 1)
                attention_pairs(act, a, pair)
                I, ends = 8 * a + 7, products("end", 0)
                turned_high(I, 7)
                take_high(I, *ends[0])
                context_high(I, 6)
                ln_act(act, 6 + a, [0])
                take_high(I, *ends[2])
                context_high(I, 7)
                ln_act(act, 6 + a, [1, 2, 3] if a == 0 else [1, 2])

            def hm_row(i):
                c, hf = TURN_ORDER[i]
                act.wait_ge(turned, 36 + i + 1)
                nc.scalar.activation(HM3[:, c, hf * HALF:(hf + 1) * HALF], banks[2 * c + hf][:, :], ACT.Identity,
                                     scale=VECA[:, LN3 + 8 + c:LN3 + 9 + c],
                                     bias=VECA[:, LN3 + 10 + c:LN3 + 11 + c]).then_inc(hm_ready, 1)

            def hm_high(i):
                c, hf = TURN_ORDER[i]
                v = slice(hf * HALF, (hf + 1) * HALF)
                act.wait_ge(hm_ready, i + 1)
                nc.scalar.copy(HMh[:, c, v], HM3[:, c, v]).then_inc(hm_hi, 1)

            for hf in range(2):
                hm_row(2 * hf)
                hm_row(2 * hf + 1)
                hm_high(2 * hf)
                hm_high(2 * hf + 1)
                if hf == 0:
                    ln_act(act, 7, [3])
            for n in range(2 * FT):
                hf, f = n // FT, n % FT
                act.wait_ge(fc1_ready, n + 1)
                nc.scalar.activation(G3[:, f, hf * HALF:(hf + 1) * HALF], banks[4 + n % 4][:, :], ACT.Gelu,
                                     bias=VECA[:, BFC1 + f:BFC1 + f + 1]).then_inc(gelu_out, 1)
                act.wait_ge(gelu_out, n + 1)
                nc.scalar.copy(G3h[:, f, hf * HALF:(hf + 1) * HALF],
                               G3[:, f, hf * HALF:(hf + 1) * HALF]).then_inc(g3_hi, 1)

        @block.vector
        def _(dve):
            def head_biases(H, par):
                nc.vector.tensor_scalar(HB[:, par, :], VECA[:, BQ:HMASK].rearrange("p (w h) -> p w h", w=3)
                                        [:, :, bass.ds(H, 1)], 1.0, None, ALU.mult).then_inc(hb_ready, 1)

            def context_low():
                for i, (c, hf) in enumerate(TURN_ORDER):
                    dve.wait_ge(ct_hi, i + 1)
                    v = slice(hf * HALF, (hf + 1) * HALF)
                    nc.vector.tensor_tensor(CTl[:, c, v], banks[4 + 2 * c + hf][:, :], CTh[:, c, v].bitcast(F32),
                                            ALU.subtract).then_inc(ct_lo, 1)

            def add_rows(sem_, n0, where):
                for pair in range(4):
                    dve.wait_ge(sem_, n0 + pair + 1)
                    nc.vector.tensor_tensor(X[:, 2 * pair:2 * pair + 2, :],
                                            banks[where[pair]][:, :].rearrange("p (m d) -> p m d", m=2),
                                            X[:, 2 * pair:2 * pair + 2, :], ALU.add).then_inc(x_sum, 1)

            def token_shift(li, second, first_mix):
                for i, (c, hf) in enumerate(TURN_ORDER):
                    v = slice(4 * c + 2 * hf, 4 * c + 2 * hf + 2)
                    if hf == 0:
                        dve.wait_ge(sx_first, 4 * li + 2 * second + i + 1)
                    else:
                        dve.wait_ge(xn_ready, 10 * li + 5 * second + i + 2)
                        nc.vector.tensor_tensor(SX[:, v, :], XN[:, v, 0:T], XN[:, v, 1:T + 1],
                                                ALU.subtract).then_inc(sx_ready, 1)
                        dve.wait_ge(sx_ready, 4 * li + 2 * second + i - 1)
                    first_mix(v, c)

            def rwkv(li, n_ln, xs, next_ln=None):
                def maa_mix(v, c):
                    nc.vector.scalar_tensor_tensor(X5[2][:, v, :], SX[:, v, :], lnw(li, MAAX, c),
                                                   XN[:, v, 1:T + 1], ALU.mult, ALU.add).then_inc(xmix_ready, 1)

                token_shift(li, 0, maa_mix)
                if li == 0:
                    dve.wait_ge(ld_c, 16)
                    ln_moments(dve, 1, CRAW, range(4))
                for n in range(5):
                    if li == 0 and n == 1:
                        context_low()
                    if li == 0 and n == 3:
                        ln_normalise(dve, 1, CRAW, range(4), XNC)
                    for i, q in enumerate(QUARTERS):
                        c, hf = q // 2, q % 2
                        v = slice(4 * c + 2 * hf, 4 * c + 2 * hf + 2)
                        dve.wait_ge(mix_ready, 20 * li + 4 * n + i + 1)
                        if n == 3:
                            dve.wait_ge(proj_ready, 22 * li + 2)
                        if n == 4:
                            dve.wait_ge(proj_ready, 22 * li + 10)
                        nc.vector.scalar_tensor_tensor(X5[n % 3][:, v, :],
                                                       banks[q][:, :].rearrange("p (b t) -> p b t", b=2),
                                                       lnw(li, STACK + 2 * MIX[n], c), SX[:, v, :], ALU.add,
                                                       ALU.mult).then_inc(mix_scaled, 1)

                def scan(k):
                    for d in range(S):
                        nc.vector.tensor_tensor_scan(SS[k % 2][:, d, 1:T + 1], WS[:, k, :], AK[k % 2][:, d, :],
                                                     S0[:, S * k + d:S * k + d + 1], ALU.mult,
                                                     ALU.add).then_inc(scanned, 1)

                for name in "kv":
                    dve.wait_ge(moved[name], 128 * (li + 1))
                dve.wait_ge(mix_scaled, 20 * (li + 1))
                nc.vector.tensor_tensor(AK[0], VS, KS[:, 0, :].unsqueeze(1).to_broadcast([P, S, T]),
                                        ALU.mult).then_inc(outer_dve, 1)
                dve.wait_ge(outer_dve, li + 1)
                dve.wait_ge(moved["w"], 128 * (li + 1))
                scan(0)
                dve.wait_ge(outer_pool, 7 * li + 1)
                scan(1)
                for i, q in enumerate(QUARTERS):
                    c, hf = q // 2, q % 2
                    v = slice(4 * c + 2 * hf, 4 * c + 2 * hf + 2)
                    dve.wait_ge(gate_th, 4 * li + i + 1)
                    nc.vector.scalar_tensor_tensor(G2[:, v, :], TH[:, v, :], 1.0,
                                                   banks[4 + q][:, :].rearrange("p (b t) -> p b t", b=2), ALU.add,
                                                   ALU.mult).then_inc(g_ready, 1)
                dve.wait_ge(moved["r"], 128 * (li + 1))
                dve.wait_ge(g_ready, 4 * (li + 1))
                for k in range(S):
                    dve.wait_ge(scanned, 64 * li + 8 * (k + 1))
                    dve.wait_ge(state0, 8 * li + k + 1)
                    if k >= 2:
                        dve.wait_ge(summed, 9 * li + k - 1)
                    nc.vector.tensor_tensor(MK[k % 2], SS[k % 2][:, :, 0:T],
                                            RS[:, k, :].unsqueeze(1).to_broadcast([P, S, T]),
                                            ALU.mult).then_inc(read_out, 1)
                    if k + 2 < S:
                        dve.wait_ge(outer_pool, 7 * li + k + 2)
                        dve.wait_ge(read_out, 8 * li + k + 1)
                        scan(k + 2)
                for q in (2, 3):
                    dve.wait_ge(summed, 9 * (li + 1))
                    nc.vector.tensor_copy(AS[:, 2 * q:2 * q + 2, :],
                                          banks[q][:, :].rearrange("p (b t) -> p b t", b=2)).then_inc(att_out, 1)
                for i, q in enumerate(QUARTERS):
                    c, hf = q // 2, q % 2
                    v = slice(4 * c + 2 * hf, 4 * c + 2 * hf + 2)
                    nc.vector.tensor_scalar(GB[:, v, :], G2[:, v, :], lnw(li, GNB, c), None,
                                            ALU.mult).then_inc(gate_offset, 1)
                for i, q in enumerate(QUARTERS):
                    c, hf = q // 2, q % 2
                    v = slice(4 * c + 2 * hf, 4 * c + 2 * hf + 2)
                    dve.wait_ge(squared, 4 * li + i + 1)
                    nc.vector.scalar_tensor_tensor(YT[:, v, :], banks[4 + q][:, :].rearrange("p (b t) -> p b t", b=2),
                                                   lnw(li, GNW, c), G2[:, v, :], ALU.mult,
                                                   ALU.mult).then_inc(gscaled, 1)
                for i, q in enumerate(QUARTERS):
                    c, hf = q // 2, q % 2
                    v = slice(4 * c + 2 * hf, 4 * c + 2 * hf + 2)
                    dve.wait_ge(gscaled, 4 * li + i + 1)
                    dve.wait_ge(ginv, 4 * li + i + 1)
                    nc.vector.tensor_tensor(YT[:, v, :], YT[:, v, :], SD[:, v, :], ALU.mult).then_inc(y_ready, 1)
                for pair in range(4):
                    v = slice(2 * pair, 2 * pair + 2)
                    dve.wait_ge(wo_ready, 4 * li + pair + 1)
                    nc.vector.scalar_tensor_tensor(X[:, v, :], banks[QUARTERS[pair]][:, :].rearrange("p (m d) -> p m d", m=2),
                                                   0.5, X[:, v, :], ALU.mult, ALU.add).then_inc(x_sum, 1)
                    ln_pair(dve, n_ln, pair, xs + pair + 1)

                def key_mix(v, c):
                    nc.vector.scalar_tensor_tensor(XK[:, v, :], SX[:, v, :], lnw(li, FMK, c),
                                                   XN[:, v, 1:T + 1], ALU.mult, ALU.add).then_inc(xkr_ready, 1)

                token_shift(li, 1, key_mix)
                for c, hf in TURN_ORDER:
                    v = slice(4 * c + 2 * hf, 4 * c + 2 * hf + 2)
                    nc.vector.scalar_tensor_tensor(XR[:, v, :], SX[:, v, :], lnw(li, FMR, c),
                                                   XN[:, v, 1:T + 1], ALU.mult, ALU.add).then_inc(xkr_ready, 1)
                for i, q in enumerate(QUARTERS):
                    c, hf = q // 2, q % 2
                    v = slice(4 * c + 2 * hf, 4 * c + 2 * hf + 2)
                    dve.wait_ge(fk_ready, 4 * li + i + 1)
                    nc.vector.tensor_scalar(KK[:, v, :], banks[4 + q][:, :].rearrange("p (b t) -> p b t", b=2), 0.0,
                                            None, ALU.max).then_inc(fk_pos, 1)
                if li == 1:
                    head_biases(0, 0)
                    head_biases(1, 1)
                for pair in range(4):
                    v = slice(2 * pair, 2 * pair + 2)
                    dve.wait_ge(fv_ready, 4 * li + pair + 1)
                    dve.wait_ge(fr_th, 4 * li + pair + 1)
                    nc.vector.scalar_tensor_tensor(FT1[:, v, :], RR[:, v, :], 1.0,
                                                   banks[4 + pair][:, :].rearrange("p (b t) -> p b t", b=2), ALU.add,
                                                   ALU.mult).then_inc(fv_mul, 1)
                    dve.wait_ge(fv_mul, 4 * li + pair + 1)
                    nc.vector.scalar_tensor_tensor(X[:, v, :], FT1[:, v, :], 0.5, X[:, v, :], ALU.mult,
                                                   ALU.add).then_inc(x_sum, 1)
                    if next_ln is not None:
                        ln_pair(dve, next_ln, pair, xs + 4 + pair + 1)

            def audio():
                dve.wait_ge(ld_mask, 16)
                nc.vector.tensor_scalar(MASKB[:, :], MU8[:, :], 1.0, -MOST_NEGATIVE, ALU.subtract,
                                        ALU.mult).then_inc(mask_f, 1)
                dve.wait_ge(mask_f, 1)
                nc.vector.tensor_scalar(MASKB[:, :], MASKB[:, :], 10.0, None, ALU.mult).then_inc(mask_b, 1)
                def values_in(h, par, c):
                    if not (isinstance(h, int) and h < 2):
                        dve.wait_ge(pv_done, 4 * h - 4)
                    else:
                        dve.wait_ge(vm_clear, 2)
                    for value, k in ((ZV[:, :, :], (h - 2) % HPC if isinstance(h, int) else h - 2 - HPC * c),
                                     (V1[:, :, bass.ds(D1 * h, D1)], h - HPC * c)):
                        nc.vector.tensor_scalar(VM[:, par, :, bass.ds(D1 * k, D1)], value, 1.0, None,
                                                ALU.mult).then_inc(vm_ready, 1)

                def keys_high(h, par, c):
                    nc.vector.tensor_scalar(KMh[:, par, :], K1[:, c, :], VECA[:, bass.ds(HMASK + h - 8 * c, 1)],
                                            None, ALU.mult).then_inc(km_hi, 1)

                def keys_low(h, par, c, hf):
                    v = slice(hf * HALF, (hf + 1) * HALF)
                    dve.wait_ge(km_hi, h + 1)
                    nc.vector.scalar_tensor_tensor(KMl[:, par, v], K1[:, c, v],
                                                   VECA[:, bass.ds(HMASK + h - 8 * c, 1)],
                                                   KMh[:, par, v].bitcast(F32), ALU.mult,
                                                   ALU.subtract).then_inc(km_lo, 1)

                def invert_sums(i, j):
                    dve.wait_ge(p1_ready, 8 * i + j + 1)
                    if not (isinstance(i, int) and 8 * i + j < 2):
                        dve.wait_ge(p1_scaled, 8 * i + j - 1)
                    nc.vector.reciprocal(RI1[:, g_par(j), :], RS1[:, g_par(j), :]).then_inc(p1_inv, 1)

                def body(i, c, c_next, last=False):
                    for j in range(8):
                        g, b = 8 * i + j, j % 4
                        dve.wait_ge(sc_ready, g + 1)
                        if not (isinstance(g, int) and g < 4):
                            dve.wait_ge(p1_turned, g - 3)
                        nc.vector.memset(CARRY[:, :], 0.0)
                        for tt in range(2):
                            nc.vector.tensor_tensor_reduce(P1[:, j % 4, tt, :],
                                                           banks[g_par(j)][:, tt * T:(tt + 1) * T],
                                                           MASKB[:, b * T:(b + 1) * T], 1.0, MOST_NEGATIVE,
                                                           ALU.add, ALU.max,
                                                           NM1[:, g_par(j), tt:tt + 1]).then_inc(sc_masked, 1)
                        dve.wait_ge(sc_masked, 2 * g + 2)
                        nc.vector.tensor_scalar(NS1[:, g_par(j), :], NM1[:, g_par(j), :], -D1 ** -0.5, None,
                                                ALU.mult).then_inc(sc_max, 1)
                        if not (isinstance(g, int) and g < 1):
                            invert_sums(i, j - 1)
                        if b == 0:
                            values_in(2 * i + j // 4, j // 4, c)
                        if b and not (last and j > 4):
                            h, par, c_ = 2 * i + j // 4 + 1, (j // 4 + 1) % 2, c if j < 4 else c_next
                            if b == 1:
                                keys_high(h, par, c_)
                            else:
                                keys_low(h, par, c_, b - 2)

                keys_high(0, 0, 0)
                keys_low(0, 0, 0, 0)
                keys_low(0, 0, 0, 1)
                for q in range(4):
                    v = slice((q % 2) * HALF, (q % 2 + 1) * HALF)
                    dve.wait_ge(q1_hi, q + 1)
                    nc.vector.tensor_tensor(Q1l[:, q // 2, v], banks[4 + q][:, :], Q1h[:, q // 2, v].bitcast(F32),
                                            ALU.subtract).then_inc(q1_lo, 1)

                dve.wait_ge(mask_b, 1)
                for c in range(C):
                    body(4 * c, c, c)
                    with dve.Fori(4 * c + 1, 4 * c + 3) as i:
                        body(i, c, c)
                    body(4 * c + 3, c, 1, c == 1)
                invert_sums(8, -1)
                dve.wait_ge(gate_done, 1)
                for pair in range(4):
                    dve.wait_ge(out1_ready, pair + 1)
                    nc.vector.scalar_tensor_tensor(X[:, 2 * pair:2 * pair + 2, :],
                                                   banks[pair][:, :].rearrange("p (m d) -> p m d", m=2),
                                                   GT[:, 0:1], X[:, 2 * pair:2 * pair + 2, :], ALU.mult,
                                                   ALU.add).then_inc(x_sum, 1)
                    ln_pair(dve, 3, pair, 8 + pair + 1)

            nc.vector.memset(EPSC[:, :], EPS).then_inc(eps_set, 1)
            for hf, loaded in enumerate((ld_x0, ld_x1)):
                dve.wait_ge(loaded, 16)
                ln_dve(dve, 0, X, (2 * hf, 2 * hf + 1))
            rwkv(0, 2, 0)
            audio()
            rwkv(1, 4, 12, next_ln=5)

            def take_low(I, kind, n, bank, before):
                if kind == "qk":
                    pr, hf = (n // 4) % 2, (n // 2) % 2
                    dve.wait_ge(qk_hi, 8 * I + (PLACE[n] if n < 4 else n) + 1)
                    if n % 2 == 0:
                        v = slice(hf * HALF, (hf + 1) * HALF)
                        nc.vector.scalar_tensor_tensor(Q3l[:, pr, v], banks[bank][:, :],
                                                       HB[:, pr, 0:1],
                                                       Q3h[:, pr, v].bitcast(F32), ALU.add,
                                                       ALU.subtract).then_inc(qk_lo, 1)
                    else:
                        v = slice(2 * hf, 2 * hf + 2)
                        nc.vector.scalar_tensor_tensor(K3l[:, pr, v, 0:T],
                                                       banks[bank][:, :].rearrange("p (b t) -> p b t", b=2),
                                                       HB[:, pr, 1:2],
                                                       K3h[:, pr, v, 0:T].bitcast(F32), ALU.add,
                                                       ALU.subtract).then_inc(qk_lo, 1)
                elif kind == "v":
                    dve.wait_ge(v_full, 4 * I + n + 1)
                    dve.wait_ge(ld_bv, 16 * (I + n // 4 + 1))
                    if not (isinstance(I, int) and 4 * I + n < 2):
                        dve.wait_ge(v_lo, 4 * I + n - 1)
                    nc.vector.tensor_tensor(V3[:, n % 2, :, :],
                                            banks[bank][:, :].rearrange("p (m d) -> p m d", m=2),
                                            BV[:, :].unsqueeze(1).to_broadcast([P, 2, 2 * D3]),
                                            ALU.add).then_inc(v_added, 1)
                else:
                    v = slice(2 * (n % 4), 2 * (n % 4) + 2)
                    dve.wait_ge(o_full, 8 * I + n + 1)
                    nc.vector.tensor_tensor(X[:, v, :], banks[bank][:, :].rearrange("p (m d) -> p m d", m=2),
                                            X[:, v, :], ALU.add).then_inc(o_added, 1)

            def row_max(I, s):
                G = 8 * I + s
                for tt in range(2):
                    dve.wait_ge(s3_ready, 2 * G + tt + 1)
                    nc.vector.tensor_reduce(NM3[:, s % 2, tt:tt + 1], banks[tt][:, 0:T + 1], AX_X,
                                            ALU.max).then_inc(s3_max, 1)
                dve.wait_ge(s3_max, 2 * G + 2)
                nc.vector.tensor_scalar(NS3[:, s % 2, :], NM3[:, s % 2, :], -D3 ** -0.5, None,
                                        ALU.mult).then_inc(s3_shift, 1)

            def turned_low(I, s):
                dve.wait_ge(pt3_hi, 8 * I + s + 1)
                nc.vector.tensor_tensor(PT3l[:, s % 2, :, :],
                                        banks[2][:, :].rearrange("p (s t) -> p s t", s=2),
                                        PT3h[:, s % 2, :, :].bitcast(F32), ALU.subtract).then_inc(pt3_lo, 1)

            def invert(I, s):
                dve.wait_ge(p3_ready, 16 * I + 2 * s + 2)
                nc.vector.reciprocal(RI3[:, s % 2, :], RS3[:, s % 2, :]).then_inc(p3_inv, 1)

            def keep_bias(I, s, a):
                b, h = s % 4, 2 * I - 16 * a + s // 4
                dve.wait_ge(p3_scaled, 16 * I + 2 * s + 2)
                nc.vector.tensor_scalar(PB[:, 2 * b:2 * b + 2, bass.ds(h, 1)], P3[:, s % 2, :, T:T + 1], 1.0,
                                        None, ALU.mult).then_inc(p3_bias, 1)

            def context_low(I, s):
                pr, v = (s // 4) % 2, slice((s % 4) * T, (s % 4 + 1) * T)
                dve.wait_ge(c3_hi, 8 * I + s + 1)
                nc.vector.tensor_tensor(C3l[:, pr, v], banks[4][:, 0:T], C3h[:, pr, v].bitcast(F32),
                                        ALU.subtract).then_inc(c3_lo, 1)

            def key_bias_low(H, par):
                dve.wait_ge(key_hi, H + 1)
                nc.vector.tensor_tensor(K3l[:, par, :, T:KEYS],
                                        HB[:, par, 2:3].unsqueeze(2).to_broadcast([P, B, 2]),
                                        K3h[:, par, :, T:KEYS].bitcast(F32), ALU.subtract).then_inc(key_lo, 1)

            def hm_low(i):
                c, hf = TURN_ORDER[i]
                v = slice(hf * HALF, (hf + 1) * HALF)
                dve.wait_ge(hm_hi, i + 1)
                nc.vector.tensor_tensor(HMl[:, c, v], HM3[:, c, v], HMh[:, c, v].bitcast(F32),
                                        ALU.subtract).then_inc(hm_lo, 1)

            for a in range(2):
                def pair(I, case):
                    final = isinstance(I, int) and I == 15
                    later = []
                    for s in range(8):
                        todo = [x for x in products(case, s) if x[0] in ("qk", "v")]
                        row_max(I, s)
                        if lagged(case, s, 1):
                            keep_bias(I, s - 1, a)
                        for x in later:
                            take_low(I, *x)
                        later = []
                        if lagged(case, s, 4):
                            n = s - 4
                            if s:
                                take_low(I, *[x for x in products(case, s - 1) if x[0] == "o"][0])
                            else:
                                take_low(I - 1, *[x for x in products("steady", 7) if x[0] == "o"][0])
                        if todo and todo[0][0] == "v":
                            take_low(I, *todo.pop(0))
                        invert(I, s)
                        if lagged(case, s, 1):
                            turned_low(I, s - 1)
                        if lagged(case, s, 2):
                            context_low(I, s - 2)
                        if s in (2, 3, 4, 5, 6):
                            later = todo
                        else:
                            for x in todo:
                                take_low(I, *x)
                        if s == 0 and not final:
                            dve.wait_ge(qk_lo, 8 * I + 4)
                            dve.wait_ge(key_hi, 2 * I + 1)
                            dve.wait_ge(key_lo, 2 * I + 1)
                            head_biases(2 * I + 2, 0)
                        if s == 1:
                            dve.wait_ge(hb_ready, 2 * I + 2)
                            key_bias_low(2 * I + 1, 1)
                        if s == 4 and not final:
                            dve.wait_ge(qk_lo, 8 * I + 8)
                            dve.wait_ge(key_lo, 2 * I + 2)
                            head_biases(2 * I + 3, 1)
                        if s == 5 and not final:
                            dve.wait_ge(hb_ready, 2 * I + 3)
                            key_bias_low(2 * I + 2, 0)

                if a == 0:
                    key_bias_low(0, 0)
                if a:
                    dve.wait_ge(pb_turned, 4)
                nc.vector.memset(PB[:, :, :], 0.0).then_inc(pb_clear, 1)
                dve.wait_ge(pb_clear, a + 1)
                nc.vector.memset(PB[:, :, 16:17], 1.0).then_inc(pb_one, 1)

                def h_low(i):
                    c, hf = TURN_ORDER[i]
                    dve.wait_ge(h_hi, 4 * a + i + 1)
                    v = slice(hf * HALF, (hf + 1) * HALF)
                    nc.vector.tensor_tensor(Hl[:, c, v], HF[:, c, v], Hh[:, c, v].bitcast(F32),
                                            ALU.subtract).then_inc(h_lo, 1)

                first = products("prologue", 0)
                h_low(0)
                h_low(1)
                take_low(8 * a, *first[0])
                h_low(2)
                h_low(3)
                for x in first[1:]:
                    take_low(8 * a, *x)
                dve.wait_ge(pb_one, a + 1)
                attention_pairs(dve, a, pair)
                I, ends = 8 * a + 7, products("end", 0)

                def moments(k):
                    dve.wait_ge(o_added, 8 * I + 5 + k)
                    ln_moments(dve, 6 + a, X, [k])

                keep_bias(I, 7, a)
                take_low(I, *[x for x in products("last", 7) if x[0] == "o"][0])
                turned_low(I, 7)
                context_low(I, 6)
                moments(0)
                ln_normalise(dve, 6 + a, X, [0])
                take_low(I, *ends[1])
                context_low(I, 7)
                moments(1)
                take_low(I, *ends[3])
                ln_normalise(dve, 6 + a, X, [1])
                moments(2)
                take_low(I, *ends[4])
                ln_normalise(dve, 6 + a, X, [2])
                moments(3)
                if a:
                    hm_low(0)
                    hm_low(1)
                ln_normalise(dve, 6 + a, X, [3])

            dve.wait_ge(ln_rows, 64)
            dve.wait_ge(ld_bfc2, 16)
            nc.vector.tensor_tensor(X[:, :, :], X[:, :, :], BFC2[:, :].unsqueeze(1).to_broadcast([P, TILES, E]),
                                    ALU.add).then_inc(x_sum, 1)
            hm_low(2)
            hm_low(3)
            for n in range(2 * FT):
                v = slice(n // FT * HALF, (n // FT + 1) * HALF)
                dve.wait_ge(g3_hi, n + 1)
                nc.vector.tensor_tensor(G3l[:, n % FT, v], G3[:, n % FT, v], G3h[:, n % FT, v].bitcast(F32),
                                        ALU.subtract).then_inc(g3_lo, 1)
            dve.wait_ge(x_sum, 21)
            add_rows(fc2_ready, 0, (0, 1, 2, 3))

        @block.gpsimd
        def _(pool):
            def token_shift(li, second):
                for c in range(C):
                    v = slice(4 * c, 4 * c + 2)
                    pool.wait_ge(xn_ready, 10 * li + 5 * second + c + 2)
                    nc.gpsimd.tensor_tensor(SX[:, v, :], XN[:, v, 0:T], XN[:, v, 1:T + 1],
                                            ALU.subtract).then_inc(sx_first, 1)

            def rwkv(li):
                token_shift(li, 0)
                for n in range(5):
                    for i, q in enumerate(QUARTERS):
                        c, hf = q // 2, q % 2
                        v = slice(4 * c + 2 * hf, 4 * c + 2 * hf + 2)
                        pool.wait_ge(mix_scaled, 20 * li + 4 * n + i + 1)
                        nc.gpsimd.tensor_tensor(X5[n % 3][:, v, :], X5[n % 3][:, v, :], XN[:, v, 1:T + 1],
                                                ALU.add).then_inc(x5_ready, 1)
                for name in "kv":
                    pool.wait_ge(moved[name], 128 * (li + 1))
                pool.wait_ge(x5_ready, 20 * (li + 1))
                for k in range(1, S):
                    if k >= 2:
                        pool.wait_ge(scanned, 64 * li + 8 * (k - 1))
                    nc.gpsimd.tensor_tensor(AK[k % 2], VS, KS[:, k, :].unsqueeze(1).to_broadcast([P, S, T]),
                                            ALU.mult).then_inc(outer_pool, 1)
                    if k == 3:
                        pool.wait_ge(coef_ru, S * (li + 1))
                        nc.gpsimd.tensor_tensor(RK, RK, KS, ALU.mult).then_inc(coef_rk, 1)
                    if k == 6:
                        pool.wait_ge(coef_ready, li + 1)
                        nc.gpsimd.tensor_tensor(T1, VS, CF[:, :].unsqueeze(1).to_broadcast([P, S, T]),
                                                ALU.mult).then_inc(bonus_ready, 1)
                token_shift(li, 1)

            def audio():
                pool.wait_ge(x_sum, 8)
                nc.gpsimd.memset(VM[:, :, :, :], 0.0).then_inc(vm_clear, 1)
                nc.gpsimd.memset(ZV[:, :, :], 0.0).then_inc(vm_clear, 1)

                def scale(i, j):
                    pool.wait_ge(p1_inv, 8 * i + j + 1)
                    nc.gpsimd.tensor_tensor(P1[:, j % 4, :, :], P1[:, j % 4, :, :],
                                            RI1[:, g_par(j), :].unsqueeze(2).to_broadcast([P, 2, T]),
                                            ALU.mult).then_inc(p1_scaled, 1)

                with pool.Fori(0, 8) as i:
                    for j in range(8):
                        scale(i, j)

            rwkv(0)
            audio()
            rwkv(1)

            def qk_low(H, par):
                pool.wait_ge(wqk_hi, H + 1)
                nc.gpsimd.tensor_tensor(WQKl[:, par, :, :], WQK[:, :, :], WQKh[:, par, :, :].bitcast(F32),
                                        ALU.subtract).then_inc(wqk_lo, 1)

            def wo_low(H, par):
                pool.wait_ge(wo_hi, H + 1)
                nc.gpsimd.tensor_tensor(WOl[:, par, :], WO3[:, :], WOh[:, par, :].bitcast(F32),
                                        ALU.subtract).then_inc(wo_lo, 1)

            def wv_low(I):
                pool.wait_ge(wv_hi, I + 1)
                nc.gpsimd.tensor_tensor(WVl[:, :, :], WV3[:, :, :], WVh[:, :, :].bitcast(F32),
                                        ALU.subtract).then_inc(wv_lo, 1)

            def values_low(I, n):
                m = 2 * (n % 4)
                pool.wait_ge(v_hi, 4 * I + n + 1)
                nc.gpsimd.tensor_tensor(V3l[:, m:m + 2, :], V3[:, n % 2, :, :],
                                        V3h[:, m:m + 2, :].bitcast(F32), ALU.subtract).then_inc(v_lo, 1)

            def scale(I, s):
                pool.wait_ge(p3_inv, 8 * I + s + 1)
                for tt in range(2):
                    nc.gpsimd.tensor_tensor(P3[:, s % 2, tt, 0:T + 1], P3[:, s % 2, tt, 0:T + 1],
                                            RI3[:, s % 2, tt:tt + 1].to_broadcast([P, T + 1]),
                                            ALU.mult).then_inc(p3_scaled, 1)

            def pair(I, case):
                final = isinstance(I, int) and I == 15
                for s in range(8):
                    scale(I, s)
                    for x in products(case, s):
                        if x[0] == "v":
                            values_low(I, x[1])
                    if s == 0 and not final:
                        qk_low(2 * I + 2, 0)
                    if s == 4 and not final:
                        qk_low(2 * I + 3, 1)
                    if s % 4 == 1:
                        wo_low(2 * I + s // 4, s // 4)
                    if s == 3 and not final:
                        wv_low(I + 1)
                    if final:
                        raw, high, low = mlp_weights(s)
                        pool.wait_ge(mlp_hi, s + 1)
                        nc.gpsimd.tensor_tensor(low, raw, high.bitcast(F32), ALU.subtract).then_inc(mlp_lo, 1)

            qk_low(0, 0)
            wv_low(0)
            qk_low(1, 1)
            for a in range(2):
                values_low(8 * a, 0)
                attention_pairs(pool, a, pair)


def kernel(**inputs):
    import numpy as np
    import concourse.bacc as _bacc
    from concourse.bass_utils import run_bass_kernel_spmd as _run

    a = {k: np.asarray(v) for k, v in inputs.items()}

    def cols(v):
        return v.reshape(-1, P).T

    def wt(w):
        return w.reshape(C, P, -1).transpose(1, 0, 2).reshape(P, -1)

    def padded(w, shape):
        z = np.zeros(shape, np.float32)
        z[:w.shape[0], :w.shape[1]] = w
        return z

    def bias_columns(v):
        z = np.zeros((P, H3, 32), np.float32)
        for h in range(H3):
            z[:, h, h] = v[h]
        return z

    def rwkv_weights(p):
        w2 = np.zeros((P, 5, E), np.float32)
        for j in range(5):
            w2[32 * (j % 4):32 * (j % 4) + 32, j] = a[p + "maa_w2"][j]
        parts = [wt(padded(a[p + "maa_w1"], (E, 256))), w2.reshape(P, -1), wt(padded(a[p + "decay_w1"], (E, P))),
                 padded(a[p + "decay_w2"], (P, E))]
        parts += [wt(a[p + n].T) for n in ("Wk", "Wv", "Wr", "Wg", "Wo", "ffn_Wk", "ffn_Wr", "ffn_Wv")]
        return np.concatenate(parts, 1)

    def rwkv_vectors(p):
        parts = [cols(a[p + n]) for n in ("ln1_w", "ln1_b", "ln2_w", "ln2_b", "maa_x")]
        parts += [cols(a[p + "maa_stack"].reshape(-1))]
        parts += [cols(a[p + n]) for n in ("time_decay", "gn_w", "gn_b", "ffn_maa_k", "ffn_maa_r")]
        return np.concatenate(parts + [np.tile(a[p + "faaaa"], (B, 1))], 1)

    q = "L3_xattn_"
    head_of = np.arange(P)[:, None] // D1 == np.arange(HPC)[None, :]
    veca = [cols(a["L1_xattn_ln_gamma"]), cols(a["L1_xattn_ln_beta"]), np.tile(a["L1_xattn_gate"], (P, 1))]
    veca += [cols(a[q + n]) for n in ("ln1_scale", "ln1_offset", "ln2_scale", "ln2_offset", "ln_mlp_scale",
                                      "ln_mlp_offset", "b_fc1", "bq1", "bq2", "bk1", "bk2")]
    veca += [a[q + n].reshape(H3, D3).T for n in ("bias_k1", "bias_k2")]
    veca += [head_of.astype(np.float32)]
    same = (np.arange(P)[:, None] // S == np.arange(P)[None, :] // S).astype(np.float32) / S
    const = np.stack([np.eye(P, dtype=np.float32), np.eye(P, dtype=np.float32) - same, same], 1)
    ctx = a["ctx_2048"]
    prev = ctx[:, 0:2, :].reshape(B, 2, C, P).transpose(3, 1, 2, 0).reshape(P, 2, C * B)
    w3 = [np.concatenate([a[q + n + s].reshape(C, P, H3, D3).transpose(2, 1, 0, 3) for n in ("wq", "wk")]
                         + [a[q + "wo" + s].reshape(H3, P, C, P)], 2).reshape(H3, P, 3, E) for s in "12"]
    wv = [a[q + "wv" + s].reshape(C, P, H3 // 2, 2 * D3).transpose(2, 1, 0, 3) for s in "12"]
    arrays = {
        "x": a["x"], "ctx": ctx, "mask": a["mask_BxS2_bf1"].reshape(1, B * T).view(np.uint8),
        "prev": prev, "s0": ctx[:, 2:10, :].reshape(P, S * S), "const": const,
        "wrk": np.stack([rwkv_weights("L0_xattn_"), rwkv_weights("L2_xattn_")]),
        "vec": np.stack([rwkv_vectors("L0_xattn_"), rwkv_vectors("L2_xattn_")], 1),
        "veca": np.concatenate(veca, 1),
        "w1l": np.stack([wt(a["L1_xattn_" + n].T) for n in ("Wq", "Wk", "Wv", "Wo")], 1).reshape(P, 4, C, E),
        "w3": np.concatenate(w3),
        "wv": np.concatenate(wv),
        "rows": np.stack([a[q + "bo1"], a[q + "bo2"], a[q + "b_fc2"]]),
        "bv": np.stack([a[q + "bv1"], a[q + "bv2"]]).reshape(H3, 2 * D3),
        "biasv": np.stack([bias_columns(a[q + "bias_v" + s].reshape(H3, D3)) for s in "12"]),
        "fc1": a[q + "w_fc1"].reshape(C, P, F3).transpose(1, 0, 2),
        "fc2": a[q + "w_fc2"].reshape(FT, P, E).transpose(1, 0, 2),
    }
    nc = _bacc.Bacc("TRN2", target_bir_lowering=False, num_devices=1)
    args = []
    for name in arrays:
        arrays[name] = np.ascontiguousarray(arrays[name])
        args.append(nc.dram_tensor(f"in_{name}", arrays[name].shape, mybir.dt.from_np(arrays[name].dtype),
                                   kind="ExternalInput").ap())
    args.append(nc.dram_tensor("out_x", (B, T, E), F32, kind="ExternalOutput").ap())
    build_program(nc, *args)
    r = _run(nc, [{f"in_{k}": v for k, v in arrays.items()}], core_ids=[0])
    return r.results[0]["out_x"]
```
